# Optimizing a Trainium2 kernel written in Bass

```python
import numpy as np
import jax
import jax.numpy as jnp

def _softmax(x, axis=-1):
    return jax.nn.softmax(x, axis=axis)

def _gelu(x):
    return jax.nn.gelu(x, approximate=True)

def _silu(x):
    return jax.nn.silu(x)

def _sigmoid(x):
    return jax.nn.sigmoid(x)

def _layernorm(x, axis=-1, eps=1e-05):
    m = jnp.mean(x, axis=axis, keepdims=True)
    v = jnp.var(x, axis=axis, keepdims=True)
    return (x - m) / jnp.sqrt(v + eps)

def _scatter_add(tgt, idx, src, axis=0):
    return tgt.at[idx].add(src)

def _segment_sum(src, seg, n):
    return jax.ops.segment_sum(src, seg, n)
kernel_name = 'mk_flamingo_gated_d1_seqx_r8_d8fb70'

def setup_inputs(seed: int=0):
    np.random.seed(seed)
    _w = jnp.asarray

    def _rec_inputs():
        import jax
        import jax.numpy as jnp
        _rk = jax.random.key(seed)
        x = 7.22e-05 + 1 * jax.random.normal(jax.random.fold_in(_rk, 1), (8, 256, 128), jnp.float32)
        _lenS = 256 - jax.random.randint(jax.random.fold_in(_rk, 7), (8,), 0, max(1, 256 // 4) + 1, jnp.int32)
        _lenS2 = 1601 - jax.random.randint(jax.random.fold_in(_rk, 8), (8,), 0, max(1, 1601 // 4) + 1, jnp.int32)
        _ctx_1024P = jax.random.normal(jax.random.fold_in(_rk, 11), (8, 16, 128), jnp.float32)
        _ctx_1024c = jax.random.dirichlet(jax.random.fold_in(_rk, 511), 0.3 * jnp.ones((16,), jnp.float32), (8, 1601))
        _ctx_1024t = jnp.einsum('bsk,bkd->bsd', _ctx_1024c, _ctx_1024P)
        _ctx_1024t = _ctx_1024t * jax.lax.rsqrt(jnp.mean(jnp.square(_ctx_1024t)) + 1e-12) * 0.953939
        ctx_1024 = 4.13588e-05 + 0.999923 * (_ctx_1024t + 0.3 * jax.random.normal(jax.random.fold_in(_rk, 611), (8, 1601, 128), jnp.float32))
        _g = jax.random.normal(jax.random.fold_in(_rk, 9001), (2, 1), jnp.float32)
        _g = jnp.sign(_g) * jnp.maximum(jnp.abs(_g), 1.0) + (_g == 0) * 1.0
        g_xattn = _g[0]
        g_ffn = _g[1]
        return (x, ctx_1024, g_xattn, g_ffn)
    x, ctx_1024, g_xattn, g_ffn = _rec_inputs()

    def _L0_xattn_setup():
        import jax, jax.numpy as jnp
        import numpy as np
        N_HEAD = 16
        key = jax.random.key(seed)
        ks = jax.random.split(key, 5)
        b, l, d = (4, 256, 128)
        dh = d // N_HEAD
        return {'q': jax.random.normal(ks[0], (b, l, d), dtype=jnp.float32), 'kv': jax.random.normal(ks[1], (b, l, d), dtype=jnp.float32), 'Wq': jax.random.normal(ks[2], (d, d), dtype=jnp.float32) * 0.02, 'Wkv': jax.random.normal(ks[3], (2 * dh, d), dtype=jnp.float32) * 0.02, 'Wc': jax.random.normal(ks[4], (d, d), dtype=jnp.float32) * 0.02}
    _L0_xattn_all = _L0_xattn_setup()
    _L0_xattn_in = {k: v for k, v in _L0_xattn_all.items() if k in ('Wq', 'Wkv', 'Wc')}
    del _L0_xattn_all

    def _L0_ffn_setup():
        import jax, jax.numpy as jnp
        import numpy as np
        TOPK = 4
        key = jax.random.key(seed)
        ks = jax.random.split(key, 9)
        B, T, D = (4, 256, 128)
        E, H = (32, 128)
        HS = H * TOPK
        s = lambda k, shape, fan: jax.random.normal(k, shape, dtype=jnp.float32) / np.sqrt(fan)
        return {'x': jax.random.normal(ks[0], (B, T, D), dtype=jnp.float32), 'router_w': s(ks[1], (E, D), D), 'router_bias': jnp.zeros((E,), dtype=jnp.float32), 'gate_w': s(ks[2], (E, H, D), D), 'up_w': s(ks[3], (E, H, D), D), 'down_w': s(ks[4], (E, D, H), H), 'sgate_w': s(ks[5], (HS, D), D), 'sup_w': s(ks[6], (HS, D), D), 'sdown_w': s(ks[7], (D, HS), HS)}
    _L0_ffn_all = _L0_ffn_setup()
    _L0_ffn_in = {k: v for k, v in _L0_ffn_all.items() if k in ('router_w', 'router_bias', 'gate_w', 'up_w', 'down_w', 'sgate_w', 'sup_w', 'sdown_w')}
    del _L0_ffn_all
    return {'x': x, 'ctx_1024': ctx_1024, 'g_xattn': g_xattn, 'g_ffn': g_ffn, 'L0_xattn_Wq': _L0_xattn_in['Wq'], 'L0_xattn_Wkv': _L0_xattn_in['Wkv'], 'L0_xattn_Wc': _L0_xattn_in['Wc'], 'L0_ffn_router_w': _L0_ffn_in['router_w'], 'L0_ffn_router_bias': _L0_ffn_in['router_bias'], 'L0_ffn_gate_w': _L0_ffn_in['gate_w'], 'L0_ffn_up_w': _L0_ffn_in['up_w'], 'L0_ffn_down_w': _L0_ffn_in['down_w'], 'L0_ffn_sgate_w': _L0_ffn_in['sgate_w'], 'L0_ffn_sup_w': _L0_ffn_in['sup_w'], 'L0_ffn_sdown_w': _L0_ffn_in['sdown_w']}

def reference(x, ctx_1024, g_xattn, g_ffn, L0_xattn_Wq, L0_xattn_Wkv, L0_xattn_Wc, L0_ffn_router_w, L0_ffn_router_bias, L0_ffn_gate_w, L0_ffn_up_w, L0_ffn_down_w, L0_ffn_sgate_w, L0_ffn_sup_w, L0_ffn_sdown_w):
    import jax
    import jax.numpy as jnp

    def _L0_xattn_ref(q, kv, Wq, Wkv, Wc):
        import jax, jax.numpy as jnp
        import numpy as np
        N_HEAD = 16
        b, l, d = q.shape
        h = N_HEAD
        dh = d // h
        qp = jnp.einsum('bld,ed->ble', q, Wq)
        scores = jnp.einsum('bld,bmd->blm', qp, kv)
        idx = jnp.argmax(scores, axis=-1)
        mem = jnp.take_along_axis(kv, idx[..., None], axis=1)
        mkv = jnp.einsum('bld,ed->ble', mem, Wkv)
        mk, mv = jnp.split(mkv, 2, axis=-1)
        qh = qp.reshape(b, l, h, dh).transpose(0, 2, 1, 3)
        scale = 1.0 / np.sqrt(dh).astype(np.float32)
        logits = jnp.einsum('bhld,bmd->bhlm', qh, mk) * scale
        attn = jax.nn.softmax(logits, axis=-1)
        out = jnp.einsum('bhlm,bmd->bhld', attn, mv)
        out = out.transpose(0, 2, 1, 3).reshape(b, l, d)
        return jnp.einsum('bld,ed->ble', out, Wc)

    def _L0_ffn_ref(x, router_w, router_bias, gate_w, up_w, down_w, sgate_w, sup_w, sdown_w):
        import jax, jax.numpy as jnp
        import numpy as np
        TOPK = 4
        B, T, D = x.shape
        flat = x.reshape(B * T, D)
        logits = flat.astype(jnp.float32) @ router_w.T + router_bias
        scores = jax.nn.softmax(logits, axis=-1)
        topk_scores, topk_idx = jax.lax.top_k(scores, TOPK)
        topk_scores = topk_scores / jnp.clip(topk_scores.sum(axis=-1, keepdims=True), 1e-12, None)
        h = jax.nn.silu(jnp.einsum('nd,ehd->neh', flat, gate_w)) * jnp.einsum('nd,ehd->neh', flat, up_w)
        expert_out = jnp.einsum('neh,edh->ned', h, down_w)
        sel = jnp.take_along_axis(expert_out, topk_idx[:, :, None], axis=1)
        out = (sel * topk_scores.astype(flat.dtype)[:, :, None]).sum(axis=1)
        out = out + jax.nn.silu(flat @ sgate_w.T) * (flat @ sup_w.T) @ sdown_w.T
        return out.reshape(B, T, D)
    x = x + jnp.tanh(g_xattn[0]) * _L0_xattn_ref(_layernorm(x, axis=-1), ctx_1024, L0_xattn_Wq, L0_xattn_Wkv, L0_xattn_Wc)
    x = x + jnp.tanh(g_ffn[0]) * _L0_ffn_ref(_layernorm(x, axis=-1), L0_ffn_router_w, L0_ffn_router_bias, L0_ffn_gate_w, L0_ffn_up_w, L0_ffn_down_w, L0_ffn_sgate_w, L0_ffn_sup_w, L0_ffn_sdown_w)
    return x

_drawn_inputs = setup_inputs


def setup_inputs(seed=0):
    import zlib

    import numpy as np

    out = dict(_drawn_inputs(seed))
    spreads = {'L0_ffn_router_bias': (0.0, 0.1)}
    factors = {'L0_xattn_Wq': 14.119}
    for name, (base, spread) in spreads.items():
        noise = np.random.default_rng([zlib.crc32(name.encode()), seed]).standard_normal(out[name].shape)
        drawn = base * np.exp(spread * noise) if base else spread * noise
        out[name] = jnp.asarray(drawn.astype(out[name].dtype))
    for name, factor in factors.items():
        out[name] = (out[name] * factor).astype(out[name].dtype)
    return out
```

```python
import concourse.bass as bass
from concourse import mybir
from contextlib import ExitStack

F32, BF16, F16, U32 = mybir.dt.float32, mybir.dt.bfloat16, mybir.dt.float16, mybir.dt.uint32
ALU, ACT, AX = mybir.AluOpType, mybir.ActivationFunctionType, mybir.AxisListType

B, L, D, M = 8, 256, 128, 1601
H, DH = 16, 8
LT = L // 128
CHUNK = [401, 400, 400, 400]
CSTART = [0, 401, 801, 1201]
NSTACK = 48
EPS = 1e-5
NT = B * L // 128
E, K, HID = 32, 4, 128
SHC = 4
NDENSE = NT * K
ITEMS = NDENSE + E
PAIRS = ITEMS // 2
TABLE = E + NT + NT + 1 + NDENSE + 128 + 128
STAGES = 5


class Count:

    def __init__(self, per, const):
        self.per, self.const = per, const

    def __mul__(self, k):
        return Count(self.per * k, self.const * k)

    def __add__(self, k):
        return Count(self.per, self.const + k)

    def __sub__(self, k):
        return self + -k


class Step:

    def __init__(self, it, c):
        self.it, self.c = it, c

    def on(self, stage):
        return 0 <= self.c - stage < B if self.it is None else True

    def b(self, stage):
        return Count(2, self.c - stage)

    def half(self, stage):
        return Count(1, (self.c - stage) // 2)

    def par(self, stage):
        return (self.c - stage) % 2

    def value(self, count):
        if self.it is None:
            return count.const
        return self.it * count.per + count.const

    def wait(self, eng, sem, count):
        if self.it is None and count.const <= 0:
            return
        assert count.const > 0, (sem, count.const)
        eng.wait_ge(sem, self.value(count))


def build(nc, x, ctx_rows, ctx_t, wq_t, wk_rep, wv_t, wc_t, kmask, g_xattn, g_ffn, table, router_t, router_bias,
          gate_up_t, down_t, sgate_t, sup_t, sdown_t, out):
    ctx = ExitStack()
    with ctx:
        def sb(name, shape, dt=F32):
            return ctx.enter_context(nc.sbuf_tensor(name, shape, dt))

        def ps(name, shape, dt=F32):
            return ctx.enter_context(nc.psum_tensor(name, shape, dt))

        def sem(name):
            return ctx.enter_context(nc.semaphore(name))

        def sem2(name):
            return [sem(name + "0"), sem(name + "1")]

        q_scr = nc.dram_tensor("q_scr", (B, 3, DH, H, L), BF16).ap()
        att_scr = nc.dram_tensor("att_scr", (B, 4, 16, 1024), F32).ap()
        x2_scr = nc.dram_tensor("x2_scr", (B * L, D), F32).ap()
        y_scr = nc.dram_tensor("y_scr", (ITEMS, 128, D), F32).ap()
        ident = sb("ident", [128, 128])
        wq_sb, wkr_sb, wv_sb, wc_sb = sb("wq_sb", [D, D]), sb("wkr_sb", [D, NSTACK]), sb("wv_sb", [D, DH]), sb("wc_sb", [D, D])
        kmask_sb = sb("kmask_sb", [NSTACK, 2])
        expo = sb("expo", [128, LT])
        gx = sb("gx", [128, 1])
        tgx = sb("tgx", [128, 1])
        x_in = sb("x_in", [128, B * LT, D])
        stats = sb("stats", [128, LT, 6])
        mean_var = sb("mean_var", [128, LT, 2])
        var_eps = sb("var_eps", [128, LT])
        rstd = sb("rstd", [128, LT])
        xn = sb("xn", [128, LT, D])
        xn_t = sb("xn_t", [D, L])
        q_t = sb("q_t", [D, 2, L])
        q_parts = sb("q_parts", [D, 3, L], BF16)
        q_rest = sb("q_rest", [D, 2, L])
        wide = sb("wide", [128, 4 * M])
        ctx_sb = wide[:, 0:2 * M].rearrange("p (b m) -> p b m", b=2)
        score_sb = wide[:, 2 * M:4 * M].rearrange("p (t m) -> p t m", t=LT)
        top8 = sb("top8", [128, LT, 8])
        top_at = sb("top_at", [128, LT, 8], U32)
        row_base = sb("row_base", [128, 1], U32)
        row_at = sb("row_at", [128, LT, 1], U32)
        mem = sb("mem", [128, LT, D])
        mem_t = sb("mem_t", [D, L])
        k_work = sb("k_work", [NSTACK, 2, L], BF16)
        k_rest = sb("k_rest", [NSTACK, L])
        k_max = sb("k_max", [NSTACK, 2, L], BF16)
        v_raw = sb("v_raw", [128, 2, LT, DH])
        stacks = sb("stacks", [128, 4 * H * L + 256], BF16)
        q_max = stacks[0:NSTACK, 0:2 * H * L].rearrange("p (b n) -> p b n", b=2)
        q_exp = stacks[0:NSTACK + 2, 2 * H * L:4 * H * L].rearrange("p (b n) -> p b n", b=2)
        k_exp = sb("k_exp", [NSTACK + 2, 2, L], BF16)
        v_aug = sb("v_aug", [128, 2, LT, 32])
        row_max = sb("row_max", [128, 2, LT, H])
        neg_max = sb("neg_max", [128, LT, H])
        shift_hi = sb("shift_hi", [H, L], BF16)
        shift_lo = sb("shift_lo", [H, L], BF16)
        probs = sb("probs", [128, LT, H * L])
        att_raw = sb("att_raw", [128, 2, 512])
        att_num = sb("att_num", [D, L])
        att_den = sb("att_den", [D, L])
        att_inv = sb("att_inv", [D, L])
        att_t = sb("att_t", [D, L])
        stats2 = sb("stats2", [128, LT, 6])
        mean_var2 = sb("mean_var2", [128, LT, 2])
        var_eps2 = sb("var_eps2", [128, LT])
        rstd2 = sb("rstd2", [128, LT])
        x2 = sb("x2", [128, LT, D])
        x2_t = sb("x2_t", [D, L])
        x2_all = sb("x2_all", [D, B * L])
        logits = sb("logits", [128, NT, E])
        router_sb, bias_sb = sb("router_sb", [D, E]), sb("bias_sb", [128, E])
        gu_sb = sb("gu_sb", [D, E, 2 * HID])
        down_sb = sb("down_sb", [HID, E, D])
        sgate_sb, sup_sb = sb("sgate_sb", [D, SHC, 128]), sb("sup_sb", [D, SHC, 128])
        sdown_sb = sb("sdown_sb", [128, SHC, D])
        gf, tgf = sb("gf", [128, 1]), sb("tgf", [128, 1])
        tab = sb("tab", [128, TABLE])
        at = 0
        views = []
        for n in (E, NT, NT, 1, NDENSE, 128, 128):
            views.append(tab[:, at:at + n])
            at += n
        expert_no, tile_limit, token_no, part_no, dense_no, row_no, triangle = views
        tri_bf, ones_bf = sb("tri_bf", [128, 128], BF16), sb("ones_bf", [128, 128], BF16)
        rows_f16 = sb("rows_f16", [128, 128 + NDENSE], F16)
        small = sb("small", [128, 8, NT])
        top_p = sb("top_p", [128, NT, 8])
        top_e = sb("top_e", [128, NT, 8], U32)
        top_f = sb("top_f", [128, NT, K])
        weight = sb("weight", [128, NT, K])
        mask = sb("mask", [128, NT, E], BF16)
        ranks = sb("ranks", [128, NT, E])
        counts = sb("counts", [128, 10, E])
        pos = sb("pos", [128, NT, K])
        pos_i = sb("pos_i", [128, 2, NT, K], U32)
        pos_g, pos_r = sb("pos_g", [128, NT, K]), sb("pos_r", [128, NT, K])
        slot_token = sb("slot_token", [128, NDENSE], U32)
        token_now, pos_now = sb("token_now", [128, 4, 4], U32), sb("pos_now", [128, 4, K], U32)
        item = sb("item", [128, 8])
        item_i = sb("item_i", [128, 2], U32)
        item_row = sb("item_row", [1, 2 * 128], U32)
        flat_probs = probs[:, :, :].rearrange("p t n -> p (t n)")
        onehot = flat_probs[:, 0:NT * K * E].rearrange("p (t k e) -> p t k e", t=NT, k=K)
        onehot_r = flat_probs[:, 2048:2048 + 4096].bitcast(F16).rearrange("p (n r) -> p n r", r=128)
        onehot_g = flat_probs[:, 6144:8192].bitcast(F16).rearrange("p (n g) -> p n g", g=NDENSE)
        xs_t = stacks[:, :].bitcast(F32)
        shared = wide[:, 0:2048].rearrange("p (t d) -> p t d", d=D)
        gathered = wide[:, 2048:4096].rearrange("p (b g d) -> p b g d", b=4, g=4)
        back = wide[:, 4096:6144].rearrange("p (b k d) -> p b k d", b=4, k=K)
        sel = back.rearrange("p b k d -> p (b k d)").rearrange("p (t k e) -> p t k e", t=NT, k=K)
        x_item = flat_probs[:, 0:512].rearrange("p (b w n) -> p b w n", b=2, w=2)
        silu_e = flat_probs[:, 512:1024].rearrange("p (b w n) -> p b w n", b=2, w=2)
        hid = flat_probs[:, 1024:1536].rearrange("p (b w n) -> p b w n", b=2, w=2)
        hid_t = flat_probs[:, 1536:2048].rearrange("p (b w n) -> p b w n", b=2, w=2)
        hid_s = flat_probs[:, 2048:4096].rearrange("p (c n) -> p c n", c=SHC)
        silu_s = flat_probs[:, 4096:5120].rearrange("p (b n) -> p b n", b=2)
        mix = flat_probs[:, 5120:5632].rearrange("p (b n) -> p b n", b=4)
        result = flat_probs[:, 5632:6144].rearrange("p (b n) -> p b n", b=4)
        y_sb = flat_probs[:, 6144:6656].rearrange("p (b w n) -> p b w n", b=2, w=2)
        ffn_loaded, x2_stored = sem("ffn_loaded"), sem("x2_stored")
        dve_ln2, var2_ready, rstd2_ready, x2_ready = sem("dve_ln2"), sem("var2_ready"), sem("rstd2_ready"), sem("x2_ready")
        x2_t_done, x2_t_ready, logit_done, logit_ready = sem("x2_t_done"), sem("x2_t_ready"), sem("logit_done"), sem("logit_ready")
        ring = ps("ring", [128, 4, 512])
        lg = ps("lg", [128, 2, 512])
        pv = ps("pv", [128, 512])
        misc = ps("misc", [128, 512])

        consts_loaded, ident_ready, presets, row_base_set = sem("consts_loaded"), sem("ident_ready"), sem("presets"), sem("row_base_set")
        tanh_ready = sem("tanh_ready")
        waits_passed = sem("waits_passed")
        x_loaded, ctx_loaded = sem("x_loaded"), sem2("ctx_loaded")
        q_written = sem2("q_written")
        q_max_loaded, q_exp_loaded = sem2("q_max_loaded"), sem2("q_exp_loaded")
        shift_loaded = sem("shift_loaded")
        mem_gathered = [sem("mem_gathered0"), sem("mem_gathered1")]
        att_written, att_loaded = sem("att_written"), sem("att_loaded")
        dve_ln, dve_argmax, dve_k, dve_shift, dve_out = sem("dve_ln"), sem("dve_argmax"), sem("dve_k"), sem("dve_shift"), sem("dve_out")
        var_ready, rstd_ready, xn_ready, xn_t_done, xn_t_ready = sem("var_ready"), sem("rstd_ready"), sem("xn_ready"), sem("xn_t_done"), sem("xn_t_ready")
        q_done, q_ready, q_split = sem("q_done"), sem("q_ready"), sem("q_split")
        score_done, score_copied, argmax_read, row_ready = sem("score_done"), sem("score_copied"), sem("argmax_read"), sem("row_ready")
        mem_t_done, mem_t_ready, kv_done, v_ready, k_ready = sem("mem_t_done"), sem("mem_t_ready"), sem("kv_done"), sem("v_ready"), sem("k_ready")
        kv_kept = sem("kv_kept")
        max_done, max_reduced = sem("max_done"), sem("max_reduced")
        neg_ready, shift_t_done, shift_ready = sem("neg_ready"), sem("shift_t_done"), sem("shift_ready")
        exp_mm, exp_done, pv_done, pv_copied = sem("exp_mm"), sem("exp_done"), sem("pv_done"), sem("pv_copied")
        att_ready, out_done, x1_ready = sem("att_ready"), sem("out_done"), sem("x1_ready")

        NL, NA, NK_, NS_, NO = 6, 8, 4, 3, 4

        def passed(eng, st):
            if st.it is not None:
                eng.sem_inc(waits_passed, 1)

        class Chain:

            def __init__(self, eng, st, sm, stage, per):
                self.eng, self.st, self.sm, self.base, self.per, self.n = eng, st, sm, st.b(stage) * per, per, 0

            def link(self, ins, wait=True):
                self.n += 1
                ins.then_inc(self.sm, 1)
                if wait:
                    self.wait()

            def wait(self):
                self.st.wait(self.eng, self.sm, self.base + self.n)
                passed(self.eng, self.st)

            def end(self):
                assert self.n == self.per, self.n

        def dram_batch(ap, st, stage):
            return ap[bass.ds(st.value(st.b(stage)), 1)]

        def load_ctx(sp, st, stage):
            p = st.par(stage)
            st.wait(sp, score_done, st.b(stage) * 8 - 8)
            passed(sp, st)
            sp.dma_start(ctx_sb[:, p], dram_batch(ctx_t, st, stage).rearrange("o d m -> (o d) m")).then_inc(ctx_loaded[p], 16)

        def sp_step(sp, st):
            if st.on(4):
                st.wait(sp, att_written, st.b(4) * 64 + 64)
                passed(sp, st)
                a = dram_batch(att_scr, st, 4)
                sp.dma_start(att_num[:, :], a[:, :, 0:DH].rearrange("o j c (g l) -> (o j) (c g) l", l=L)).then_inc(att_loaded, 16)
                sp.dma_start(att_den[:, :], a[:, :, DH:16].rearrange("o j c (g l) -> (o j) (c g) l", l=L)).then_inc(att_loaded, 16)
            if st.on(1):
                p = st.par(1)
                st.wait(sp, q_written[p], st.half(1) * 48 + 48)
                passed(sp, st)
                st.wait(sp, max_done, st.b(1) * 16 - 16)
                passed(sp, st)
                a = dram_batch(q_scr, st, 1).rearrange("o s dd h l -> (o s dd) (h l)")
                sp.dma_start(q_max[0:24, p], a).then_inc(q_max_loaded[p], 16)
                sp.dma_start(q_max[24:40, p], a[0:16]).then_inc(q_max_loaded[p], 16)
                sp.dma_start(q_max[40:48, p], a[0:8]).then_inc(q_max_loaded[p], 16)
            if st.on(0):
                load_ctx(sp, st, 0)
            if st.on(3):
                p = st.par(3)
                st.wait(sp, shift_ready, st.b(3) * 2 + 2)
                passed(sp, st)
                sp.dma_start(q_exp[NSTACK:NSTACK + 1, p], shift_hi[:, :]).then_inc(shift_loaded, 16)
                sp.dma_start(q_exp[NSTACK + 1:NSTACK + 2, p], shift_lo[:, :]).then_inc(shift_loaded, 16)
            if st.on(2):
                p = st.par(2)
                st.wait(sp, q_max_loaded[p], st.half(2) * 48 + 48)
                passed(sp, st)
                st.wait(sp, exp_mm, st.b(2) * 16 - 16)
                passed(sp, st)
                sp.dma_start(q_exp[0:NSTACK, p], q_max[:, p]).then_inc(q_exp_loaded[p], 16)
            if st.on(0):
                st.wait(sp, q_split, st.b(0) * 4 + 4)
                passed(sp, st)
                a = dram_batch(q_scr, st, 0)
                for s in range(3):
                    sp.dma_start(a[:, s].rearrange("o dd h l -> (o h) dd l"), q_parts[:, s]).then_inc(q_written[st.par(0)], 16)
            if st.on(4):
                st.wait(sp, x2_ready, st.b(4) * LT + LT)
                passed(sp, st)
                sp.dma_start(dram_batch(x2_scr.rearrange("(b n) d -> b n d", b=B), st, 4).rearrange("o (t p) d -> p (o t) d", p=128),
                             x2[:, :, :]).then_inc(x2_stored, 16)
            if st.on(3):
                st.wait(sp, pv_copied, st.b(3) * 2 + 2)
                passed(sp, st)
                a = dram_batch(att_scr, st, 3)
                for j in range(4):
                    sp.dma_start(a[:, j].rearrange("o c n -> (o c) n"), att_raw[32 * j:32 * j + 16].rearrange("p r n -> p (r n)")).then_inc(att_written, 16)

        def pool_step(pool, st):
            if st.on(0):
                st.wait(pool, var_ready, st.b(0) + 1)
                nc.gpsimd.tensor_tensor(rstd[:, :], var_eps[:, :], expo[:, :], ALU.pow).then_inc(rstd_ready, 1)
            if st.on(2):
                p = st.par(2)
                st.wait(pool, k_ready, st.b(2) + 1)
                st.wait(pool, v_ready, st.b(2) + 1)
                st.wait(pool, exp_mm, st.b(2) * 16 - 16)
                passed(pool, st)
                nc.gpsimd.tensor_copy(k_exp[0:NSTACK, p], k_max[:, p]).then_inc(kv_kept, 1)
                st.wait(pool, pv_done, st.b(2) * 2 - 2)
                passed(pool, st)
                nc.gpsimd.tensor_copy(v_aug[:, p, :, 0:DH], v_raw[:, p]).then_inc(kv_kept, 1)
            if st.on(1):
                for t in range(LT):
                    st.wait(pool, row_ready, st.b(1) * LT + t + 1)
                    st.wait(pool, mem_t_done, st.b(1))
                    passed(pool, st)
                    nc.gpsimd.indirect_dma_start(
                        out=mem[:, t], out_offset=None, in_=ctx_rows,
                        in_offset=bass.IndirectOffsetOnAxis(ap=row_at[:, t], axis=0)).then_inc(mem_gathered[t], 16)
            if st.on(4):
                st.wait(pool, var2_ready, st.b(4) + 1)
                nc.gpsimd.tensor_tensor(rstd2[:, :], var_eps2[:, :], expo[:, :], ALU.pow).then_inc(rstd2_ready, 1)
            if st.on(0):
                p = st.par(0)
                st.wait(pool, q_ready, st.b(0) + 1)
                if st.it is None:
                    st.wait(pool, q_written[1 - p], Count(0, 48 * ((st.c + 1) // 2)) if p == 1 else Count(0, 48 * (st.c // 2)))
                else:
                    st.wait(pool, q_written[1 - p], (st.half(0) + p) * 48)
                q = q_t[:, p]
                passed(pool, st)
                nc.gpsimd.tensor_copy(q_parts[:, 0], q).then_inc(q_split, 1)
                st.wait(pool, q_split, st.b(0) * 4 + 1)
                nc.gpsimd.tensor_tensor(q_rest[:, 0], q, q_parts[:, 0], ALU.subtract).then_inc(q_split, 1)
                st.wait(pool, q_split, st.b(0) * 4 + 2)
                passed(pool, st)
                nc.gpsimd.tensor_copy(q_parts[:, 1], q_rest[:, 0]).then_inc(q_split, 1)
                st.wait(pool, q_split, st.b(0) * 4 + 3)
                nc.gpsimd.tensor_tensor(q_parts[:, 2], q_rest[:, 0], q_parts[:, 1], ALU.subtract).then_inc(q_split, 1)

        def score_tile(pe, st, t):
            p = st.par(1)
            for c, (at, n) in enumerate(zip(CSTART, CHUNK)):
                if t == 0:
                    st.wait(pe, max_reduced, st.b(3) * 16 + 12 + c + 1) if st.it is not None or st.c >= 3 else None
                    if st.it is None and st.c < 3:
                        st.wait(pe, score_copied, st.b(1) * 8 - 3 + c)
                elif st.on(2):
                    st.wait(pe, max_reduced, st.b(2) * 16 + c + 1)
                else:
                    st.wait(pe, score_copied, st.b(1) * 8 + c + 1)
                nc.tensor.matmul(ring[:, c, 0:n], q_t[:, p, 128 * t:128 * t + 128], ctx_sb[:, p, at:at + n],
                                 start=True, stop=True).then_inc(score_done, 1)

        def max_fill(pe, st, n):
            p = st.par(2)
            k = n % 4
            t, hp = n // 8, n % 8
            if n < 4:
                if st.on(1):
                    st.wait(pe, score_copied, st.b(1) * 8 + k + 1)
                else:
                    st.wait(pe, max_reduced, st.b(2) * 16 - 4 + k + 1)
            elif n < 8:
                if st.on(1):
                    st.wait(pe, score_copied, st.b(1) * 8 + 4 + k + 1)
                else:
                    st.wait(pe, max_reduced, st.b(2) * 16 + n - 4 + 1)
            else:
                st.wait(pe, max_reduced, st.b(2) * 16 + n - 4 + 1)
            for w in range(2):
                h = 2 * hp + w
                last = nc.tensor.matmul(ring[:, k, 256 * w:256 * w + 256],
                                        q_max[:, p, h * L + 128 * t:h * L + 128 * t + 128], k_max[:, p],
                                        start=True, stop=True)
            last.then_inc(max_done, 1)

        def exp_fill(pe, st, n):
            p = st.par(3)
            c, j = n // 2, n % 2
            st.wait(pe, exp_done, st.b(3) * 16 + n - 1)
            nc.tensor.matmul(lg[:, n % 2], k_exp[:, p, 128 * j:128 * j + 128], q_exp[:, p, 512 * c:512 * c + 512],
                             start=True, stop=True).then_inc(exp_mm, 1)

        def pv_round(pe, st, r):
            p = st.par(3)
            st.wait(pe, kv_kept, st.b(3) * 2 + 2)
            st.wait(pe, exp_done, st.b(3) * 16 + 8 * r + 8)
            st.wait(pe, pv_copied, st.b(3) * 2 + r)
            for j in range(LT):
                for g in range(4):
                    c = 4 * r + g
                    last = nc.tensor.matmul(pv[32 * g:32 * g + 32], v_aug[:, p, j], probs[:, j, 512 * c:512 * c + 512],
                                            start=(j == 0), stop=(j == LT - 1))
            last.then_inc(pv_done, 1)

        def pe_step(pe, st):
            if st.on(1):
                p = st.par(1)
                st.wait(pe, q_ready, st.b(1) + 1)
                st.wait(pe, ctx_loaded[p], st.half(1) * 16 + 16)
                score_tile(pe, st, 0)
            if st.on(3):
                st.wait(pe, neg_ready, st.b(3) + 1)
                for t in range(LT):
                    last = nc.tensor.transpose(misc[0:H, 128 * t:128 * t + 128], neg_max[:, t], ident[:, :])
                last.then_inc(shift_t_done, 1)
            if st.on(0):
                st.wait(pe, xn_ready, st.b(0) * LT + LT)
                st.wait(pe, shift_ready, st.b(3) * 2 + 2) if st.on(3) else None
                for t in range(LT):
                    last = nc.tensor.transpose(misc[:, 128 * t:128 * t + 128], xn[:, t], ident[:, :])
                last.then_inc(xn_t_done, 1)
            if st.on(2):
                p = st.par(2)
                st.wait(pe, k_ready, st.b(2) + 1)
                st.wait(pe, q_max_loaded[p], st.half(2) * 48 + 48)
                for n in range(4):
                    max_fill(pe, st, n)
            if st.on(1):
                score_tile(pe, st, 1)
            if st.on(0):
                st.wait(pe, xn_t_ready, st.b(0) + 1)
                nc.tensor.matmul(misc[:, 0:L], wq_sb[:, :], xn_t[:, :], start=True, stop=True).then_inc(q_done, 1)
            if st.on(3):
                p = st.par(3)
                st.wait(pe, shift_loaded, st.b(3) * 32 + 32)
                st.wait(pe, q_exp_loaded[p], st.half(3) * 16 + 16)
                st.wait(pe, kv_kept, st.b(3) * 2 + 1)
            for n in range(12):
                if st.on(3):
                    exp_fill(pe, st, n)
                if st.on(2):
                    max_fill(pe, st, 4 + n)
                if n == 3 and st.on(4):
                    st.wait(pe, att_ready, st.b(4) + 1)
                    if st.on(0):
                        st.wait(pe, q_ready, st.b(0) + 1)
                    elif st.on(3):
                        st.wait(pe, shift_ready, st.b(3) * 2 + 2)
                    for t in range(LT):
                        last = nc.tensor.matmul(misc[:, 128 * t:128 * t + 128], att_t[:, 128 * t:128 * t + 128], wc_sb[:, :],
                                                start=True, stop=True)
                    last.then_inc(out_done, 1)
                if n == 9 and st.on(3):
                    pv_round(pe, st, 0)
            if st.on(4):
                st.wait(pe, x2_ready, st.b(4) * LT + LT)
                for t in range(LT):
                    last = nc.tensor.transpose(misc[:, 128 * t:128 * t + 128], x2[:, t], ident[:, :])
                last.then_inc(x2_t_done, 1)
            if st.on(1):
                if st.on(4):
                    st.wait(pe, x2_t_ready, st.b(4) * 2 + 2)
                elif st.on(0):
                    st.wait(pe, q_ready, st.b(0) + 1)
                elif st.on(3):
                    st.wait(pe, shift_ready, st.b(3) * 2 + 2)
                for t in range(LT):
                    st.wait(pe, mem_gathered[t], st.b(1) * 16 + 16)
                    last = nc.tensor.transpose(misc[:, 128 * t:128 * t + 128], mem[:, t], ident[:, :])
                last.then_inc(mem_t_done, 1)
            if st.on(3):
                for n in range(12, 16):
                    exp_fill(pe, st, n)
            if st.on(4):
                st.wait(pe, x2_t_ready, st.b(4) * 2 + 2)
                if st.on(1):
                    st.wait(pe, mem_t_ready, st.b(1) + 1)
                for t in range(LT):
                    last = nc.tensor.matmul(misc[:, E * t:E * t + E], x2_t[:, 128 * t:128 * t + 128], router_sb[:, :],
                                            start=True, stop=True)
                last.then_inc(logit_done, 1)
                st.wait(pe, logit_ready, st.b(4) + 1)
            if st.on(1):
                st.wait(pe, mem_t_ready, st.b(1) + 1)
                nc.tensor.matmul(misc[0:NSTACK, 0:L], wkr_sb[:, :], mem_t[:, :], start=True, stop=True)
                for j in range(LT):
                    last = nc.tensor.matmul(misc[:, L + DH * j:L + DH * j + DH], mem_t[:, 128 * j:128 * j + 128], wv_sb[:, :],
                                            start=True, stop=True)
                last.then_inc(kv_done, 1)
            if st.on(3):
                pv_round(pe, st, 1)
            if st.on(1):
                st.wait(pe, k_ready, st.b(1) + 1)
                st.wait(pe, v_ready, st.b(1) + 1)

        def copy_scores(act, st, t):
            if t == 0:
                st.wait(act, argmax_read, st.b(1) * LT - 1)
            else:
                st.wait(act, argmax_read, st.b(1) * LT)
            for c, (at, n) in enumerate(zip(CSTART, CHUNK)):
                st.wait(act, score_done, st.b(1) * 8 + 4 * t + c + 1)
                nc.scalar.copy(score_sb[:, t, at:at + n], ring[:, c, 0:n]).then_inc(score_copied, 1)

        def exp_tile(act, st, n):
            c, j = n // 2, n % 2
            st.wait(act, exp_mm, st.b(3) * 16 + n + 1)
            if n % 8 == 0:
                st.wait(act, pv_done, st.b(3) * 2 + n // 8 - 1)
            nc.scalar.activation(probs[:, j, 512 * c:512 * c + 512], lg[:, n % 2], ACT.Exp,
                                 scale=DH ** -0.5).then_inc(exp_done, 1)

        def act_step(act, st):
            if st.on(1):
                copy_scores(act, st, 0)
            if st.on(0):
                st.wait(act, xn_t_done, st.b(0) + 1)
                st.wait(act, q_done, st.b(0))
                nc.scalar.copy(xn_t[:, :], misc[:, 0:L]).then_inc(xn_t_ready, 1)
            if st.on(1):
                copy_scores(act, st, 1)
            if st.on(0):
                p = st.par(0)
                st.wait(act, q_done, st.b(0) + 1)
                st.wait(act, score_done, st.b(0) * 8 - 8)
                st.wait(act, q_split, st.b(0) * 4 - 4)
                nc.scalar.copy(q_t[:, p], misc[:, 0:L]).then_inc(q_ready, 1)
            if st.on(3):
                for n in range(12):
                    exp_tile(act, st, n)
                st.wait(act, pv_done, st.b(3) * 2 + 1)
                st.wait(act, att_written, st.b(3) * 64)
                nc.scalar.copy(att_raw[:, 0], pv[:, :]).then_inc(pv_copied, 1)
            if st.on(4):
                st.wait(act, x2_t_done, st.b(4) + 1)
                nc.scalar.copy(x2_t[:, :], misc[:, 0:L]).then_inc(x2_t_ready, 1)
                nc.scalar.copy(x2_all[:, bass.ds(st.value(st.b(4) * L), L)], misc[:, 0:L]).then_inc(x2_t_ready, 1)
            if st.on(1):
                st.wait(act, mem_t_done, st.b(1) + 1)
                st.wait(act, kv_done, st.b(1))
                nc.scalar.copy(mem_t[:, :], misc[:, 0:L]).then_inc(mem_t_ready, 1)
            if st.on(3):
                for n in range(12, 16):
                    exp_tile(act, st, n)
            if st.on(3):
                st.wait(act, pv_done, st.b(3) * 2 + 2)
                nc.scalar.copy(att_raw[:, 1], pv[:, :]).then_inc(pv_copied, 1)

        def argmax_tile(dve, st, t, ch):
            st.wait(dve, score_copied, st.b(1) * 8 + 4 * t + 4)
            passed(dve, st)
            ch.link(nc.vector.max(top8[:, t], score_sb[:, t]))
            nc.vector.max_index(top_at[:, t], top8[:, t], score_sb[:, t]).then_inc(argmax_read, 1)
            st.wait(dve, argmax_read, st.b(1) * LT + t + 1)
            st.wait(dve, mem_gathered[t], st.b(1) * 16)
            passed(dve, st)
            nc.vector.tensor_tensor(row_at[:, t], top_at[:, t, 0:1], row_base[:, :], ALU.add).then_inc(row_ready, 1)

        def reduce_max(dve, st, n):
            p = st.par(2)
            t, hp = n // 8, n % 8
            st.wait(dve, max_done, st.b(2) * 16 + n + 1)
            nc.vector.tensor_reduce(row_max[:, p, t, 2 * hp:2 * hp + 2], ring[:, n % 4].rearrange("p (w m) -> p w m", w=2),
                                    AX.X, ALU.max).then_inc(max_reduced, 1)

        def dve_step(dve, st):
            if st.on(3):
                p = st.par(3)
                st.wait(dve, max_reduced, st.b(3) * 16 + 16)
                st.wait(dve, shift_t_done, st.b(3))
                nc.vector.tensor_scalar(neg_max[:, :], row_max[:, p], -1.0, None, ALU.mult).then_inc(neg_ready, 1)
            if st.on(0):
                p = st.par(0)
                ch = Chain(dve, st, dve_ln, 0, 2 * LT)
                xb = x_in[:, bass.ds(st.value(st.b(0) * LT), LT)]
                for t in range(LT):
                    ch.link(nc.vector.bn_stats(stats[:, t], xb[:, t]), wait=False)
                ch.wait()
                for t in range(LT):
                    ch.link(nc.vector.bn_aggr(mean_var[:, t], stats[:, t]), wait=False)
                ch.wait()
                ch.end()
                nc.vector.tensor_scalar(var_eps[:, :], mean_var[:, :, 1], EPS, None, ALU.add).then_inc(var_ready, 1)
                st.wait(dve, rstd_ready, st.b(0) + 1)
                st.wait(dve, xn_t_done, st.b(0))
                for t in range(LT):
                    nc.vector.tensor_scalar(xn[:, t], xb[:, t], mean_var[:, t, 0:1], rstd[:, t:t + 1],
                                            ALU.subtract, ALU.mult).then_inc(xn_ready, 1)
            if st.on(3):
                st.wait(dve, shift_t_done, st.b(3) + 1)
                st.wait(dve, shift_loaded, st.b(3) * 32)
                nc.vector.tensor_copy(shift_hi[:, :], misc[0:H, 0:L]).then_inc(shift_ready, 1)
                st.wait(dve, shift_ready, st.b(3) * 2 + 1)
                nc.vector.tensor_tensor(shift_lo[:, :], misc[0:H, 0:L], shift_hi[:, :], ALU.subtract).then_inc(shift_ready, 1)
            if st.on(1):
                argmax_ch = Chain(dve, st, dve_argmax, 1, LT)
                argmax_tile(dve, st, 0, argmax_ch)
            if st.on(2):
                for n in range(4):
                    reduce_max(dve, st, n)
            if st.on(4):
                st.wait(dve, att_loaded, st.b(4) * 32 + 32)
                ch = Chain(dve, st, dve_out, 4, 1)
                ch.link(nc.vector.reciprocal(att_inv[:, :], att_den[:, :]))
                ch.end()
                nc.vector.tensor_tensor(att_t[:, :], att_num[:, :], att_inv[:, :], ALU.mult).then_inc(att_ready, 1)
            if st.on(1):
                argmax_tile(dve, st, 1, argmax_ch)
                argmax_ch.end()
                st.wait(dve, row_ready, st.b(1) * LT + LT)
                nc.vector.tensor_scalar(row_base[:, :], row_base[:, :], float(M), None, ALU.add).then_inc(row_base_set, 1)
                st.wait(dve, row_base_set, st.b(1) + 2)
            for n in range(4, 16):
                if st.on(2):
                    reduce_max(dve, st, n)
                if n == 8 and st.on(4):
                    st.wait(dve, out_done, st.b(4) + 1)
                    xb = x_in[:, bass.ds(st.value(st.b(4) * LT), LT)]
                    for t in range(LT):
                        nc.vector.scalar_tensor_tensor(xb[:, t], misc[:, 128 * t:128 * t + 128], tgx[:, :], xb[:, t],
                                                       ALU.mult, ALU.add).then_inc(x1_ready, 1)
                    st.wait(dve, x1_ready, st.b(4) * LT + LT)
                    ch = Chain(dve, st, dve_ln2, 4, 2 * LT)
                    passed(dve, st)
                    for t in range(LT):
                        ch.link(nc.vector.bn_stats(stats2[:, t], xb[:, t]), wait=False)
                    ch.wait()
                    for t in range(LT):
                        ch.link(nc.vector.bn_aggr(mean_var2[:, t], stats2[:, t]), wait=False)
                    ch.wait()
                    ch.end()
                    nc.vector.tensor_scalar(var_eps2[:, :], mean_var2[:, :, 1], EPS, None, ALU.add).then_inc(var2_ready, 1)
                if n == 11 and st.on(4):
                    st.wait(dve, rstd2_ready, st.b(4) + 1)
                    st.wait(dve, x2_stored, st.b(4) * 16 + 1)
                    for t in range(LT):
                        nc.vector.tensor_scalar(x2[:, t], xb[:, t], mean_var2[:, t, 0:1], rstd2[:, t:t + 1],
                                                ALU.subtract, ALU.mult).then_inc(x2_ready, 1)
            if st.on(4):
                st.wait(dve, logit_done, st.b(4) + 1)
                nc.vector.tensor_tensor(logits[:, bass.ds(st.value(st.b(4) * LT), LT)],
                                        misc[:, 0:LT * E].rearrange("p (t e) -> p t e", e=E),
                                        bias_sb[:, :].unsqueeze(1).broadcast_to([128, LT, E]), ALU.add).then_inc(logit_ready, 1)
            if st.on(1):
                p = st.par(1)
                ch = Chain(dve, st, dve_k, 1, 3)
                keys = misc[0:NSTACK, 0:L]
                st.wait(dve, kv_done, st.b(1) + 1)
                st.wait(dve, kv_kept, st.b(1) * 2 - 2)
                nc.vector.tensor_copy(v_raw[:, p], misc[:, L:L + LT * DH].rearrange("p (j v) -> p j v", v=DH)).then_inc(v_ready, 1)
                ch.link(nc.vector.tensor_copy(k_work[:, 0], keys))
                ch.link(nc.vector.scalar_tensor_tensor(k_rest[:, :], k_work[:, 0], kmask_sb[:, 0:1], keys, ALU.mult, ALU.add))
                ch.link(nc.vector.tensor_copy(k_work[:, 1], k_rest[:, :]))
                ch.end()
                st.wait(dve, max_done, st.b(1) * 16 - 16)
                nc.vector.scalar_tensor_tensor(k_max[:, p], k_work[:, 1], kmask_sb[:, 1:2], k_rest[:, :],
                                               ALU.mult, ALU.add).then_inc(k_ready, 1)

        def run(nc_engine, eng, step):
            for c in range(STAGES - 1):
                step(eng, Step(None, c))
            with eng.Fori(0, (B - STAGES + 1) // 2) as it:
                for u in range(2):
                    step(eng, Step(it, STAGES - 1 + u))
            for c in range(B, B + STAGES - 1):
                step(eng, Step(None, c))

        routed = sem("routed")
        exp_ready, mask_ready, rank_done, onehots_ready, slot_done = (
            sem("exp_ready"), sem("mask_ready"), sem("rank_done"), sem("onehots_ready"), sem("slot_done"))
        slot_ready, items_ready, items_loaded, pos_ready = sem("slot_ready"), sem("items_ready"), sem("items_loaded"), sem("pos_ready")
        sh_done, sh_silu, sh_hid, sh_out, sh_copied = sem("sh_done"), sem("sh_silu"), sem("sh_hid"), sem("sh_out"), sem("sh_copied")
        rows_gathered = [sem(f"rows_gathered{i}") for i in range(4)]
        xs_done, xs_copied = sem("xs_done"), sem("xs_copied")
        item_x, gu_done, silu_done, hid_ready = sem("item_x"), sem("gu_done"), sem("silu_done"), sem("hid_ready")
        hid_t_done, hid_t_ready, y_done, y_copied = sem("hid_t_done"), sem("hid_t_ready"), sem("y_done"), sem("y_copied")
        y_stored = [sem("y_stored0"), sem("y_stored1")]
        back_gathered = [sem(f"back_gathered{i}") for i in range(4)]
        mixed, result_ready, out_stored = sem("mixed"), sem("result_ready"), [sem(f"out_stored{i}") for i in range(4)]
        pad_zeroed = sem("pad_zeroed")
        token_named, pos_named = sem("token_named"), sem("pos_named")

        def bc(ap, axis, shape):
            return ap.unsqueeze(axis).broadcast_to(shape)

        def softmax_and_top(dve):
            n = [0]

            def step(ins):
                n[0] += 1
                ins.then_inc(routed, 1)
                dve.wait_ge(routed, n[0])

            top1, total, inv, four, inv4 = (small[:, i] for i in range(5))
            ex = onehot.rearrange("p t k e -> p (t k e)")[:, 0:NT * E].rearrange("p (t e) -> p t e", e=E)
            dve.wait_ge(logit_ready, B)
            step(nc.vector.tensor_reduce(top1, logits[:, :], AX.X, ALU.max))
            step(nc.vector.tensor_tensor(logits[:, :], logits[:, :], bc(top1, 2, [128, NT, E]), ALU.subtract))
            dve.wait_ge(exp_ready, 1)
            step(nc.vector.tensor_reduce(total, logits[:, :], AX.X, ALU.add))
            step(nc.vector.reciprocal(inv, total))
            step(nc.vector.tensor_tensor(logits[:, :], logits[:, :], bc(inv, 2, [128, NT, E]), ALU.mult))
            for t in range(NT):
                ins = nc.vector.max(top_p[:, t], logits[:, t])
            step(ins)
            for t in range(NT):
                ins = nc.vector.max_index(top_e[:, t], top_p[:, t], logits[:, t])
            step(ins)
            step(nc.vector.tensor_copy(top_f[:, :], top_e[:, :, 0:K]))
            step(nc.vector.tensor_tensor(onehot, bc(bc(expert_no, 1, [128, NT, E]), 2, [128, NT, K, E]),
                                         bc(top_f[:, :], 3, [128, NT, K, E]), ALU.is_equal))
            step(nc.vector.tensor_reduce(mask[:, :], onehot.rearrange("p t k e -> p t e k"), AX.X, ALU.max))
            dve.sem_inc(mask_ready, 1)
            step(nc.vector.tensor_reduce(four, top_p[:, :, 0:K], AX.X, ALU.add))
            step(nc.vector.tensor_scalar(four, four, 1e-12, None, ALU.max))
            step(nc.vector.reciprocal(inv4, four))
            step(nc.vector.tensor_tensor(weight[:, :], top_p[:, :, 0:K], bc(inv4, 2, [128, NT, K]), ALU.mult))
            dve.wait_ge(rank_done, 1)
            cnt, tiles, tiles_to, cnt_to, tile_at, start, row_base_e, one = (counts[:, i] for i in range(8))
            step(nc.vector.tensor_copy(cnt, lg[:, 1, 0:E]))
            more = sel.rearrange("p t k e -> p (t k e)")[:, 0:E * NT].rearrange("p (e t) -> p e t", t=NT)
            step(nc.vector.tensor_tensor(more, bc(cnt, 2, [128, E, NT]), bc(tile_limit, 1, [128, E, NT]), ALU.is_gt))
            step(nc.vector.tensor_reduce(tiles, more, AX.X, ALU.add))
            step(nc.vector.memset(one, 1.0))
            step(nc.vector.tensor_tensor_scan(tiles_to, one, tiles, 0.0, ALU.mult, ALU.add))
            step(nc.vector.tensor_tensor_scan(cnt_to, one, cnt, 0.0, ALU.mult, ALU.add))
            step(nc.vector.tensor_tensor(start, cnt_to, cnt, ALU.subtract))
            step(nc.vector.tensor_tensor(tile_at, tiles_to, tiles, ALU.subtract))

            def positions(base):
                step(nc.vector.tensor_tensor(ranks[:, :], lg[:, 0].rearrange("p (t e) -> p t e", e=E), bc(base, 1, [128, NT, E]), ALU.add))
                step(nc.vector.tensor_tensor(sel, onehot, bc(ranks[:, :], 2, [128, NT, K, E]), ALU.mult))
                step(nc.vector.tensor_reduce(pos[:, :], sel, AX.X, ALU.add))

            positions(start)
            step(nc.vector.tensor_copy(pos_i[:, 0], pos[:, :]))
            step(nc.vector.tensor_scalar(pos_i[:, 1], pos_i[:, 0], 7, None, ALU.logical_shift_right))
            step(nc.vector.tensor_copy(pos_g[:, :], pos_i[:, 1]))
            step(nc.vector.scalar_tensor_tensor(pos_r[:, :], pos_g[:, :], -128.0, pos[:, :], ALU.mult, ALU.add))
            for t in range(NT):
                for k in range(K):
                    nc.vector.tensor_scalar(onehot_g[:, t * K + k], rows_f16[:, 128:128 + NDENSE], pos_g[:, t, k:k + 1],
                                            token_no[:, t:t + 1], ALU.is_equal, ALU.mult)
                    nc.vector.tensor_scalar(onehot_r[:, t * K + k], rows_f16[:, 0:128], pos_r[:, t, k:k + 1],
                                            None, ALU.is_equal).then_inc(onehots_ready, 1)
            ended, no_e, g, at_tile, at_start, off = (item[:, c:c + 1] for c in range(6))
            cmp, hot = counts[:, 8], counts[:, 9]
            step(nc.vector.tensor_scalar(cmp, tiles_to, part_no, None, ALU.is_le))
            step(nc.vector.tensor_reduce(ended, cmp, AX.X, ALU.add))
            step(nc.vector.tensor_scalar(no_e, ended, float(E - 1), None, ALU.min))
            step(nc.vector.tensor_scalar(hot, expert_no, no_e, None, ALU.is_equal))
            step(nc.vector.tensor_tensor(cmp, hot, tile_at, ALU.mult))
            step(nc.vector.tensor_reduce(at_tile, cmp, AX.X, ALU.add))
            step(nc.vector.tensor_tensor(cmp, hot, start, ALU.mult))
            step(nc.vector.tensor_reduce(at_start, cmp, AX.X, ALU.add))
            step(nc.vector.tensor_tensor(g, part_no, at_tile, ALU.subtract))
            step(nc.vector.scalar_tensor_tensor(off, g, 128.0, at_start, ALU.mult, ALU.add))
            step(nc.vector.tensor_scalar(off, off, float(NDENSE * 128), None, ALU.min))
            step(nc.vector.tensor_copy(item_i[:, 0:1], no_e))
            nc.vector.tensor_copy(item_i[:, 1:2], off).then_inc(items_ready, 1)
            dve.wait_ge(slot_done, 1)
            nc.vector.tensor_copy(slot_token[:, :], misc[:, 0:NDENSE]).then_inc(slot_ready, 1)
            step(nc.vector.tensor_scalar(row_base_e, tile_at, 128.0, None, ALU.mult))
            positions(row_base_e)
            nc.vector.tensor_copy(pos_i[:, 0], pos[:, :]).then_inc(pos_ready, 1)

        def pe_route(pe):
            pe.wait_ge(mask_ready, 1)
            flat = mask[:, :].rearrange("p t e -> p (t e)")
            nc.tensor.matmul(lg[:, 0], tri_bf[:, :], flat, start=True, stop=False)
            for s in range(1, NT):
                nc.tensor.matmul(lg[:, 0, s * E:NT * E], ones_bf[:, :], flat[:, 0:(NT - s) * E], start=False, stop=(s == NT - 1))
            for t in range(NT):
                last = nc.tensor.matmul(lg[:, 1, 0:E], ones_bf[:, :], mask[:, t], start=(t == 0), stop=(t == NT - 1))
            last.then_inc(rank_done, 1)
            for n in range(NDENSE):
                pe.wait_ge(onehots_ready, n + 1)
                last = nc.tensor.matmul(misc[:, 0:NDENSE], onehot_r[:, n], onehot_g[:, n], start=(n == 0), stop=(n == NDENSE - 1))
            last.then_inc(slot_done, 1)

        def pe_shared(pe, n):
            for c in range(SHC):
                b = 2 * (c % 2)
                if isinstance(n, int):
                    if 4 * n + c >= 2:
                        pe.wait_ge(sh_hid, 4 * n + c - 1)
                else:
                    pe.wait_ge(sh_hid, n * 4 + (c - 1))
                xs = x2_all[:, bass.ds(n * 512, 512)]
                nc.tensor.matmul(ring[:, b], sgate_sb[:, c], xs, start=True, stop=True)
                nc.tensor.matmul(ring[:, b + 1], sup_sb[:, c], xs, start=True, stop=True).then_inc(sh_done, 1)
            pe.wait_ge(sh_hid, n * 4 + 4)
            if not isinstance(n, int) or n:
                pe.wait_ge(sh_copied, n)
            for t in range(4):
                for c in range(SHC):
                    last = nc.tensor.matmul(pv[:, 128 * t:128 * t + 128], hid_s[:, c, 128 * t:128 * t + 128], sdown_sb[:, c],
                                            start=(c == 0), stop=(c == SHC - 1))
            last.then_inc(sh_out, 1)

        def act_shared(act, n):
            for c in range(SHC):
                act.wait_ge(sh_done, n * 4 + (c + 1))
                if isinstance(n, int):
                    if 4 * n + c >= 2:
                        act.wait_ge(sh_hid, 4 * n + c - 1)
                else:
                    act.wait_ge(sh_hid, n * 4 + (c - 1))
                nc.scalar.activation(silu_s[:, c % 2], ring[:, 2 * (c % 2)], ACT.Silu).then_inc(sh_silu, 1)
            act.wait_ge(sh_out, n + 1)
            nc.scalar.copy(shared.rearrange("p t d -> p (t d)")[:, bass.ds(n * 512, 512)], pv[:, :]).then_inc(sh_copied, 1)

        def dve_shared(dve, n):
            for c in range(SHC):
                dve.wait_ge(sh_silu, n * 4 + (c + 1))
                if (not isinstance(n, int) or n) and c == 0:
                    dve.wait_ge(sh_out, n)
                nc.vector.tensor_tensor(hid_s[:, c], silu_s[:, c % 2], ring[:, 2 * (c % 2) + 1], ALU.mult).then_inc(sh_hid, 1)

        def pe_xs(pe, n, u, first):
            pe.wait_ge(rows_gathered[u], (n - u) * 16 + 64)
            if not first or u >= 2:
                pe.wait_ge(xs_copied, n - 1)
            for g in range(4):
                last = nc.tensor.transpose(lg[:, u % 2, 128 * g:128 * g + 128], gathered[:, u, g], ident[:, :])
            last.then_inc(xs_done, 1)

        def act_xs(act, n, u):
            act.wait_ge(xs_done, n + 1)
            nc.scalar.copy(xs_t[:, bass.ds(n * 512, 512)], lg[:, u % 2]).then_inc(xs_copied, 1)

        def pool_rows(pool, n, u, first):
            if not first:
                pool.wait_ge(xs_done, n - 3)
                pool.sem_inc(waits_passed, 1)
            nc.gpsimd.tensor_copy(token_now[:, u], slot_token[:, bass.ds(n * 4, 4)]).then_inc(token_named, 1)
            pool.wait_ge(token_named, n + 1)
            if not first:
                pool.sem_inc(waits_passed, 1)
            for g in range(4):
                nc.gpsimd.indirect_dma_start(
                    out=gathered[:, u, g], out_offset=None, in_=x2_scr,
                    in_offset=bass.IndirectOffsetOnAxis(ap=token_now[:, u, g:g + 1], axis=0)).then_inc(rows_gathered[u], 16)

        def item_value(eng, q, w, c, top):
            return eng.value_load(item_row[0:1, bass.ds(q * 4 + (2 * w + c), 1)], min_val=0, max_val=top)

        def pe_gate_up(pe, q, b, first):
            pe.wait_ge(item_x, q + 1)
            if not first:
                pe.wait_ge(hid_ready, q - 1)
            for w in range(2):
                e = item_value(pe, q, w, 0, E - 1)
                last = nc.tensor.matmul(ring[:, b, 256 * w:256 * w + 256], x_item[:, b, w], gu_sb[:, bass.ds(e, 1)].rearrange("p o n -> p (o n)"),
                                        start=True, stop=True)
            last.then_inc(gu_done, 1)

        def pe_transpose_hid(pe, q, b, first):
            pe.wait_ge(hid_ready, q + 1)
            if not first:
                pe.wait_ge(hid_t_ready, q - 1)
            for w in range(2):
                last = nc.tensor.transpose(ring[:, 2 + b, 128 * w:128 * w + 128], hid[:, b, w], ident[:, :])
            last.then_inc(hid_t_done, 1)

        def pe_down(pe, q, b, first):
            pe.wait_ge(hid_t_ready, q + 1)
            if not first:
                pe.wait_ge(y_copied, q - 1)
            for w in range(2):
                e = item_value(pe, q, w, 0, E - 1)
                last = nc.tensor.matmul(lg[:, b, 128 * w:128 * w + 128], hid_t[:, b, w], down_sb[:, bass.ds(e, 1)].rearrange("p o n -> p (o n)"),
                                        start=True, stop=True)
            last.then_inc(y_done, 1)

        def dve_item_x(dve, q, b, first):
            if not first:
                dve.wait_ge(gu_done, q - 1)
            for w in range(2):
                off = item_value(dve, q, w, 1, NDENSE * 128)
                last = nc.vector.tensor_copy(x_item[:, b, w], xs_t[:, bass.ds(off, 128)])
            last.then_inc(item_x, 1)

        def dve_hid(dve, q, b, first):
            dve.wait_ge(silu_done, q + 1)
            if not first:
                dve.wait_ge(hid_t_done, q - 1)
            nc.vector.tensor_tensor(hid[:, b], silu_e[:, b], ring[:, b].rearrange("p (w c n) -> p w c n", w=2, c=2)[:, :, 1],
                                    ALU.mult).then_inc(hid_ready, 1)

        def act_silu(act, q, b, first):
            act.wait_ge(gu_done, q + 1)
            if not first:
                act.wait_ge(hid_ready, q - 1)
            nc.scalar.activation(silu_e[:, b], ring[:, b].rearrange("p (w c n) -> p w c n", w=2, c=2)[:, :, 0],
                                 ACT.Silu).then_inc(silu_done, 1)

        def act_hid_t(act, q, b, first):
            act.wait_ge(hid_t_done, q + 1)
            if not first:
                act.wait_ge(y_done, q - 1)
            nc.scalar.copy(hid_t[:, b].rearrange("p w n -> p (w n)"), ring[:, 2 + b, 0:256]).then_inc(hid_t_ready, 1)

        def act_y(act, q, b, first):
            act.wait_ge(y_done, q + 1)
            if not first:
                act.wait_ge(y_stored[b], q * 8 - 8 * b)
            nc.scalar.copy(y_sb[:, b].rearrange("p w n -> p (w n)"), lg[:, b, 0:256]).then_inc(y_copied, 1)

        def sp_y(sp, q, b):
            sp.wait_ge(y_copied, q + 1)
            if not isinstance(q, int):
                sp.sem_inc(waits_passed, 1)
            sp.dma_start(y_scr[bass.ds(q * 2, 2)].rearrange("w p d -> p w d"), y_sb[:, b]).then_inc(y_stored[b], 16)

        def pairs(eng, parts):
            deepest = max(lag for _, lag in parts)
            head = 2 + deepest + deepest % 2
            for s in range(head):
                for f, lag in parts:
                    if s - lag >= 0:
                        f(eng, s - lag, (s - lag) % 2, s - lag < 2)
            with eng.Fori(0, (PAIRS - head) // 2) as it:
                for u in range(2):
                    for f, lag in parts:
                        f(eng, it * 2 + (head + u - lag), (head + u - lag) % 2, False)
            for s in range(PAIRS, PAIRS + deepest):
                for f, lag in parts:
                    if s - lag < PAIRS:
                        f(eng, s - lag, (s - lag) % 2, False)

        def pool_back(pool, n, u, first):
            if not first:
                pool.wait_ge(mixed, n * 4 - 12)
                pool.sem_inc(waits_passed, 1)
            nc.gpsimd.tensor_copy(pos_now[:, u], pos_i[:, 0].rearrange("p t k -> p (t k)")[:, bass.ds(n * K, K)]).then_inc(pos_named, 1)
            pool.wait_ge(pos_named, n + 1)
            if not first:
                pool.sem_inc(waits_passed, 1)
            for k in range(K):
                nc.gpsimd.indirect_dma_start(
                    out=back[:, u, k], out_offset=None, in_=y_scr.rearrange("g p d -> (g p) d"),
                    in_offset=bass.IndirectOffsetOnAxis(ap=pos_now[:, u, k:k + 1], axis=0)).then_inc(back_gathered[u], 16)

        def dve_mix(dve, n, u, first):
            dve.wait_ge(back_gathered[u], (n - u) * 16 + 64)
            if not first:
                dve.wait_ge(out_stored[u], (n - u) * 4)
            for k in range(K):
                acc = shared[:, bass.ds(n, 1)] if k == 0 else mix[:, u].unsqueeze(1)
                nc.vector.scalar_tensor_tensor(mix[:, u].unsqueeze(1), back[:, u, k].unsqueeze(1),
                                               weight[:, bass.ds(n, 1), k:k + 1].rearrange("p a b -> p (a b)"),
                                               acc, ALU.mult, ALU.add).then_inc(mixed, 1)
                dve.wait_ge(mixed, n * 4 + (k + 1))
            nc.vector.scalar_tensor_tensor(result[:, u].unsqueeze(1), mix[:, u].unsqueeze(1), tgf[:, :],
                                           x_in[:, bass.ds(n, 1)], ALU.mult, ALU.add).then_inc(result_ready, 1)

        def sp_out(sp, n, u):
            sp.wait_ge(result_ready, n + 1)
            if not isinstance(n, int):
                sp.sem_inc(waits_passed, 1)
            sp.dma_start(out.rearrange("b (t p) d -> p (b t) d", p=128)[:, bass.ds(n, 1)].rearrange("p o d -> p (o d)"),
                         result[:, u]).then_inc(out_stored[u], 16)

        def quads(eng, f, first_arg=True):
            for u in range(4):
                f(eng, u, u, True) if first_arg else f(eng, u, u)
            with eng.Fori(1, NT // 4) as it:
                for u in range(4):
                    f(eng, it * 4 + u, u, False) if first_arg else f(eng, it * 4 + u, u)

        block = ctx.enter_context(nc.Block())

        @block.sync
        def _(sp):
            for dst, src in ((wq_sb, wq_t), (wkr_sb, wk_rep), (wv_sb, wv_t), (wc_sb, wc_t), (kmask_sb, kmask),
                             (router_sb, router_t)):
                sp.dma_start(dst[:, :], src).then_inc(consts_loaded, 16)
            for dst, src in ((gx, g_xattn), (gf, g_ffn), (bias_sb, router_bias)):
                sp.dma_start(dst[:, :], src.rearrange("(o a) -> o a", o=1).broadcast_to([128, dst.shape[1]])).then_inc(consts_loaded, 16)
            for b in range(B):
                sp.dma_start(x_in[:, b * LT:(b + 1) * LT], x[b].rearrange("(t p) d -> p t d", p=128)).then_inc(x_loaded, 16)
            run(nc.sync, sp, sp_step)
            sp.wait_ge(items_ready, 1)
            sp.dma_start(item_row[:, :], item_i[:, :]).then_inc(items_loaded, 16)
            pairs(sp, [(lambda e, q, b, first: sp_y(e, q, b), 0)])
            quads(sp, sp_out, False)
            for b in range(2):
                sp.wait_ge(y_stored[b], 16 * PAIRS // 2)
            sp.wait_ge(x2_stored, 16 * B + 1)
            for u in range(4):
                sp.wait_ge(out_stored[u], 16 * NT // 4)

        @block.gpsimd
        def _(pool):
            nc.gpsimd.memset(ident[:, :], 0.0).then_inc(ident_ready, 1)
            pool.wait_ge(ident_ready, 1)
            nc.gpsimd.affine_select(out=ident[:, :], in_=ident[:, :], compare_op=ALU.not_equal, fill=1.0, base=0,
                                    pattern=[[-1, 128]], channel_multiplier=1).then_inc(ident_ready, 1)
            nc.gpsimd.memset(expo[:, :], -0.5).then_inc(presets, 1)
            nc.gpsimd.memset(k_exp[:, :], 1.0).then_inc(presets, 1)
            nc.gpsimd.memset(v_aug[:, :], 0.0).then_inc(presets, 1)
            pool.wait_ge(presets, 3)
            nc.gpsimd.memset(v_aug[:, :, :, DH:16], 1.0).then_inc(presets, 1)
            nc.gpsimd.memset(xs_t[:, NDENSE * 128:NDENSE * 128 + 128], 0.0).then_inc(pad_zeroed, 1)
            pool.wait_ge(presets, 4)
            run(nc.gpsimd, pool, pool_step)
            pool.wait_ge(x2_stored, 16 * B + 1)
            pool.wait_ge(slot_ready, 1)
            quads(pool, pool_rows)
            pool.wait_ge(pos_ready, 1)
            for b in range(2):
                pool.wait_ge(y_stored[b], 16 * PAIRS // 2)
            quads(pool, pool_back)

        @block.scalar
        def _(act):
            act.dma_start(tab[:, :], table).then_inc(ffn_loaded, 16)
            act.dma_start(sgate_sb[:, :], sgate_t.rearrange("d (c h) -> d c h", c=SHC)).then_inc(ffn_loaded, 16)
            act.dma_start(sup_sb[:, :], sup_t.rearrange("d (c h) -> d c h", c=SHC)).then_inc(ffn_loaded, 16)
            act.dma_start(sdown_sb[:, :], sdown_t.rearrange("(c h) d -> h c d", c=SHC)).then_inc(ffn_loaded, 16)
            act.dma_start(gu_sb[:, :], gate_up_t).then_inc(ffn_loaded, 16)
            act.dma_start(down_sb[:, :], down_t).then_inc(ffn_loaded, 16)
            act.wait_ge(consts_loaded, 144)
            nc.scalar.activation(tgx[:, :], gx[:, :], ACT.Tanh).then_inc(tanh_ready, 1)
            nc.scalar.activation(tgf[:, :], gf[:, :], ACT.Tanh).then_inc(tanh_ready, 1)
            run(nc.scalar, act, act_step)
            act.wait_ge(routed, 2)
            nc.scalar.activation(logits[:, :], logits[:, :], ACT.Exp).then_inc(exp_ready, 1)
            act_shared(act, 0)
            with act.Fori(1, NT // 4) as it:
                act_shared(act, it)
            for u in range(4):
                act_xs(act, u, u)
            with act.Fori(1, NDENSE // 16) as it:
                for u in range(4):
                    act_xs(act, it * 4 + u, u)
            pairs(act, [(act_y, 2), (act_hid_t, 1), (act_silu, 0)])

        @block.tensor
        def _(pe):
            pe.wait_ge(ident_ready, 2)
            pe.wait_ge(presets, 4)
            pe.wait_ge(consts_loaded, 144)
            run(nc.tensor, pe, pe_step)
            pe_route(pe)
            pe.wait_ge(ffn_loaded, 96)
            pe_shared(pe, 0)
            with pe.Fori(1, NT // 4) as it:
                pe_shared(pe, it)
            for u in range(4):
                pe_xs(pe, u, u, True)
            with pe.Fori(1, NDENSE // 16) as it:
                for u in range(4):
                    pe_xs(pe, it * 4 + u, u, False)
            pe.wait_ge(items_loaded, 16)
            pe.wait_ge(xs_copied, NDENSE // 4)
            pairs(pe, [(pe_down, 2), (pe_transpose_hid, 1), (pe_gate_up, 0)])

        @block.vector
        def _(dve):
            nc.vector.memset(row_base[:, :], 0).then_inc(row_base_set, 1)
            nc.vector.memset(x2[:, :], 0.0).then_inc(x2_stored, 1)
            nc.vector.memset(ones_bf[:, :], 1.0)
            dve.wait_ge(ffn_loaded, 96)
            nc.vector.tensor_copy(tri_bf[:, :], triangle)
            nc.vector.tensor_copy(rows_f16[:, 0:128], row_no)
            nc.vector.tensor_copy(rows_f16[:, 128:128 + NDENSE], dense_no)
            dve.wait_ge(row_base_set, 1)
            dve.wait_ge(consts_loaded, 144)
            dve.wait_ge(tanh_ready, 2)
            dve.wait_ge(x_loaded, B * 16)
            run(nc.vector, dve, dve_step)
            softmax_and_top(dve)
            dve_shared(dve, 0)
            with dve.Fori(1, NT // 4) as it:
                dve_shared(dve, it)
            dve.wait_ge(xs_copied, NDENSE // 4)
            dve.wait_ge(pad_zeroed, 1)
            dve.wait_ge(items_loaded, 16)
            pairs(dve, [(dve_item_x, 0), (dve_hid, 0)])
            dve.wait_ge(sh_copied, NT // 4)
            quads(dve, dve_mix)


def kernel(**inp):
    import numpy as np
    import concourse.bacc as bacc
    from concourse.bass_utils import run_bass_kernel_spmd

    f = {k: np.ascontiguousarray(v) for k, v in inp.items()}
    ctx_in = f["ctx_1024"]
    wkv = f["L0_xattn_Wkv"]
    order = [8 * (8 * r + 2 * j + w) + dd for j in range(4) for dd in range(DH) for r in range(2) for w in range(2)]
    mask = np.zeros((NSTACK, 2), np.float32)
    mask[24:, 0] = -1.0
    mask[40:, 1] = -1.0
    part = np.arange(128, dtype=np.float32)[:, None]

    def row(n, scale=1):
        return np.tile(np.arange(n, dtype=np.float32) * scale, (128, 1))

    table = np.concatenate([row(E), row(NT, 128), row(NT, 128) + part, part, row(NDENSE), row(128),
                            np.triu(np.ones((128, 128), np.float32), 1)], 1)
    gate, up, down = (f["L0_ffn_" + n] for n in ("gate_w", "up_w", "down_w"))
    arrays = {
        "x": f["x"], "ctx_rows": ctx_in.reshape(B * M, D), "ctx_t": ctx_in.transpose(0, 2, 1), "wq_t": f["L0_xattn_Wq"].T,
        "wk_rep": np.tile(wkv[0:DH].T, (1, 6)), "wv_t": wkv[DH:].T, "wc_t": f["L0_xattn_Wc"].T[order],
        "kmask": mask, "g_xattn": f["g_xattn"], "g_ffn": f["g_ffn"], "table": table,
        "router_t": f["L0_ffn_router_w"].T, "router_bias": f["L0_ffn_router_bias"],
        "gate_up_t": np.concatenate([gate, up], 1).transpose(2, 0, 1), "down_t": down.transpose(2, 0, 1),
        "sgate_t": f["L0_ffn_sgate_w"].T, "sup_t": f["L0_ffn_sup_w"].T, "sdown_t": f["L0_ffn_sdown_w"].T,
    }
    arrays = {k: np.ascontiguousarray(v) for k, v in arrays.items()}
    nc = bacc.Bacc("TRN2", target_bir_lowering=False, num_devices=1)
    args = [nc.dram_tensor("in_" + k, v.shape, mybir.dt.from_np(v.dtype), kind="ExternalInput").ap() for k, v in arrays.items()]
    out = nc.dram_tensor("out", (B, L, D), F32, kind="ExternalOutput").ap()
    build(nc, *args, out)
    r = run_bass_kernel_spmd(nc, [{"in_" + k: v for k, v in arrays.items()}], core_ids=[0])
    return r.results[0]["out"]
```

```python
import concourse.bass as bass
from concourse import mybir
from contextlib import ExitStack

F32, BF16, F16, U32 = mybir.dt.float32, mybir.dt.bfloat16, mybir.dt.float16, mybir.dt.uint32
ALU, ACT, AX = mybir.AluOpType, mybir.ActivationFunctionType, mybir.AxisListType

B, L, D, M = 8, 256, 128, 1601
H, DH = 16, 8
LT = L // 128
CHUNK = [401, 400, 400, 400]
CSTART = [0, 401, 801, 1201]
NSTACK = 48
EPS = 1e-5
NT = B * L // 128
E, K, HID = 32, 4, 128
SHC = 4
NDENSE = NT * K
ITEMS = NDENSE + E
PAIRS = ITEMS // 2
TABLE = E + NT + NT + 1 + NDENSE + 128 + 128
STAGES = 5


class Count:

    def __init__(self, per, const):
        self.per, self.const = per, const

    def __mul__(self, k):
        return Count(self.per * k, self.const * k)

    def __add__(self, k):
        return Count(self.per, self.const + k)

    def __sub__(self, k):
        return self + -k


class Step:

    def __init__(self, it, c):
        self.it, self.c = it, c

    def on(self, stage):
        return 0 <= self.c - stage < B if self.it is None else True

    def b(self, stage):
        return Count(2, self.c - stage)

    def half(self, stage):
        return Count(1, (self.c - stage) // 2)

    def par(self, stage):
        return (self.c - stage) % 2

    def value(self, count):
        if self.it is None:
            return count.const
        return self.it * count.per + count.const

    def wait(self, eng, sem, count):
        if self.it is None and count.const <= 0:
            return
        assert count.const > 0, (sem, count.const)
        eng.wait_ge(sem, self.value(count))


def build(nc, x, ctx_rows, ctx_t, wq_t, wk_rep, wv_t, wc_t, kmask, g_xattn, g_ffn, table, router_t, router_bias,
          gate_up_t, down_t, sgate_t, sup_t, sdown_t, out):
    ctx = ExitStack()
    with ctx:
        def sb(name, shape, dt=F32):
            return ctx.enter_context(nc.sbuf_tensor(name, shape, dt))

        def ps(name, shape, dt=F32):
            return ctx.enter_context(nc.psum_tensor(name, shape, dt))

        def sem(name):
            return ctx.enter_context(nc.semaphore(name))

        def sem2(name):
            return [sem(name + "0"), sem(name + "1")]

        q_scr = nc.dram_tensor("q_scr", (B, 3, DH, H, L), BF16).ap()
        att_scr = nc.dram_tensor("att_scr", (B, 4, 16, 1024), F32).ap()
        x2_scr = nc.dram_tensor("x2_scr", (B * L, D), F32).ap()
        y_scr = nc.dram_tensor("y_scr", (ITEMS, 128, D), F32).ap()
        ident = sb("ident", [128, 128])
        wq_sb, wkr_sb, wv_sb, wc_sb = sb("wq_sb", [D, D]), sb("wkr_sb", [D, NSTACK]), sb("wv_sb", [D, DH]), sb("wc_sb", [D, D])
        kmask_sb = sb("kmask_sb", [NSTACK, 2])
        expo = sb("expo", [128, LT])
        gx = sb("gx", [128, 1])
        tgx = sb("tgx", [128, 1])
        x_in = sb("x_in", [128, B * LT, D])
        stats = sb("stats", [128, LT, 6])
        mean_var = sb("mean_var", [128, LT, 2])
        var_eps = sb("var_eps", [128, LT])
        rstd = sb("rstd", [128, LT])
        xn = sb("xn", [128, LT, D])
        xn_t = sb("xn_t", [D, L])
        q_t = sb("q_t", [D, 2, L])
        q_parts = sb("q_parts", [D, 3, L], BF16)
        q_rest = sb("q_rest", [D, 2, L])
        wide = sb("wide", [128, 4 * M])
        ctx_sb = wide[:, 0:2 * M].rearrange("p (b m) -> p b m", b=2)
        score_sb = wide[:, 2 * M:4 * M].rearrange("p (t m) -> p t m", t=LT)
        top8 = sb("top8", [128, LT, 8])
        top_at = sb("top_at", [128, LT, 8], U32)
        row_base = sb("row_base", [128, 1], U32)
        row_at = sb("row_at", [128, LT, 1], U32)
        mem = sb("mem", [128, LT, D])
        mem_t = sb("mem_t", [D, L])
        k_work = sb("k_work", [NSTACK, 2, L], BF16)
        k_rest = sb("k_rest", [NSTACK, L])
        k_max = sb("k_max", [NSTACK, 2, L], BF16)
        v_raw = sb("v_raw", [128, 2, LT, DH])
        stacks = sb("stacks", [128, 4 * H * L + 256], BF16)
        q_max = stacks[0:NSTACK, 0:2 * H * L].rearrange("p (b n) -> p b n", b=2)
        q_exp = stacks[0:NSTACK + 2, 2 * H * L:4 * H * L].rearrange("p (b n) -> p b n", b=2)
        k_exp = sb("k_exp", [NSTACK + 2, 2, L], BF16)
        v_aug = sb("v_aug", [128, 2, LT, 32])
        row_max = sb("row_max", [128, 2, LT, H])
        neg_max = sb("neg_max", [128, LT, H])
        shift_hi = sb("shift_hi", [H, L], BF16)
        shift_lo = sb("shift_lo", [H, L], BF16)
        probs = sb("probs", [128, LT, H * L])
        att_raw = sb("att_raw", [128, 2, 512])
        att_num = sb("att_num", [D, L])
        att_den = sb("att_den", [D, L])
        att_inv = sb("att_inv", [D, L])
        att_t = sb("att_t", [D, L])
        stats2 = sb("stats2", [128, LT, 6])
        mean_var2 = sb("mean_var2", [128, LT, 2])
        var_eps2 = sb("var_eps2", [128, LT])
        rstd2 = sb("rstd2", [128, LT])
        x2 = sb("x2", [128, LT, D])
        x2_t = sb("x2_t", [D, L])
        x2_all = sb("x2_all", [D, B * L])
        logits = sb("logits", [128, NT, E])
        router_sb, bias_sb = sb("router_sb", [D, E]), sb("bias_sb", [128, E])
        gu_sb = sb("gu_sb", [D, E, 2 * HID])
        down_sb = sb("down_sb", [HID, E, D])
        sgate_sb, sup_sb = sb("sgate_sb", [D, SHC, 128]), sb("sup_sb", [D, SHC, 128])
        sdown_sb = sb("sdown_sb", [128, SHC, D])
        gf, tgf = sb("gf", [128, 1]), sb("tgf", [128, 1])
        tab = sb("tab", [128, TABLE])
        at = 0
        views = []
        for n in (E, NT, NT, 1, NDENSE, 128, 128):
            views.append(tab[:, at:at + n])
            at += n
        expert_no, tile_limit, token_no, part_no, dense_no, row_no, triangle = views
        tri_bf, ones_bf = sb("tri_bf", [128, 128], BF16), sb("ones_bf", [128, 128], BF16)
        rows_f16 = sb("rows_f16", [128, 128 + NDENSE], F16)
        small = sb("small", [128, 8, NT])
        top_p = sb("top_p", [128, NT, 8])
        top_e = sb("top_e", [128, NT, 8], U32)
        top_f = sb("top_f", [128, NT, K])
        weight = sb("weight", [128, NT, K])
        mask = sb("mask", [128, NT, E], BF16)
        ranks = sb("ranks", [128, NT, E])
        counts = sb("counts", [128, 10, E])
        pos = sb("pos", [128, NT, K])
        pos_i = sb("pos_i", [128, 2, NT, K], U32)
        pos_g, pos_r = sb("pos_g", [128, NT, K]), sb("pos_r", [128, NT, K])
        slot_token = sb("slot_token", [128, NDENSE], U32)
        token_now, pos_now = sb("token_now", [128, 4, 4], U32), sb("pos_now", [128, 4, K], U32)
        item = sb("item", [128, 8])
        item_i = sb("item_i", [128, 2], U32)
        item_row = sb("item_row", [1, 2 * 128], U32)
        flat_probs = probs[:, :, :].rearrange("p t n -> p (t n)")
        onehot = flat_probs[:, 0:NT * K * E].rearrange("p (t k e) -> p t k e", t=NT, k=K)
        onehot_r = flat_probs[:, 2048:2048 + 4096].bitcast(F16).rearrange("p (n r) -> p n r", r=128)
        onehot_g = flat_probs[:, 6144:8192].bitcast(F16).rearrange("p (n g) -> p n g", g=NDENSE)
        xs_t = stacks[:, :].bitcast(F32)
        shared = wide[:, 0:2048].rearrange("p (t d) -> p t d", d=D)
        gathered = wide[:, 2048:4096].rearrange("p (b g d) -> p b g d", b=4, g=4)
        back = wide[:, 4096:6144].rearrange("p (b k d) -> p b k d", b=4, k=K)
        sel = back.rearrange("p b k d -> p (b k d)").rearrange("p (t k e) -> p t k e", t=NT, k=K)
        x_item = flat_probs[:, 0:512].rearrange("p (b w n) -> p b w n", b=2, w=2)
        silu_e = flat_probs[:, 512:1024].rearrange("p (b w n) -> p b w n", b=2, w=2)
        hid = flat_probs[:, 1024:1536].rearrange("p (b w n) -> p b w n", b=2, w=2)
        hid_t = flat_probs[:, 1536:2048].rearrange("p (b w n) -> p b w n", b=2, w=2)
        hid_s = flat_probs[:, 2048:4096].rearrange("p (c n) -> p c n", c=SHC)
        silu_s = flat_probs[:, 4096:5120].rearrange("p (b n) -> p b n", b=2)
        mix = flat_probs[:, 5120:5632].rearrange("p (b n) -> p b n", b=4)
        result = flat_probs[:, 5632:6144].rearrange("p (b n) -> p b n", b=4)
        y_sb = flat_probs[:, 6144:6656].rearrange("p (b w n) -> p b w n", b=2, w=2)
        ffn_loaded, x2_stored = sem("ffn_loaded"), sem("x2_stored")
        dve_ln2, var2_ready, rstd2_ready, x2_ready = sem("dve_ln2"), sem("var2_ready"), sem("rstd2_ready"), sem("x2_ready")
        x2_t_done, x2_t_ready, logit_done, logit_ready = sem("x2_t_done"), sem("x2_t_ready"), sem("logit_done"), sem("logit_ready")
        ring = ps("ring", [128, 4, 512])
        lg = ps("lg", [128, 2, 512])
        pv = ps("pv", [128, 512])
        misc = ps("misc", [128, 512])

        consts_loaded, ident_ready, presets, row_base_set = sem("consts_loaded"), sem("ident_ready"), sem("presets"), sem("row_base_set")
        tanh_ready = sem("tanh_ready")
        waits_passed = sem("waits_passed")
        x_loaded, ctx_loaded = sem("x_loaded"), sem2("ctx_loaded")
        q_written = sem2("q_written")
        q_max_loaded, q_exp_loaded = sem2("q_max_loaded"), sem2("q_exp_loaded")
        shift_loaded = sem("shift_loaded")
        mem_gathered = [sem("mem_gathered0"), sem("mem_gathered1")]
        att_written, att_loaded = sem("att_written"), sem("att_loaded")
        dve_ln, dve_argmax, dve_k, dve_shift, dve_out = sem("dve_ln"), sem("dve_argmax"), sem("dve_k"), sem("dve_shift"), sem("dve_out")
        var_ready, rstd_ready, xn_ready, xn_t_done, xn_t_ready = sem("var_ready"), sem("rstd_ready"), sem("xn_ready"), sem("xn_t_done"), sem("xn_t_ready")
        q_done, q_ready, q_split = sem("q_done"), sem("q_ready"), sem("q_split")
        score_done, score_copied, argmax_read, row_ready = sem("score_done"), sem("score_copied"), sem("argmax_read"), sem("row_ready")
        mem_t_done, mem_t_ready, kv_done, v_ready, k_ready = sem("mem_t_done"), sem("mem_t_ready"), sem("kv_done"), sem("v_ready"), sem("k_ready")
        kv_kept = sem("kv_kept")
        max_done, max_reduced = sem("max_done"), sem("max_reduced")
        neg_ready, shift_t_done, shift_ready = sem("neg_ready"), sem("shift_t_done"), sem("shift_ready")
        exp_mm, exp_done, pv_done, pv_copied = sem("exp_mm"), sem("exp_done"), sem("pv_done"), sem("pv_copied")
        att_ready, out_done, x1_ready = sem("att_ready"), sem("out_done"), sem("x1_ready")

        NL, NA, NK_, NS_, NO = 6, 8, 4, 3, 4

        def passed(eng, st):
            if st.it is not None:
                eng.sem_inc(waits_passed, 1)

        class Chain:

            def __init__(self, eng, st, sm, stage, per):
                self.eng, self.st, self.sm, self.base, self.per, self.n = eng, st, sm, st.b(stage) * per, per, 0

            def link(self, ins, wait=True):
                self.n += 1
                ins.then_inc(self.sm, 1)
                if wait:
                    self.wait()

            def wait(self):
                self.st.wait(self.eng, self.sm, self.base + self.n)
                passed(self.eng, self.st)

            def end(self):
                assert self.n == self.per, self.n

        def dram_batch(ap, st, stage):
            return ap[bass.ds(st.value(st.b(stage)), 1)]

        def load_ctx(sp, st, stage):
            p = st.par(stage)
            st.wait(sp, score_done, st.b(stage) * 8 - 8)
            passed(sp, st)
            sp.dma_start(ctx_sb[:, p], dram_batch(ctx_t, st, stage).rearrange("o d m -> (o d) m")).then_inc(ctx_loaded[p], 16)

        def sp_step(sp, st):
            if st.on(4):
                st.wait(sp, att_written, st.b(4) * 64 + 64)
                passed(sp, st)
                a = dram_batch(att_scr, st, 4)
                sp.dma_start(att_num[:, :], a[:, :, 0:DH].rearrange("o j c (g l) -> (o j) (c g) l", l=L)).then_inc(att_loaded, 16)
                sp.dma_start(att_den[:, :], a[:, :, DH:16].rearrange("o j c (g l) -> (o j) (c g) l", l=L)).then_inc(att_loaded, 16)
            if st.on(1):
                p = st.par(1)
                st.wait(sp, q_written[p], st.half(1) * 48 + 48)
                passed(sp, st)
                st.wait(sp, max_done, st.b(1) * 16 - 16)
                passed(sp, st)
                a = dram_batch(q_scr, st, 1).rearrange("o s dd h l -> (o s dd) (h l)")
                sp.dma_start(q_max[0:24, p], a).then_inc(q_max_loaded[p], 16)
                sp.dma_start(q_max[24:40, p], a[0:16]).then_inc(q_max_loaded[p], 16)
                sp.dma_start(q_max[40:48, p], a[0:8]).then_inc(q_max_loaded[p], 16)
            if st.on(0):
                load_ctx(sp, st, 0)
            if st.on(3):
                p = st.par(3)
                st.wait(sp, shift_ready, st.b(3) * 2 + 2)
                passed(sp, st)
                sp.dma_start(q_exp[NSTACK:NSTACK + 1, p], shift_hi[:, :]).then_inc(shift_loaded, 16)
                sp.dma_start(q_exp[NSTACK + 1:NSTACK + 2, p], shift_lo[:, :]).then_inc(shift_loaded, 16)
            if st.on(2):
                p = st.par(2)
                st.wait(sp, q_max_loaded[p], st.half(2) * 48 + 48)
                passed(sp, st)
                st.wait(sp, exp_mm, st.b(2) * 16 - 16)
                passed(sp, st)
                sp.dma_start(q_exp[0:NSTACK, p], q_max[:, p]).then_inc(q_exp_loaded[p], 16)
            if st.on(0):
                st.wait(sp, q_split, st.b(0) * 4 + 4)
                passed(sp, st)
                a = dram_batch(q_scr, st, 0)
                for s in range(3):
                    sp.dma_start(a[:, s].rearrange("o dd h l -> (o h) dd l"), q_parts[:, s]).then_inc(q_written[st.par(0)], 16)
            if st.on(4):
                st.wait(sp, x2_ready, st.b(4) * LT + LT)
                passed(sp, st)
                sp.dma_start(dram_batch(x2_scr.rearrange("(b n) d -> b n d", b=B), st, 4).rearrange("o (t p) d -> p (o t) d", p=128),
                             x2[:, :, :]).then_inc(x2_stored, 16)
            if st.on(3):
                st.wait(sp, pv_copied, st.b(3) * 2 + 2)
                passed(sp, st)
                a = dram_batch(att_scr, st, 3)
                for j in range(4):
                    sp.dma_start(a[:, j].rearrange("o c n -> (o c) n"), att_raw[32 * j:32 * j + 16].rearrange("p r n -> p (r n)")).then_inc(att_written, 16)

        def pool_step(pool, st):
            if st.on(0):
                st.wait(pool, var_ready, st.b(0) + 1)
                nc.gpsimd.tensor_tensor(rstd[:, :], var_eps[:, :], expo[:, :], ALU.pow).then_inc(rstd_ready, 1)
            if st.on(2):
                p = st.par(2)
                st.wait(pool, k_ready, st.b(2) + 1)
                st.wait(pool, v_ready, st.b(2) + 1)
                st.wait(pool, exp_mm, st.b(2) * 16 - 16)
                passed(pool, st)
                nc.gpsimd.tensor_copy(k_exp[0:NSTACK, p], k_max[:, p]).then_inc(kv_kept, 1)
                st.wait(pool, pv_done, st.b(2) * 2 - 2)
                passed(pool, st)
                nc.gpsimd.tensor_copy(v_aug[:, p, :, 0:DH], v_raw[:, p]).then_inc(kv_kept, 1)
            if st.on(1):
                for t in range(LT):
                    st.wait(pool, row_ready, st.b(1) * LT + t + 1)
                    st.wait(pool, mem_t_done, st.b(1))
                    passed(pool, st)
                    nc.gpsimd.indirect_dma_start(
                        out=mem[:, t], out_offset=None, in_=ctx_rows,
                        in_offset=bass.IndirectOffsetOnAxis(ap=row_at[:, t], axis=0)).then_inc(mem_gathered[t], 16)
            if st.on(4):
                st.wait(pool, var2_ready, st.b(4) + 1)
                nc.gpsimd.tensor_tensor(rstd2[:, :], var_eps2[:, :], expo[:, :], ALU.pow).then_inc(rstd2_ready, 1)
            if st.on(0):
                p = st.par(0)
                st.wait(pool, q_ready, st.b(0) + 1)
                if st.it is None:
                    st.wait(pool, q_written[1 - p], Count(0, 48 * ((st.c + 1) // 2)) if p == 1 else Count(0, 48 * (st.c // 2)))
                else:
                    st.wait(pool, q_written[1 - p], (st.half(0) + p) * 48)
                q = q_t[:, p]
                passed(pool, st)
                nc.gpsimd.tensor_copy(q_parts[:, 0], q).then_inc(q_split, 1)
                st.wait(pool, q_split, st.b(0) * 4 + 1)
                nc.gpsimd.tensor_tensor(q_rest[:, 0], q, q_parts[:, 0], ALU.subtract).then_inc(q_split, 1)
                st.wait(pool, q_split, st.b(0) * 4 + 2)
                passed(pool, st)
                nc.gpsimd.tensor_copy(q_parts[:, 1], q_rest[:, 0]).then_inc(q_split, 1)
                st.wait(pool, q_split, st.b(0) * 4 + 3)
                nc.gpsimd.tensor_tensor(q_parts[:, 2], q_rest[:, 0], q_parts[:, 1], ALU.subtract).then_inc(q_split, 1)

        def score_fill(pe, st, i):
            p, t, c = st.par(1), i // 4, i % 4
            st.wait(pe, score_copied, st.b(1) * 8 + i - 1)
            nc.tensor.matmul(ring[:, i % 2, 0:CHUNK[c]], q_t[:, p, 128 * t:128 * t + 128], ctx_sb[:, p, CSTART[c]:CSTART[c] + CHUNK[c]],
                             start=True, stop=True).then_inc(score_done, 1)

        def max_fill(pe, st, n):
            p, t, hp = st.par(2), n // 8, n % 8
            st.wait(pe, max_reduced, st.b(2) * 16 + n - 1)
            for w in range(2):
                h = 2 * hp + w
                last = nc.tensor.matmul(ring[:, 2 + n % 2, 256 * w:256 * w + 256],
                                        q_max[:, p, h * L + 128 * t:h * L + 128 * t + 128], k_max[:, p],
                                        start=True, stop=True)
            last.then_inc(max_done, 1)

        def exp_fill(pe, st, n):
            p = st.par(3)
            c, j = n // 2, n % 2
            st.wait(pe, exp_done, st.b(3) * 16 + n - 1)
            nc.tensor.matmul(lg[:, n % 2], k_exp[:, p, 128 * j:128 * j + 128], q_exp[:, p, 512 * c:512 * c + 512],
                             start=True, stop=True).then_inc(exp_mm, 1)

        def pv_round(pe, st, r):
            p = st.par(3)
            st.wait(pe, kv_kept, st.b(3) * 2 + 2)
            st.wait(pe, exp_done, st.b(3) * 16 + 8 * r + 8)
            st.wait(pe, pv_copied, st.b(3) * 2 + r)
            for j in range(LT):
                for g in range(4):
                    c = 4 * r + g
                    last = nc.tensor.matmul(pv[32 * g:32 * g + 32], v_aug[:, p, j], probs[:, j, 512 * c:512 * c + 512],
                                            start=(j == 0), stop=(j == LT - 1))
            last.then_inc(pv_done, 1)

        def pe_scores(pe, st, span):
            if st.on(1):
                if span[0] == 0:
                    st.wait(pe, q_ready, st.b(1) + 1)
                    st.wait(pe, ctx_loaded[st.par(1)], st.half(1) * 16 + 16)
                for i in range(*span):
                    score_fill(pe, st, i)

        def pe_max(pe, st, span):
            if st.on(2):
                if span[0] == 0:
                    st.wait(pe, k_ready, st.b(2) + 1)
                    st.wait(pe, q_max_loaded[st.par(2)], st.half(2) * 48 + 48)
                for n in range(*span):
                    max_fill(pe, st, n)

        def pe_exp(pe, st, span):
            if st.on(3):
                if span[0] == 0:
                    st.wait(pe, shift_loaded, st.b(3) * 32 + 32)
                    st.wait(pe, q_exp_loaded[st.par(3)], st.half(3) * 16 + 16)
                    st.wait(pe, kv_kept, st.b(3) * 2 + 1)
                for n in range(*span):
                    exp_fill(pe, st, n)

        def misc_free(pe, st, use):
            readers = [(3, shift_ready, 2), (0, xn_t_ready, 1), (0, q_ready, 1), (4, x1_ready, LT), (1, mem_t_ready, 1),
                       (1, k_ready, 1), (4, x2_t_ready, 2), (4, logit_ready, 1)]
            for n in range(use - 1, -1, -1):
                stage, sm, per = readers[n]
                if st.on(stage):
                    st.wait(pe, sm, st.b(stage) * per + per)
                    return

        def pe_shift(pe, st):
            if st.on(3):
                st.wait(pe, neg_ready, st.b(3) + 1)
                misc_free(pe, st, 0)
                for t in range(LT):
                    last = nc.tensor.transpose(misc[0:H, 128 * t:128 * t + 128], neg_max[:, t], ident[:, :])
                last.then_inc(shift_t_done, 1)

        def pe_xn(pe, st):
            if st.on(0):
                st.wait(pe, xn_ready, st.b(0) * LT + LT)
                misc_free(pe, st, 1)
                for t in range(LT):
                    last = nc.tensor.transpose(misc[:, 128 * t:128 * t + 128], xn[:, t], ident[:, :])
                last.then_inc(xn_t_done, 1)

        def pe_q(pe, st):
            if st.on(0):
                misc_free(pe, st, 2)
                nc.tensor.matmul(misc[:, 0:L], wq_sb[:, :], xn_t[:, :], start=True, stop=True).then_inc(q_done, 1)

        def pe_out(pe, st):
            if st.on(4):
                st.wait(pe, att_ready, st.b(4) + 1)
                misc_free(pe, st, 3)
                for t in range(LT):
                    last = nc.tensor.matmul(misc[:, 128 * t:128 * t + 128], att_t[:, 128 * t:128 * t + 128], wc_sb[:, :],
                                            start=True, stop=True)
                last.then_inc(out_done, 1)

        def pe_mem(pe, st):
            if st.on(1):
                misc_free(pe, st, 4)
                for t in range(LT):
                    st.wait(pe, mem_gathered[t], st.b(1) * 16 + 16)
                    last = nc.tensor.transpose(misc[:, 128 * t:128 * t + 128], mem[:, t], ident[:, :])
                last.then_inc(mem_t_done, 1)

        def pe_kv(pe, st):
            if st.on(1):
                misc_free(pe, st, 5)
                nc.tensor.matmul(misc[0:NSTACK, 0:L], wkr_sb[:, :], mem_t[:, :], start=True, stop=True)
                for j in range(LT):
                    last = nc.tensor.matmul(misc[:, L + DH * j:L + DH * j + DH], mem_t[:, 128 * j:128 * j + 128], wv_sb[:, :],
                                            start=True, stop=True)
                last.then_inc(kv_done, 1)

        def pe_x2(pe, st):
            if st.on(4):
                st.wait(pe, x2_ready, st.b(4) * LT + LT)
                misc_free(pe, st, 6)
                for t in range(LT):
                    last = nc.tensor.transpose(misc[:, 128 * t:128 * t + 128], x2[:, t], ident[:, :])
                last.then_inc(x2_t_done, 1)

        def pe_logits(pe, st):
            if st.on(4):
                misc_free(pe, st, 7)
                for t in range(LT):
                    last = nc.tensor.matmul(misc[:, E * t:E * t + E], x2_t[:, 128 * t:128 * t + 128], router_sb[:, :],
                                            start=True, stop=True)
                last.then_inc(logit_done, 1)

        def pe_step(pe, st):
            pe_scores(pe, st, (0, 4))
            pe_shift(pe, st)
            pe_scores(pe, st, (4, 6))
            pe_xn(pe, st)
            pe_max(pe, st, (0, 2))
            pe_scores(pe, st, (6, 8))
            pe_max(pe, st, (2, 4))
            pe_q(pe, st)
            pe_exp(pe, st, (0, 4))
            pe_max(pe, st, (4, 6))
            pe_exp(pe, st, (4, 6))
            pe_max(pe, st, (6, 8))
            pe_exp(pe, st, (6, 8))
            pe_max(pe, st, (8, 10))
            pe_out(pe, st)
            pe_exp(pe, st, (8, 10))
            if st.on(3):
                pv_round(pe, st, 0)
            pe_mem(pe, st)
            pe_max(pe, st, (10, 12))
            pe_exp(pe, st, (10, 12))
            pe_kv(pe, st)
            pe_max(pe, st, (12, 14))
            pe_exp(pe, st, (12, 14))
            pe_x2(pe, st)
            pe_max(pe, st, (14, 15))
            pe_exp(pe, st, (14, 16))
            pe_logits(pe, st)
            pe_max(pe, st, (15, 16))
            misc_free(pe, st, 8)
            if st.on(3):
                pv_round(pe, st, 1)

        def copy_scores(act, st, span):
            if st.on(1):
                for i in range(*span):
                    t, c = i // 4, i % 4
                    if c == 0:
                        st.wait(act, argmax_read, st.b(1) * LT + t - 1)
                    st.wait(act, score_done, st.b(1) * 8 + i + 1)
                    nc.scalar.copy(score_sb[:, t, CSTART[c]:CSTART[c] + CHUNK[c]], ring[:, i % 2, 0:CHUNK[c]]).then_inc(score_copied, 1)

        def exp_tile(act, st, n):
            c, j = n // 2, n % 2
            st.wait(act, exp_mm, st.b(3) * 16 + n + 1)
            if n % 8 == 0:
                st.wait(act, pv_done, st.b(3) * 2 + n // 8 - 1)
            nc.scalar.activation(probs[:, j, 512 * c:512 * c + 512], lg[:, n % 2], ACT.Exp,
                                 scale=DH ** -0.5).then_inc(exp_done, 1)

        def act_exp(act, st, span):
            if st.on(3):
                for n in range(*span):
                    exp_tile(act, st, n)

        def act_att(act, st, r):
            if st.on(3):
                st.wait(act, pv_done, st.b(3) * 2 + r + 1)
                if r == 0:
                    st.wait(act, att_written, st.b(3) * 64)
                nc.scalar.copy(att_raw[:, r], pv[:, :]).then_inc(pv_copied, 1)

        def act_step(act, st):
            copy_scores(act, st, (0, 6))
            if st.on(0):
                st.wait(act, xn_t_done, st.b(0) + 1)
                st.wait(act, q_done, st.b(0))
                nc.scalar.copy(xn_t[:, :], misc[:, 0:L]).then_inc(xn_t_ready, 1)
            copy_scores(act, st, (6, 8))
            if st.on(0):
                p = st.par(0)
                st.wait(act, q_done, st.b(0) + 1)
                st.wait(act, score_done, st.b(0) * 8 - 8)
                st.wait(act, q_split, st.b(0) * 4 - 4)
                nc.scalar.copy(q_t[:, p], misc[:, 0:L]).then_inc(q_ready, 1)
            act_exp(act, st, (0, 10))
            act_att(act, st, 0)
            if st.on(1):
                st.wait(act, mem_t_done, st.b(1) + 1)
                st.wait(act, kv_done, st.b(1))
                nc.scalar.copy(mem_t[:, :], misc[:, 0:L]).then_inc(mem_t_ready, 1)
            act_exp(act, st, (10, 14))
            if st.on(4):
                st.wait(act, x2_t_done, st.b(4) + 1)
                nc.scalar.copy(x2_t[:, :], misc[:, 0:L]).then_inc(x2_t_ready, 1)
                nc.scalar.copy(x2_all[:, bass.ds(st.value(st.b(4) * L), L)], misc[:, 0:L]).then_inc(x2_t_ready, 1)
            act_exp(act, st, (14, 16))
            act_att(act, st, 1)

        def dve_argmax_value(dve, st, t):
            if st.on(1):
                st.wait(dve, score_copied, st.b(1) * 8 + 4 * t + 4)
                passed(dve, st)
                nc.vector.max(top8[:, t], score_sb[:, t]).then_inc(dve_argmax, 1)

        def dve_argmax_index(dve, st, t):
            if st.on(1):
                st.wait(dve, dve_argmax, st.b(1) * LT + t + 1)
                passed(dve, st)
                nc.vector.max_index(top_at[:, t], top8[:, t], score_sb[:, t]).then_inc(argmax_read, 1)
                st.wait(dve, argmax_read, st.b(1) * LT + t + 1)
                st.wait(dve, mem_gathered[t], st.b(1) * 16)
                passed(dve, st)
                nc.vector.tensor_tensor(row_at[:, t], top_at[:, t, 0:1], row_base[:, :], ALU.add).then_inc(row_ready, 1)
                if t == LT - 1:
                    st.wait(dve, row_ready, st.b(1) * LT + LT)
                    nc.vector.tensor_scalar(row_base[:, :], row_base[:, :], float(M), None, ALU.add).then_inc(row_base_set, 1)
                    st.wait(dve, row_base_set, st.b(1) + 2)

        def reduce_max(dve, st, span):
            if st.on(2):
                p = st.par(2)
                for n in range(*span):
                    t, hp = n // 8, n % 8
                    st.wait(dve, max_done, st.b(2) * 16 + n + 1)
                    nc.vector.tensor_reduce(row_max[:, p, t, 2 * hp:2 * hp + 2],
                                            ring[:, 2 + n % 2].rearrange("p (w m) -> p w m", w=2),
                                            AX.X, ALU.max).then_inc(max_reduced, 1)

        def dve_neg(dve, st):
            if st.on(3):
                st.wait(dve, max_reduced, st.b(3) * 16 + 16)
                st.wait(dve, shift_t_done, st.b(3))
                nc.vector.tensor_scalar(neg_max[:, :], row_max[:, st.par(3)], -1.0, None, ALU.mult).then_inc(neg_ready, 1)

        def dve_shift_parts(dve, st):
            if st.on(3):
                st.wait(dve, shift_t_done, st.b(3) + 1)
                st.wait(dve, shift_loaded, st.b(3) * 32)
                nc.vector.tensor_copy(shift_hi[:, :], misc[0:H, 0:L]).then_inc(shift_ready, 1)
                st.wait(dve, shift_ready, st.b(3) * 2 + 1)
                nc.vector.tensor_tensor(shift_lo[:, :], misc[0:H, 0:L], shift_hi[:, :], ALU.subtract).then_inc(shift_ready, 1)

        def layer_stats(dve, st, stage, xb, stats_, mean_var_, var_, link_sem, var_sem):
            ch = Chain(dve, st, link_sem, stage, 2 * LT)
            passed(dve, st)
            for t in range(LT):
                ch.link(nc.vector.bn_stats(stats_[:, t], xb[:, t]), wait=False)
            ch.wait()
            for t in range(LT):
                ch.link(nc.vector.bn_aggr(mean_var_[:, t], stats_[:, t]), wait=False)
            ch.wait()
            ch.end()
            nc.vector.tensor_scalar(var_[:, :], mean_var_[:, :, 1], EPS, None, ALU.add).then_inc(var_sem, 1)

        def batch_rows(st, stage):
            return x_in[:, bass.ds(st.value(st.b(stage) * LT), LT)]

        def dve_xn(dve, st):
            if st.on(0):
                xb = batch_rows(st, 0)
                st.wait(dve, rstd_ready, st.b(0) + 1)
                st.wait(dve, xn_t_done, st.b(0))
                for t in range(LT):
                    nc.vector.tensor_scalar(xn[:, t], xb[:, t], mean_var[:, t, 0:1], rstd[:, t:t + 1],
                                            ALU.subtract, ALU.mult).then_inc(xn_ready, 1)

        def dve_att(dve, st):
            if st.on(4):
                st.wait(dve, att_loaded, st.b(4) * 32 + 32)
                ch = Chain(dve, st, dve_out, 4, 1)
                ch.link(nc.vector.reciprocal(att_inv[:, :], att_den[:, :]))
                ch.end()
                nc.vector.tensor_tensor(att_t[:, :], att_num[:, :], att_inv[:, :], ALU.mult).then_inc(att_ready, 1)

        def dve_x1(dve, st):
            if st.on(4):
                xb = batch_rows(st, 4)
                st.wait(dve, out_done, st.b(4) + 1)
                for t in range(LT):
                    nc.vector.scalar_tensor_tensor(xb[:, t], misc[:, 128 * t:128 * t + 128], tgx[:, :], xb[:, t],
                                                   ALU.mult, ALU.add).then_inc(x1_ready, 1)
                st.wait(dve, x1_ready, st.b(4) * LT + LT)
                layer_stats(dve, st, 4, xb, stats2, mean_var2, var_eps2, dve_ln2, var2_ready)

        def dve_x2(dve, st):
            if st.on(4):
                xb = batch_rows(st, 4)
                st.wait(dve, rstd2_ready, st.b(4) + 1)
                st.wait(dve, x2_stored, st.b(4) * 16 + 1)
                for t in range(LT):
                    nc.vector.tensor_scalar(x2[:, t], xb[:, t], mean_var2[:, t, 0:1], rstd2[:, t:t + 1],
                                            ALU.subtract, ALU.mult).then_inc(x2_ready, 1)

        def dve_keys(dve, st):
            if st.on(1):
                p = st.par(1)
                ch = Chain(dve, st, dve_k, 1, 3)
                keys = misc[0:NSTACK, 0:L]
                st.wait(dve, kv_done, st.b(1) + 1)
                st.wait(dve, kv_kept, st.b(1) * 2 - 2)
                nc.vector.tensor_copy(v_raw[:, p], misc[:, L:L + LT * DH].rearrange("p (j v) -> p j v", v=DH)).then_inc(v_ready, 1)
                ch.link(nc.vector.tensor_copy(k_work[:, 0], keys))
                ch.link(nc.vector.scalar_tensor_tensor(k_rest[:, :], k_work[:, 0], kmask_sb[:, 0:1], keys, ALU.mult, ALU.add))
                ch.link(nc.vector.tensor_copy(k_work[:, 1], k_rest[:, :]))
                ch.end()
                st.wait(dve, max_done, st.b(1) * 16 - 16)
                nc.vector.scalar_tensor_tensor(k_max[:, p], k_work[:, 1], kmask_sb[:, 1:2], k_rest[:, :],
                                               ALU.mult, ALU.add).then_inc(k_ready, 1)

        def dve_logits(dve, st):
            if st.on(4):
                st.wait(dve, logit_done, st.b(4) + 1)
                nc.vector.tensor_tensor(logits[:, bass.ds(st.value(st.b(4) * LT), LT)],
                                        misc[:, 0:LT * E].rearrange("p (t e) -> p t e", e=E),
                                        bias_sb[:, :].unsqueeze(1).broadcast_to([128, LT, E]), ALU.add).then_inc(logit_ready, 1)

        def dve_step(dve, st):
            dve_neg(dve, st)
            if st.on(0):
                layer_stats(dve, st, 0, batch_rows(st, 0), stats, mean_var, var_eps, dve_ln, var_ready)
            dve_shift_parts(dve, st)
            dve_xn(dve, st)
            dve_argmax_value(dve, st, 0)
            reduce_max(dve, st, (0, 2))
            dve_argmax_index(dve, st, 0)
            reduce_max(dve, st, (2, 4))
            dve_argmax_value(dve, st, 1)
            reduce_max(dve, st, (4, 6))
            dve_argmax_index(dve, st, 1)
            reduce_max(dve, st, (6, 8))
            dve_att(dve, st)
            reduce_max(dve, st, (8, 10))
            dve_x1(dve, st)
            reduce_max(dve, st, (10, 12))
            dve_keys(dve, st)
            reduce_max(dve, st, (12, 13))
            dve_x2(dve, st)
            reduce_max(dve, st, (13, 15))
            dve_logits(dve, st)
            reduce_max(dve, st, (15, 16))

        def run(nc_engine, eng, step):
            for c in range(STAGES - 1):
                step(eng, Step(None, c))
            with eng.Fori(0, (B - STAGES + 1) // 2) as it:
                for u in range(2):
                    step(eng, Step(it, STAGES - 1 + u))
            for c in range(B, B + STAGES - 1):
                step(eng, Step(None, c))

        routed = sem("routed")
        exp_ready, mask_ready, rank_done, onehots_ready, slot_done = (
            sem("exp_ready"), sem("mask_ready"), sem("rank_done"), sem("onehots_ready"), sem("slot_done"))
        slot_ready, items_ready, items_loaded, pos_ready = sem("slot_ready"), sem("items_ready"), sem("items_loaded"), sem("pos_ready")
        sh_done, sh_silu, sh_hid, sh_out, sh_copied = sem("sh_done"), sem("sh_silu"), sem("sh_hid"), sem("sh_out"), sem("sh_copied")
        rows_gathered = [sem(f"rows_gathered{i}") for i in range(4)]
        xs_done, xs_copied = sem("xs_done"), sem("xs_copied")
        item_x, gu_done, silu_done, hid_ready = sem("item_x"), sem("gu_done"), sem("silu_done"), sem("hid_ready")
        hid_t_done, hid_t_ready, y_done, y_copied = sem("hid_t_done"), sem("hid_t_ready"), sem("y_done"), sem("y_copied")
        y_stored = [sem("y_stored0"), sem("y_stored1")]
        back_gathered = [sem(f"back_gathered{i}") for i in range(4)]
        mixed, result_ready, out_stored = sem("mixed"), sem("result_ready"), [sem(f"out_stored{i}") for i in range(4)]
        pad_zeroed = sem("pad_zeroed")
        xs_bank = [pv, misc]
        token_named, pos_named = sem("token_named"), sem("pos_named")

        def bc(ap, axis, shape):
            return ap.unsqueeze(axis).broadcast_to(shape)

        def softmax_and_top(dve):
            n = [0]

            def step(ins):
                n[0] += 1
                ins.then_inc(routed, 1)
                dve.wait_ge(routed, n[0])

            top1, total, inv, four, inv4 = (small[:, i] for i in range(5))
            ex = onehot.rearrange("p t k e -> p (t k e)")[:, 0:NT * E].rearrange("p (t e) -> p t e", e=E)
            dve.wait_ge(logit_ready, B)
            step(nc.vector.tensor_reduce(top1, logits[:, :], AX.X, ALU.max))
            step(nc.vector.tensor_tensor(logits[:, :], logits[:, :], bc(top1, 2, [128, NT, E]), ALU.subtract))
            dve.wait_ge(exp_ready, 1)
            step(nc.vector.tensor_reduce(total, logits[:, :], AX.X, ALU.add))
            step(nc.vector.reciprocal(inv, total))
            step(nc.vector.tensor_tensor(logits[:, :], logits[:, :], bc(inv, 2, [128, NT, E]), ALU.mult))
            for t in range(NT):
                ins = nc.vector.max(top_p[:, t], logits[:, t])
            step(ins)
            for t in range(NT):
                ins = nc.vector.max_index(top_e[:, t], top_p[:, t], logits[:, t])
            step(ins)
            step(nc.vector.tensor_copy(top_f[:, :], top_e[:, :, 0:K]))
            step(nc.vector.tensor_tensor(onehot, bc(bc(expert_no, 1, [128, NT, E]), 2, [128, NT, K, E]),
                                         bc(top_f[:, :], 3, [128, NT, K, E]), ALU.is_equal))
            step(nc.vector.tensor_reduce(mask[:, :], onehot.rearrange("p t k e -> p t e k"), AX.X, ALU.max))
            dve.sem_inc(mask_ready, 1)
            step(nc.vector.tensor_reduce(four, top_p[:, :, 0:K], AX.X, ALU.add))
            step(nc.vector.tensor_scalar(four, four, 1e-12, None, ALU.max))
            step(nc.vector.reciprocal(inv4, four))
            step(nc.vector.tensor_tensor(weight[:, :], top_p[:, :, 0:K], bc(inv4, 2, [128, NT, K]), ALU.mult))
            dve.wait_ge(rank_done, 1)
            cnt, tiles, tiles_to, cnt_to, tile_at, start, row_base_e, one = (counts[:, i] for i in range(8))
            step(nc.vector.tensor_copy(cnt, lg[:, 1, 0:E]))
            more = sel.rearrange("p t k e -> p (t k e)")[:, 0:E * NT].rearrange("p (e t) -> p e t", t=NT)
            step(nc.vector.tensor_tensor(more, bc(cnt, 2, [128, E, NT]), bc(tile_limit, 1, [128, E, NT]), ALU.is_gt))
            step(nc.vector.tensor_reduce(tiles, more, AX.X, ALU.add))
            step(nc.vector.memset(one, 1.0))
            step(nc.vector.tensor_tensor_scan(tiles_to, one, tiles, 0.0, ALU.mult, ALU.add))
            step(nc.vector.tensor_tensor_scan(cnt_to, one, cnt, 0.0, ALU.mult, ALU.add))
            step(nc.vector.tensor_tensor(start, cnt_to, cnt, ALU.subtract))
            step(nc.vector.tensor_tensor(tile_at, tiles_to, tiles, ALU.subtract))

            def positions(base):
                step(nc.vector.tensor_tensor(ranks[:, :], lg[:, 0].rearrange("p (t e) -> p t e", e=E), bc(base, 1, [128, NT, E]), ALU.add))
                step(nc.vector.tensor_tensor(sel, onehot, bc(ranks[:, :], 2, [128, NT, K, E]), ALU.mult))
                step(nc.vector.tensor_reduce(pos[:, :], sel, AX.X, ALU.add))

            positions(start)
            step(nc.vector.tensor_copy(pos_i[:, 0], pos[:, :]))
            step(nc.vector.tensor_scalar(pos_i[:, 1], pos_i[:, 0], 7, None, ALU.logical_shift_right))
            step(nc.vector.tensor_copy(pos_g[:, :], pos_i[:, 1]))
            step(nc.vector.scalar_tensor_tensor(pos_r[:, :], pos_g[:, :], -128.0, pos[:, :], ALU.mult, ALU.add))
            for t in range(NT):
                for k in range(K):
                    nc.vector.tensor_scalar(onehot_g[:, t * K + k], rows_f16[:, 128:128 + NDENSE], pos_g[:, t, k:k + 1],
                                            token_no[:, t:t + 1], ALU.is_equal, ALU.mult)
                    nc.vector.tensor_scalar(onehot_r[:, t * K + k], rows_f16[:, 0:128], pos_r[:, t, k:k + 1],
                                            None, ALU.is_equal).then_inc(onehots_ready, 1)
            ended, no_e, g, at_tile, at_start, off = (item[:, c:c + 1] for c in range(6))
            cmp, hot = counts[:, 8], counts[:, 9]
            step(nc.vector.tensor_scalar(cmp, tiles_to, part_no, None, ALU.is_le))
            step(nc.vector.tensor_reduce(ended, cmp, AX.X, ALU.add))
            step(nc.vector.tensor_scalar(no_e, ended, float(E - 1), None, ALU.min))
            step(nc.vector.tensor_scalar(hot, expert_no, no_e, None, ALU.is_equal))
            step(nc.vector.tensor_tensor(cmp, hot, tile_at, ALU.mult))
            step(nc.vector.tensor_reduce(at_tile, cmp, AX.X, ALU.add))
            step(nc.vector.tensor_tensor(cmp, hot, start, ALU.mult))
            step(nc.vector.tensor_reduce(at_start, cmp, AX.X, ALU.add))
            step(nc.vector.tensor_tensor(g, part_no, at_tile, ALU.subtract))
            step(nc.vector.scalar_tensor_tensor(off, g, 128.0, at_start, ALU.mult, ALU.add))
            step(nc.vector.tensor_scalar(off, off, float(NDENSE * 128), None, ALU.min))
            step(nc.vector.tensor_copy(item_i[:, 0:1], no_e))
            nc.vector.tensor_copy(item_i[:, 1:2], off).then_inc(items_ready, 1)
            dve.wait_ge(slot_done, 1)
            nc.vector.tensor_copy(slot_token[:, :], misc[:, 0:NDENSE]).then_inc(slot_ready, 1)
            step(nc.vector.tensor_scalar(row_base_e, tile_at, 128.0, None, ALU.mult))
            positions(row_base_e)
            nc.vector.tensor_copy(pos_i[:, 0], pos[:, :]).then_inc(pos_ready, 1)

        def pe_route(pe):
            pe.wait_ge(mask_ready, 1)
            flat = mask[:, :].rearrange("p t e -> p (t e)")
            nc.tensor.matmul(lg[:, 0], tri_bf[:, :], flat, start=True, stop=False)
            for s in range(1, NT):
                nc.tensor.matmul(lg[:, 0, s * E:NT * E], ones_bf[:, :], flat[:, 0:(NT - s) * E], start=False, stop=(s == NT - 1))
            for t in range(NT):
                last = nc.tensor.matmul(lg[:, 1, 0:E], ones_bf[:, :], mask[:, t], start=(t == 0), stop=(t == NT - 1))
            last.then_inc(rank_done, 1)
            for n in range(NDENSE):
                pe.wait_ge(onehots_ready, n + 1)
                last = nc.tensor.matmul(misc[:, 0:NDENSE], onehot_r[:, n], onehot_g[:, n], start=(n == 0), stop=(n == NDENSE - 1))
            last.then_inc(slot_done, 1)

        def pe_shared(pe, n):
            for c in range(SHC):
                b = 2 * (c % 2)
                if isinstance(n, int):
                    if 4 * n + c >= 2:
                        pe.wait_ge(sh_hid, 4 * n + c - 1)
                else:
                    pe.wait_ge(sh_hid, n * 4 + (c - 1))
                xs = x2_all[:, bass.ds(n * 512, 512)]
                nc.tensor.matmul(ring[:, b], sgate_sb[:, c], xs, start=True, stop=True)
                nc.tensor.matmul(ring[:, b + 1], sup_sb[:, c], xs, start=True, stop=True).then_inc(sh_done, 1)
            pe.wait_ge(sh_hid, n * 4 + 4)
            if not isinstance(n, int) or n:
                pe.wait_ge(sh_copied, n)
            for t in range(4):
                for c in range(SHC):
                    last = nc.tensor.matmul(pv[:, 128 * t:128 * t + 128], hid_s[:, c, 128 * t:128 * t + 128], sdown_sb[:, c],
                                            start=(c == 0), stop=(c == SHC - 1))
            last.then_inc(sh_out, 1)

        def act_shared(act, n):
            for c in range(SHC):
                act.wait_ge(sh_done, n * 4 + (c + 1))
                if isinstance(n, int):
                    if 4 * n + c >= 2:
                        act.wait_ge(sh_hid, 4 * n + c - 1)
                else:
                    act.wait_ge(sh_hid, n * 4 + (c - 1))
                nc.scalar.activation(silu_s[:, c % 2], ring[:, 2 * (c % 2)], ACT.Silu).then_inc(sh_silu, 1)
            act.wait_ge(sh_out, n + 1)
            nc.scalar.copy(shared.rearrange("p t d -> p (t d)")[:, bass.ds(n * 512, 512)], pv[:, :]).then_inc(sh_copied, 1)

        def dve_shared(dve, n):
            for c in range(SHC):
                dve.wait_ge(sh_silu, n * 4 + (c + 1))
                if (not isinstance(n, int) or n) and c == 0:
                    dve.wait_ge(sh_out, n)
                nc.vector.tensor_tensor(hid_s[:, c], silu_s[:, c % 2], ring[:, 2 * (c % 2) + 1], ALU.mult).then_inc(sh_hid, 1)

        def pe_xs(pe, n, u, first):
            pe.wait_ge(rows_gathered[u], (n - u) * 32 + 64)
            if not first:
                pe.wait_ge(xs_copied, n - 1)
            for g in range(4):
                last = nc.tensor.transpose(xs_bank[u][:, 128 * g:128 * g + 128], gathered[:, u, g], ident[:, :])
            last.then_inc(xs_done, 1)

        def act_xs(act, n, u, first):
            act.wait_ge(xs_done, n + 1)
            nc.scalar.copy(xs_t[:, bass.ds(n * 512, 512)], xs_bank[u][:, :]).then_inc(xs_copied, 1)

        def pool_rows(pool, n, u, first):
            if not first:
                pool.wait_ge(xs_done, n - 1)
                pool.sem_inc(waits_passed, 1)
            nc.gpsimd.tensor_copy(token_now[:, u], slot_token[:, bass.ds(n * 4, 4)]).then_inc(token_named, 1)
            pool.wait_ge(token_named, n + 1)
            if not first:
                pool.sem_inc(waits_passed, 1)
            for g in range(4):
                nc.gpsimd.indirect_dma_start(
                    out=gathered[:, u, g], out_offset=None, in_=x2_scr,
                    in_offset=bass.IndirectOffsetOnAxis(ap=token_now[:, u, g:g + 1], axis=0)).then_inc(rows_gathered[u], 16)

        def item_values(engine, at, n, c, top):
            _, values = nc.values_load_multi_w_load_instructions(
                item_row[0:1, bass.ds(at + 128 * c, n)], engines=[engine], min_val=0, max_val=top,
                skip_runtime_bounds_check_because="VectorE has clamped them to the table's range")
            return values

        def pe_gate_up(pe, q, b, first, experts):
            pe.wait_ge(item_x, q + 1)
            if not first:
                pe.wait_ge(hid_ready, q - 1)
            for w in range(2):
                e = experts[w]
                last = nc.tensor.matmul(ring[:, b, 256 * w:256 * w + 256], x_item[:, b, w], gu_sb[:, bass.ds(e, 1)].rearrange("p o n -> p (o n)"),
                                        start=True, stop=True)
            last.then_inc(gu_done, 1)

        def pe_transpose_hid(pe, q, b, first, experts):
            pe.wait_ge(hid_ready, q + 1)
            if not first:
                pe.wait_ge(hid_t_ready, q - 1)
            for w in range(2):
                last = nc.tensor.transpose(ring[:, 2 + b, 128 * w:128 * w + 128], hid[:, b, w], ident[:, :])
            last.then_inc(hid_t_done, 1)

        def pe_down(pe, q, b, first, experts):
            pe.wait_ge(hid_t_ready, q + 1)
            if not first:
                pe.wait_ge(y_copied, q - 1)
            for w in range(2):
                e = experts[w]
                last = nc.tensor.matmul(lg[:, b, 128 * w:128 * w + 128], hid_t[:, b, w], down_sb[:, bass.ds(e, 1)].rearrange("p o n -> p (o n)"),
                                        start=True, stop=True)
            last.then_inc(y_done, 1)

        def dve_item_x(dve, q, b, first, rows):
            if not first:
                dve.wait_ge(gu_done, q - 1)
            for w in range(2):
                last = nc.vector.tensor_copy(x_item[:, b, w], xs_t[:, bass.ds(rows[w], 128)])
            last.then_inc(item_x, 1)

        def dve_hid(dve, q, b, first, _):
            dve.wait_ge(silu_done, q + 1)
            if not first:
                dve.wait_ge(hid_t_done, q - 1)
            nc.vector.tensor_tensor(hid[:, b], silu_e[:, b], ring[:, b].rearrange("p (w c n) -> p w c n", w=2, c=2)[:, :, 1],
                                    ALU.mult).then_inc(hid_ready, 1)

        def act_silu(act, q, b, first, _):
            act.wait_ge(gu_done, q + 1)
            if not first:
                act.wait_ge(hid_ready, q - 1)
            nc.scalar.activation(silu_e[:, b], ring[:, b].rearrange("p (w c n) -> p w c n", w=2, c=2)[:, :, 0],
                                 ACT.Silu).then_inc(silu_done, 1)

        def act_hid_t(act, q, b, first, _):
            act.wait_ge(hid_t_done, q + 1)
            if not first:
                act.wait_ge(y_done, q - 1)
            nc.scalar.copy(hid_t[:, b].rearrange("p w n -> p (w n)"), ring[:, 2 + b, 0:256]).then_inc(hid_t_ready, 1)

        def act_y(act, q, b, first, _):
            act.wait_ge(y_done, q + 1)
            if not first:
                act.wait_ge(y_stored[b], q * 8 - 8 * b)
            nc.scalar.copy(y_sb[:, b].rearrange("p w n -> p (w n)"), lg[:, b, 0:256]).then_inc(y_copied, 1)

        def sp_y(sp, q, b, first, _):
            sp.wait_ge(y_copied, q + 1)
            if not isinstance(q, int):
                sp.sem_inc(waits_passed, 1)
            sp.dma_start(y_scr[bass.ds(q * 2, 2)].rearrange("w p d -> p w d"), y_sb[:, b]).then_inc(y_stored[b], 16)

        def run_items(eng, parts, engine=None, column=0, top=0, group=None, chase=False):
            back = max(lag for _, lag in parts)

            def turn(j, groups, wait):
                start, peeled = (0, True) if isinstance(j, int) and j == 0 else (2 * back, False)
                values = item_values(engine, j * 8 - start, 8 + start, column, top) if engine else None
                for s in range(4):
                    if wait:
                        eng.wait_ge(xs_copied, j * 2 + (s // 2 + 1))
                    for f, lag in parts:
                        if peeled and s < lag:
                            continue
                        at = start + 2 * (s - lag)
                        f(eng, j * 4 + (s - lag), (s - lag) % 2, peeled and s - lag < 2, values[at:at + 2] if engine else None)
                    if groups and s % 2:
                        group(eng, j * 2 + (2 + s // 2), s // 2, False)

            if group:
                group(eng, 0, 0, True)
                group(eng, 1, 1, True)
            turn(0, group, chase)
            last_group_turn = (NDENSE // 4 - 2) // 2
            last_chase_turn = NDENSE // 8
            split = last_group_turn if group else last_chase_turn if chase else PAIRS // 4
            with eng.Fori(1, split) as j:
                turn(j, group, chase)
            if split < PAIRS // 4:
                with eng.Fori(split, PAIRS // 4) as j:
                    turn(j, None, False)
            if back:
                values = item_values(engine, ITEMS - 2 * back, 2 * back, column, top) if engine else None
                for s in range(back):
                    for f, lag in parts:
                        if s < lag:
                            at = 2 * back + 2 * (s - lag)
                            f(eng, PAIRS + s - lag, (s - lag) % 2, False, values[at:at + 2] if engine else None)

        def pool_back(pool, n, u, first):
            if not first:
                pool.wait_ge(mixed, n * 4 - 12)
                pool.sem_inc(waits_passed, 1)
            nc.gpsimd.tensor_copy(pos_now[:, u], pos_i[:, 0].rearrange("p t k -> p (t k)")[:, bass.ds(n * K, K)]).then_inc(pos_named, 1)
            pool.wait_ge(pos_named, n + 1)
            if not first:
                pool.sem_inc(waits_passed, 1)
            for k in range(K):
                nc.gpsimd.indirect_dma_start(
                    out=back[:, u, k], out_offset=None, in_=y_scr.rearrange("g p d -> (g p) d"),
                    in_offset=bass.IndirectOffsetOnAxis(ap=pos_now[:, u, k:k + 1], axis=0)).then_inc(back_gathered[u], 16)

        def dve_mix(dve, n, u, first):
            dve.wait_ge(back_gathered[u], (n - u) * 16 + 64)
            if not first:
                dve.wait_ge(out_stored[u], (n - u) * 4)
            for k in range(K):
                acc = shared[:, bass.ds(n, 1)] if k == 0 else mix[:, u].unsqueeze(1)
                nc.vector.scalar_tensor_tensor(mix[:, u].unsqueeze(1), back[:, u, k].unsqueeze(1),
                                               weight[:, bass.ds(n, 1), k:k + 1].rearrange("p a b -> p (a b)"),
                                               acc, ALU.mult, ALU.add).then_inc(mixed, 1)
                dve.wait_ge(mixed, n * 4 + (k + 1))
            nc.vector.scalar_tensor_tensor(result[:, u].unsqueeze(1), mix[:, u].unsqueeze(1), tgf[:, :],
                                           x_in[:, bass.ds(n, 1)], ALU.mult, ALU.add).then_inc(result_ready, 1)

        def sp_out(sp, n, u):
            sp.wait_ge(result_ready, n + 1)
            if not isinstance(n, int):
                sp.sem_inc(waits_passed, 1)
            sp.dma_start(out.rearrange("b (t p) d -> p (b t) d", p=128)[:, bass.ds(n, 1)].rearrange("p o d -> p (o d)"),
                         result[:, u]).then_inc(out_stored[u], 16)

        def quads(eng, f, first_arg=True):
            for u in range(4):
                f(eng, u, u, True) if first_arg else f(eng, u, u)
            with eng.Fori(1, NT // 4) as it:
                for u in range(4):
                    f(eng, it * 4 + u, u, False) if first_arg else f(eng, it * 4 + u, u)

        block = ctx.enter_context(nc.Block())

        @block.sync
        def _(sp):
            for dst, src in ((wq_sb, wq_t), (wkr_sb, wk_rep), (wv_sb, wv_t), (wc_sb, wc_t), (kmask_sb, kmask),
                             (router_sb, router_t)):
                sp.dma_start(dst[:, :], src).then_inc(consts_loaded, 16)
            for dst, src in ((gx, g_xattn), (gf, g_ffn), (bias_sb, router_bias)):
                sp.dma_start(dst[:, :], src.rearrange("(o a) -> o a", o=1).broadcast_to([128, dst.shape[1]])).then_inc(consts_loaded, 16)
            for b in range(B):
                sp.dma_start(x_in[:, b * LT:(b + 1) * LT], x[b].rearrange("(t p) d -> p t d", p=128)).then_inc(x_loaded, 16)
            run(nc.sync, sp, sp_step)
            sp.wait_ge(items_ready, 1)
            sp.dma_start(item_row[0:1, 0:128], item_i[:, 0:1]).then_inc(items_loaded, 16)
            sp.dma_start(item_row[0:1, 128:256], item_i[:, 1:2]).then_inc(items_loaded, 16)
            run_items(sp, [(sp_y, 0)])
            quads(sp, sp_out, False)
            for b in range(2):
                sp.wait_ge(y_stored[b], 16 * PAIRS // 2)
            sp.wait_ge(x2_stored, 16 * B + 1)
            for u in range(4):
                sp.wait_ge(out_stored[u], 16 * NT // 4)

        @block.gpsimd
        def _(pool):
            nc.gpsimd.memset(ident[:, :], 0.0).then_inc(ident_ready, 1)
            pool.wait_ge(ident_ready, 1)
            nc.gpsimd.affine_select(out=ident[:, :], in_=ident[:, :], compare_op=ALU.not_equal, fill=1.0, base=0,
                                    pattern=[[-1, 128]], channel_multiplier=1).then_inc(ident_ready, 1)
            nc.gpsimd.memset(expo[:, :], -0.5).then_inc(presets, 1)
            nc.gpsimd.memset(k_exp[:, :], 1.0).then_inc(presets, 1)
            nc.gpsimd.memset(v_aug[:, :], 0.0).then_inc(presets, 1)
            pool.wait_ge(presets, 3)
            nc.gpsimd.memset(v_aug[:, :, :, DH:16], 1.0).then_inc(presets, 1)
            nc.gpsimd.memset(xs_t[:, NDENSE * 128:NDENSE * 128 + 128], 0.0).then_inc(pad_zeroed, 1)
            pool.wait_ge(presets, 4)
            run(nc.gpsimd, pool, pool_step)
            pool.wait_ge(x2_stored, 16 * B + 1)
            pool.wait_ge(slot_ready, 1)
            for u in range(2):
                pool_rows(pool, u, u, True)
            with pool.Fori(1, NDENSE // 8) as it:
                for u in range(2):
                    pool_rows(pool, it * 2 + u, u, False)
            pool.wait_ge(pos_ready, 1)
            for b in range(2):
                pool.wait_ge(y_stored[b], 16 * PAIRS // 2)
            quads(pool, pool_back)

        @block.scalar
        def _(act):
            act.dma_start(tab[:, :], table).then_inc(ffn_loaded, 16)
            act.dma_start(sgate_sb[:, :], sgate_t.rearrange("d (c h) -> d c h", c=SHC)).then_inc(ffn_loaded, 16)
            act.dma_start(sup_sb[:, :], sup_t.rearrange("d (c h) -> d c h", c=SHC)).then_inc(ffn_loaded, 16)
            act.dma_start(sdown_sb[:, :], sdown_t.rearrange("(c h) d -> h c d", c=SHC)).then_inc(ffn_loaded, 16)
            act.dma_start(gu_sb[:, :], gate_up_t).then_inc(ffn_loaded, 16)
            act.dma_start(down_sb[:, :], down_t).then_inc(ffn_loaded, 16)
            act.wait_ge(consts_loaded, 144)
            nc.scalar.activation(tgx[:, :], gx[:, :], ACT.Tanh).then_inc(tanh_ready, 1)
            nc.scalar.activation(tgf[:, :], gf[:, :], ACT.Tanh).then_inc(tanh_ready, 1)
            run(nc.scalar, act, act_step)
            act.wait_ge(routed, 2)
            nc.scalar.activation(logits[:, :], logits[:, :], ACT.Exp).then_inc(exp_ready, 1)
            act_shared(act, 0)
            with act.Fori(1, NT // 4) as it:
                act_shared(act, it)
            run_items(act, [(act_silu, 0), (act_hid_t, 1), (act_y, 2)], group=act_xs)

        @block.tensor
        def _(pe):
            pe.wait_ge(ident_ready, 2)
            pe.wait_ge(presets, 4)
            pe.wait_ge(consts_loaded, 144)
            run(nc.tensor, pe, pe_step)
            pe_route(pe)
            pe.wait_ge(ffn_loaded, 96)
            pe_shared(pe, 0)
            with pe.Fori(1, NT // 4) as it:
                pe_shared(pe, it)
            pe.wait_ge(sh_copied, NT // 4)
            pe.wait_ge(items_loaded, 32)
            run_items(pe, [(pe_gate_up, 0), (pe_transpose_hid, 1), (pe_down, 2)], mybir.EngineType.PE, 0, E - 1, group=pe_xs)

        @block.vector
        def _(dve):
            nc.vector.memset(row_base[:, :], 0).then_inc(row_base_set, 1)
            nc.vector.memset(x2[:, :], 0.0).then_inc(x2_stored, 1)
            nc.vector.memset(ones_bf[:, :], 1.0)
            dve.wait_ge(row_base_set, 1)
            dve.wait_ge(consts_loaded, 144)
            dve.wait_ge(tanh_ready, 2)
            dve.wait_ge(x_loaded, B * 16)
            run(nc.vector, dve, dve_step)
            dve.wait_ge(ffn_loaded, 96)
            nc.vector.tensor_copy(tri_bf[:, :], triangle)
            nc.vector.tensor_copy(rows_f16[:, 0:128], row_no)
            nc.vector.tensor_copy(rows_f16[:, 128:128 + NDENSE], dense_no)
            softmax_and_top(dve)
            dve_shared(dve, 0)
            with dve.Fori(1, NT // 4) as it:
                dve_shared(dve, it)
            dve.wait_ge(pad_zeroed, 1)
            dve.wait_ge(items_loaded, 32)
            run_items(dve, [(dve_hid, 2), (dve_item_x, 0)], mybir.EngineType.DVE, 1, NDENSE * 128, chase=True)
            dve.wait_ge(sh_copied, NT // 4)
            quads(dve, dve_mix)


def kernel(**inp):
    import numpy as np
    import concourse.bacc as bacc
    from concourse.bass_utils import run_bass_kernel_spmd

    f = {k: np.ascontiguousarray(v) for k, v in inp.items()}
    ctx_in = f["ctx_1024"]
    wkv = f["L0_xattn_Wkv"]
    order = [8 * (8 * r + 2 * j + w) + dd for j in range(4) for dd in range(DH) for r in range(2) for w in range(2)]
    mask = np.zeros((NSTACK, 2), np.float32)
    mask[24:, 0] = -1.0
    mask[40:, 1] = -1.0
    part = np.arange(128, dtype=np.float32)[:, None]

    def row(n, scale=1):
        return np.tile(np.arange(n, dtype=np.float32) * scale, (128, 1))

    table = np.concatenate([row(E), row(NT, 128), row(NT, 128) + part, part, row(NDENSE), row(128),
                            np.triu(np.ones((128, 128), np.float32), 1)], 1)
    gate, up, down = (f["L0_ffn_" + n] for n in ("gate_w", "up_w", "down_w"))
    arrays = {
        "x": f["x"], "ctx_rows": ctx_in.reshape(B * M, D), "ctx_t": ctx_in.transpose(0, 2, 1), "wq_t": f["L0_xattn_Wq"].T,
        "wk_rep": np.tile(wkv[0:DH].T, (1, 6)), "wv_t": wkv[DH:].T, "wc_t": f["L0_xattn_Wc"].T[order],
        "kmask": mask, "g_xattn": f["g_xattn"], "g_ffn": f["g_ffn"], "table": table,
        "router_t": f["L0_ffn_router_w"].T, "router_bias": f["L0_ffn_router_bias"],
        "gate_up_t": np.concatenate([gate, up], 1).transpose(2, 0, 1), "down_t": down.transpose(2, 0, 1),
        "sgate_t": f["L0_ffn_sgate_w"].T, "sup_t": f["L0_ffn_sup_w"].T, "sdown_t": f["L0_ffn_sdown_w"].T,
    }
    arrays = {k: np.ascontiguousarray(v) for k, v in arrays.items()}
    nc = bacc.Bacc("TRN2", target_bir_lowering=False, num_devices=1)
    args = [nc.dram_tensor("in_" + k, v.shape, mybir.dt.from_np(v.dtype), kind="ExternalInput").ap() for k, v in arrays.items()]
    out = nc.dram_tensor("out", (B, L, D), F32, kind="ExternalOutput").ap()
    build(nc, *args, out)
    r = run_bass_kernel_spmd(nc, [{"in_" + k: v for k, v in arrays.items()}], core_ids=[0])
    return r.results[0]["out"]
```

```python
import concourse.bass as bass
from concourse import mybir
from contextlib import ExitStack

F32, BF16, F16, U32 = mybir.dt.float32, mybir.dt.bfloat16, mybir.dt.float16, mybir.dt.uint32
ALU, ACT, AX = mybir.AluOpType, mybir.ActivationFunctionType, mybir.AxisListType

B, L, D, M = 8, 256, 128, 1601
H, DH = 16, 8
LT = L // 128
CHUNK = [401, 400, 400, 400]
CSTART = [0, 401, 801, 1201]
NSTACK = 48
EPS = 1e-5
CONST_LOADS, FFN_LOADS = 8, 12
NT = B * L // 128
E, K, HID = 32, 4, 128
SHC = 4
NDENSE = NT * K
ITEMS = NDENSE + E
PAIRS = ITEMS // 2
TABLE = E + NT + 1 + 128
GPSIMD_CHUNKS = [(1, 0), (1, 1), (1, 2), (1, 3)]
STAGES = 5


class Count:

    def __init__(self, per, const):
        self.per, self.const = per, const

    def __mul__(self, k):
        return Count(self.per * k, self.const * k)

    def __add__(self, k):
        return Count(self.per, self.const + k)

    def __sub__(self, k):
        return self + -k


class Step:

    def __init__(self, it, c):
        self.it, self.c = it, c

    def on(self, stage):
        return 0 <= self.c - stage < B if self.it is None else True

    def b(self, stage):
        return Count(2, self.c - stage)

    def half(self, stage):
        return Count(1, (self.c - stage) // 2)

    def par(self, stage):
        return (self.c - stage) % 2

    def value(self, count):
        if self.it is None:
            return count.const
        return self.it * count.per + count.const

    def wait(self, eng, sem, count):
        if self.it is None and count.const <= 0:
            return
        assert count.const > 0, (sem, count.const)
        eng.wait_ge(sem, self.value(count))


def build(nc, x, ctx_rows, ctx_t, wq_t, wk_rep, wv_t, wc_t, kmask, g_xattn, g_ffn, table, repeats, router_t, router_bias,
          gate_up_t, down_t, sgate_t, sup_t, sdown_t, out):
    ctx = ExitStack()
    with ctx:
        def sb(name, shape, dt=F32):
            return ctx.enter_context(nc.sbuf_tensor(name, shape, dt))

        def ps(name, shape, dt=F32):
            return ctx.enter_context(nc.psum_tensor(name, shape, dt))

        def sem(name):
            return ctx.enter_context(nc.semaphore(name))

        def sem2(name):
            return [sem(name + "0"), sem(name + "1")]

        q_scr = nc.dram_tensor("q_scr", (B, 3, DH, H, L), BF16).ap()
        att_scr = nc.dram_tensor("att_scr", (B, 4, 16, 1024), F32).ap()
        x2_scr = nc.dram_tensor("x2_scr", (B * L, D), F32).ap()
        y_scr = nc.dram_tensor("y_scr", (ITEMS, 128, D), F32).ap()
        ident = sb("ident", [128, 128])
        wq_sb, wkr_sb, wv_sb, wc_sb = sb("wq_sb", [D, D]), sb("wkr_sb", [D, NSTACK]), sb("wv_sb", [D, DH]), sb("wc_sb", [D, D])
        kmask_sb = sb("kmask_sb", [NSTACK, 2])
        expo = sb("expo", [128, LT])
        gx = sb("gx", [128, 1])
        tgx = sb("tgx", [128, 1])
        x_in = sb("x_in", [128, B * LT, D])
        stats = sb("stats", [128, LT, 6])
        mean_var = sb("mean_var", [128, LT, 2])
        var_eps = sb("var_eps", [128, LT])
        rstd = sb("rstd", [128, LT])
        xn = sb("xn", [128, LT, D])
        xn_t = sb("xn_t", [D, L])
        q_t = sb("q_t", [D, 2, L])
        q_parts = sb("q_parts", [D, 3, L], BF16)
        q_rest = sb("q_rest", [D, 2, L])
        wide = sb("wide", [128, 4 * M])
        ctx_sb = wide[:, 0:2 * M].rearrange("p (b m) -> p b m", b=2)
        score_sb = wide[:, 2 * M:4 * M].rearrange("p (t m) -> p t m", t=LT)
        top8 = sb("top8", [128, LT, 8])
        top_at = sb("top_at", [128, LT, 8], U32)
        row_base = sb("row_base", [128, 1], U32)
        row_at = sb("row_at", [128, LT, 1], U32)
        mem = sb("mem", [128, LT, D])
        mem_t = sb("mem_t", [D, L])
        k_work = sb("k_work", [NSTACK, 2, L], BF16)
        keys = sb("keys", [NSTACK, L])
        k_rest = sb("k_rest", [NSTACK, 2, L])
        k_max = sb("k_max", [NSTACK, 2, L], BF16)
        v_raw = sb("v_raw", [128, 2, LT, DH])
        stacks = sb("stacks", [128, 4 * H * L + 256], BF16)
        q_max = stacks[0:NSTACK, 0:2 * H * L].rearrange("p (b n) -> p b n", b=2)
        q_exp = stacks[0:NSTACK + 2, 2 * H * L:4 * H * L].rearrange("p (b n) -> p b n", b=2)
        k_exp = sb("k_exp", [NSTACK + 2, 2, L], BF16)
        v_aug = sb("v_aug", [128, 2, LT, 32])
        row_max = sb("row_max", [128, 2, LT, H])
        neg_max = sb("neg_max", [128, LT, H])
        shift_hi = sb("shift_hi", [H, L], BF16)
        shift_lo = sb("shift_lo", [H, L], BF16)
        probs = sb("probs", [128, LT, H * L])
        att_raw = sb("att_raw", [128, 2, 512])
        att_num = sb("att_num", [D, L])
        att_den = sb("att_den", [D, L])
        att_inv = sb("att_inv", [D, L])
        att_t = sb("att_t", [D, L])
        stats2 = sb("stats2", [128, LT, 6])
        mean_var2 = sb("mean_var2", [128, LT, 2])
        var_eps2 = sb("var_eps2", [128, LT])
        rstd2 = sb("rstd2", [128, LT])
        x2 = sb("x2", [128, LT, D])
        x2_t = sb("x2_t", [D, L])
        x2_all = sb("x2_all", [D, B * L])
        logits = sb("logits", [128, NT, E])
        router_sb, bias_sb = sb("router_sb", [D, E]), sb("bias_sb", [128, E])
        gu_sb = sb("gu_sb", [D, E, 2 * HID])
        down_sb = sb("down_sb", [HID, E, D])
        sgate_sb, sup_sb = sb("sgate_sb", [D, SHC, 128]), sb("sup_sb", [D, SHC, 128])
        sdown_sb = sb("sdown_sb", [128, SHC, D])
        gf, tgf = sb("gf", [128, 1]), sb("tgf", [128, 1])
        tab = sb("tab", [128, TABLE])
        at = 0
        views = []
        for n in (E, NT, 1, 128):
            views.append(tab[:, at:at + n])
            at += n
        expert_no, token_no, part_no, triangle = views
        tri_bf, ones_bf = sb("tri_bf", [128, 128], BF16), sb("ones_bf", [128, 128], BF16)
        token_f16 = sb("token_f16", [128, NT], F16)
        small = sb("small", [128, 8, NT])
        top_p = sb("top_p", [128, NT, 8])
        top_e = sb("top_e", [128, NT, 8], U32)
        top_f = sb("top_f", [128, K, NT], F16)
        weight = sb("weight", [128, NT, K])
        mask = sb("mask", [128, E, NT], BF16)
        ranks = sb("ranks", [128, E, NT])
        tiles_i = sb("tiles_i", [128, E], U32)
        counts = sb("counts", [128, 10, E])
        pos = sb("pos", [128, K, NT])
        pos_i = sb("pos_i", [128, 2, K, NT], U32)
        pos_g, pos_r = sb("pos_g", [128, K, NT], F16), sb("pos_r", [128, K, NT], F16)
        slot_token = sb("slot_token", [128, NDENSE], U32)
        token_now, pos_now = sb("token_now", [128, 4, 4], U32), sb("pos_now", [128, 4, K], U32)
        item = sb("item", [128, 8])
        item_i = sb("item_i", [128, 2], U32)
        item_row = sb("item_row", [1, 2 * 128], U32)
        flat_probs = probs[:, :, :].rearrange("p t n -> p (t n)")
        onehot = flat_probs[:, 0:1024].bitcast(F16).rearrange("p (e k t) -> p e k t", e=E, k=K)
        half_mask = flat_probs[:, 1024:1536].bitcast(F16).rearrange("p (e k t) -> p e k t", e=E, k=2)
        onehot_r = flat_probs[:, 2048:2048 + 4096].bitcast(F16).rearrange("p (k r t) -> p k r t", k=K, t=NT)
        onehot_g = flat_probs[:, 6144:8192].bitcast(F16).rearrange("p (k g t) -> p k g t", k=K, t=NT)
        xs_t = stacks[:, :].bitcast(F32)
        silu_s = xs_t[:, 0:1024].rearrange("p (b n) -> p b n", b=2)
        up_s = xs_t[:, 1024:2048].rearrange("p (b n) -> p b n", b=2)
        reps = xs_t[:, 2048:4096].bitcast(F16)
        expert_rep = reps[:, 0:E * K * NT].rearrange("p (e k t) -> p e k t", e=E, k=K)
        row_rep = reps[:, E * K * NT:E * K * NT + 128 * NT].rearrange("p (r t) -> p r t", t=NT)
        hid_s = xs_t[:, 4096:6144].rearrange("p (c n) -> p c n", c=SHC)
        shared = wide[:, 0:2048].rearrange("p (t d) -> p t d", d=D)
        gathered = wide[:, 2048:4096].rearrange("p (b g d) -> p b g d", b=4, g=4)
        back = wide[:, 4096:6144].rearrange("p (b k d) -> p b k d", b=4, k=K)
        sel = back.rearrange("p b k d -> p (b k d)").rearrange("p (e k t) -> p e k t", e=E, k=K)
        w_item = flat_probs[:, 0:2048].rearrange("p (b w n) -> p b w n", b=4, w=2)
        silu_e = flat_probs[:, 2048:2560].rearrange("p (b w n) -> p b w n", b=2, w=2)
        hid = flat_probs[:, 2560:3072].rearrange("p (b w n) -> p b w n", b=2, w=2)
        mix = flat_probs[:, 5120:5632].rearrange("p (b n) -> p b n", b=4)
        result = flat_probs[:, 5632:6144].rearrange("p (b n) -> p b n", b=4)
        y_sb = flat_probs[:, 6144:6656].rearrange("p (b w n) -> p b w n", b=2, w=2)
        ffn_loaded, x2_stored = sem("ffn_loaded"), sem("x2_stored")
        dve_ln2, var2_ready, rstd2_ready, x2_ready = sem("dve_ln2"), sem("var2_ready"), sem("rstd2_ready"), sem("x2_ready")
        x2_t_done, x2_t_ready, logit_done, logit_ready = sem("x2_t_done"), sem("x2_t_ready"), sem("logit_done"), sem("logit_ready")
        ring = ps("ring", [128, 4, 512])
        lg = ps("lg", [128, 2, 512])
        pv = ps("pv", [128, 512])
        misc = ps("misc", [128, 512])

        consts_loaded, ident_ready, presets, row_base_set = sem("consts_loaded"), sem("ident_ready"), sem("presets"), sem("row_base_set")
        tanh_ready = sem("tanh_ready")
        waits_passed = sem("waits_passed")
        x_first, x_loaded, wq_loaded, ctx_loaded = sem("x_first"), sem("x_loaded"), sem("wq_loaded"), sem2("ctx_loaded")
        q_written = sem2("q_written")
        q_max_loaded, q_exp_loaded = sem2("q_max_loaded"), sem2("q_exp_loaded")
        shift_loaded = sem("shift_loaded")
        mem_gathered = [sem("mem_gathered0"), sem("mem_gathered1")]
        att_written, att_loaded = sem("att_written"), sem("att_loaded")
        dve_ln, dve_argmax, pool_k, dve_out = sem("dve_ln"), sem("dve_argmax"), sem("pool_k"), sem("dve_out")
        var_ready, rstd_ready, xn_ready, xn_t_done, xn_t_ready = sem("var_ready"), sem("rstd_ready"), sem("xn_ready"), sem("xn_t_done"), sem("xn_t_ready")
        q_done, q_ready, q_split = sem("q_done"), sem("q_ready"), sem("q_split")
        score_done, score_copied, argmax_read, row_ready = sem("score_done"), sem("score_copied"), sem("argmax_read"), sem("row_ready")
        mem_t_done, mem_t_ready, kv_done, kv_copied, k_ready = sem("mem_t_done"), sem("mem_t_ready"), sem("kv_done"), sem("kv_copied"), sem("k_ready")
        kv_kept = sem("kv_kept")
        max_done, max_reduced = sem("max_done"), sem("max_reduced")
        neg_ready, shift_t_done, shift_ready = sem("neg_ready"), sem("shift_t_done"), sem("shift_ready")
        exp_mm, exp_done, pv_done, pv_copied = sem("exp_mm"), sem("exp_done"), sem("pv_done"), sem("pv_copied")
        att_ready, out_done, x1_ready = sem("att_ready"), sem("out_done"), sem("x1_ready")

        def passed(eng, st):
            if st.it is not None:
                eng.sem_inc(waits_passed, 1)

        class Chain:

            def __init__(self, eng, st, sm, stage, per):
                self.eng, self.st, self.sm, self.base, self.per, self.n = eng, st, sm, st.b(stage) * per, per, 0

            def link(self, ins, wait=True):
                self.n += 1
                ins.then_inc(self.sm, 1)
                if wait:
                    self.wait()

            def wait(self):
                self.st.wait(self.eng, self.sm, self.base + self.n)
                passed(self.eng, self.st)

            def end(self):
                assert self.n == self.per, self.n

        def dram_batch(ap, st, stage):
            return ap[bass.ds(st.value(st.b(stage)), 1)]

        def sp_att(sp, st):
            if st.on(4):
                st.wait(sp, pv_copied, st.b(4) * 2 + 2)
                passed(sp, st)
                a = dram_batch(att_scr, st, 4)
                for j in range(4):
                    sp.dma_start(a[:, j].rearrange("o c n -> (o c) n"), att_raw[32 * j:32 * j + 16].rearrange("p r n -> p (r n)")).then_inc(att_written, 16)
            if st.on(4):
                st.wait(sp, att_written, st.b(4) * 64 + 64)
                passed(sp, st)
                a = dram_batch(att_scr, st, 4)
                sp.dma_start(att_num[:, :], a[:, :, 0:DH].rearrange("o j c (g l) -> (o j) (c g) l", l=L)).then_inc(att_loaded, 16)
                sp.dma_start(att_den[:, :], a[:, :, DH:16].rearrange("o j c (g l) -> (o j) (c g) l", l=L)).then_inc(att_loaded, 16)

        def sp_last_att(sp):
            st = Step(None, B + 2)
            st.wait(sp, max_done, Count(0, 16 * B))
            for p in range(2):
                st.wait(sp, q_exp_loaded[p], Count(0, 16 * B // 2))
            sp.dma_start(reps, repeats).then_inc(reps_loaded, 16)
            sp_att(sp, Step(None, B + 3))

        def sp_ctx(sp, st):
            if st.on(0):
                p = st.par(0)
                st.wait(sp, score_done, st.b(0) * 8 - 8)
                passed(sp, st)
                sp.dma_start(ctx_sb[:, p], dram_batch(ctx_t, st, 0).rearrange("o d m -> (o d) m")).then_inc(ctx_loaded[p], 16)

        def sp_q(sp, st):
            if st.on(0):
                st.wait(sp, q_split, st.b(0) * 4 + 4)
                passed(sp, st)
                a = dram_batch(q_scr, st, 0)
                for s in range(3):
                    sp.dma_start(a[:, s].rearrange("o dd h l -> (o h) dd l"), q_parts[:, s]).then_inc(q_written[st.par(0)], 16)

        def sp_q_max(sp, st):
            if st.on(1):
                p = st.par(1)
                st.wait(sp, q_written[p], st.half(1) * 48 + 48)
                passed(sp, st)
                st.wait(sp, max_done, st.b(1) * 16 - 16)
                passed(sp, st)
                st.wait(sp, q_exp_loaded[p], st.half(1) * 16)
                passed(sp, st)
                a = dram_batch(q_scr, st, 1).rearrange("o s dd h l -> (o s dd) (h l)")
                sp.dma_start(q_max[0:24, p], a).then_inc(q_max_loaded[p], 16)
                sp.dma_start(q_max[24:40, p], a[0:16]).then_inc(q_max_loaded[p], 16)
                sp.dma_start(q_max[40:48, p], a[0:8]).then_inc(q_max_loaded[p], 16)

        def sp_q_exp(sp, st):
            if st.on(2):
                p = st.par(2)
                st.wait(sp, q_max_loaded[p], st.half(2) * 48 + 48)
                passed(sp, st)
                st.wait(sp, exp_mm, st.b(2) * 16 - 16)
                passed(sp, st)
                sp.dma_start(q_exp[0:NSTACK, p], q_max[:, p]).then_inc(q_exp_loaded[p], 16)

        def sp_shift(sp, st):
            if st.on(3):
                p = st.par(3)
                st.wait(sp, shift_ready, st.b(3) * 2 + 2)
                passed(sp, st)
                sp.dma_start(q_exp[NSTACK:NSTACK + 1, p], shift_hi[:, :]).then_inc(shift_loaded, 16)
                sp.dma_start(q_exp[NSTACK + 1:NSTACK + 2, p], shift_lo[:, :]).then_inc(shift_loaded, 16)

        def sp_x2(sp, st):
            if st.on(4):
                st.wait(sp, x2_ready, st.b(4) * LT + LT)
                passed(sp, st)
                sp.dma_start(dram_batch(x2_scr.rearrange("(b n) d -> b n d", b=B), st, 4).rearrange("o (t p) d -> p (o t) d", p=128),
                             x2[:, :, :]).then_inc(x2_stored, 16)

        def sp_step(sp, st):
            sp_ctx(sp, st)
            sp_q_exp(sp, st)
            sp_shift(sp, st)
            sp_q_max(sp, st)
            if st.it is not None or st.c < B + 3:
                sp_att(sp, st)
            if st.it is None and st.c == B + 2:
                sp_last_att(sp)
            sp_x2(sp, st)
            sp_q(sp, st)

        def pool_rstd(pool, st):
            if st.on(0):
                st.wait(pool, var_ready, st.b(0) + 1)
                nc.gpsimd.tensor_tensor(rstd[:, :], var_eps[:, :], expo[:, :], ALU.pow).then_inc(rstd_ready, 1)

        def pool_keys(pool, st):
            if st.on(2):
                p = st.par(2)
                st.wait(pool, k_ready, st.b(2) + 1)
                st.wait(pool, kv_copied, st.b(2) * 2 + 2)
                st.wait(pool, exp_mm, st.b(2) * 16 - 16)
                passed(pool, st)
                nc.gpsimd.tensor_copy(k_exp[0:NSTACK, p], k_max[:, p]).then_inc(kv_kept, 1)
                st.wait(pool, pv_done, st.b(2) * 2 - 2)
                passed(pool, st)
                nc.gpsimd.tensor_copy(v_aug[:, p, :, 0:DH], v_raw[:, p]).then_inc(kv_kept, 1)

        def pool_k_parts(pool, st):
            if st.on(1):
                p = st.par(1)
                ch = Chain(pool, st, pool_k, 1, 5)
                st.wait(pool, kv_copied, st.b(1) * 2 + 2)
                passed(pool, st)
                ch.link(nc.gpsimd.tensor_copy(k_work[:, 0], keys[:, :]))
                ch.link(nc.gpsimd.tensor_tensor(k_rest[:, 0], k_work[:, 0], kmask_sb[:, 0:1].broadcast_to([NSTACK, L]), ALU.mult))
                ch.link(nc.gpsimd.tensor_tensor(k_rest[:, 0], k_rest[:, 0], keys[:, :], ALU.add))
                ch.link(nc.gpsimd.tensor_copy(k_work[:, 1], k_rest[:, 0]))
                ch.link(nc.gpsimd.tensor_tensor(k_rest[:, 1], k_work[:, 1], kmask_sb[:, 1:2].broadcast_to([NSTACK, L]), ALU.mult))
                ch.end()
                st.wait(pool, max_done, st.b(1) * 16 - 16)
                nc.gpsimd.tensor_tensor(k_max[:, p], k_rest[:, 1], k_rest[:, 0], ALU.add).then_inc(k_ready, 1)

        def pool_gather(pool, st, t):
            if st.on(1):
                st.wait(pool, row_ready, st.b(1) * LT + t + 1)
                st.wait(pool, mem_t_done, st.b(1))
                passed(pool, st)
                nc.gpsimd.indirect_dma_start(
                    out=mem[:, t], out_offset=None, in_=ctx_rows,
                    in_offset=bass.IndirectOffsetOnAxis(ap=row_at[:, t], axis=0)).then_inc(mem_gathered[t], 16)

        def pool_rstd2(pool, st):
            if st.on(4):
                st.wait(pool, var2_ready, st.b(4) + 1)
                nc.gpsimd.tensor_tensor(rstd2[:, :], var_eps2[:, :], expo[:, :], ALU.pow).then_inc(rstd2_ready, 1)

        def pool_split(pool, st):
            if st.on(0):
                p = st.par(0)
                st.wait(pool, q_ready, st.b(0) + 1)
                if st.it is None:
                    st.wait(pool, q_written[1 - p], Count(0, 48 * ((st.c + 1) // 2)) if p == 1 else Count(0, 48 * (st.c // 2)))
                else:
                    st.wait(pool, q_written[1 - p], (st.half(0) + p) * 48)
                q = q_t[:, p]
                passed(pool, st)
                nc.gpsimd.tensor_copy(q_parts[:, 0], q).then_inc(q_split, 1)
                st.wait(pool, q_split, st.b(0) * 4 + 1)
                nc.gpsimd.tensor_tensor(q_rest[:, 0], q, q_parts[:, 0], ALU.subtract).then_inc(q_split, 1)
                st.wait(pool, q_split, st.b(0) * 4 + 2)
                passed(pool, st)
                nc.gpsimd.tensor_copy(q_parts[:, 1], q_rest[:, 0]).then_inc(q_split, 1)
                st.wait(pool, q_split, st.b(0) * 4 + 3)
                nc.gpsimd.tensor_tensor(q_parts[:, 2], q_rest[:, 0], q_parts[:, 1], ALU.subtract).then_inc(q_split, 1)

        def pool_step(pool, st):
            pool_rstd(pool, st)
            pool_gather(pool, st, 0)
            pool_gather(pool, st, 1)
            pool_keys(pool, st)
            pool_split(pool, st)
            pool_rstd2(pool, st)
            pool_k_parts(pool, st)

        def score_fill(pe, st, stage, i):
            p, t, c = st.par(stage), i // 4, i % 4
            st.wait(pe, score_copied, st.b(stage) * 8 + i - 1)
            nc.tensor.matmul(ring[:, i % 2, 0:CHUNK[c]], q_t[:, p, 128 * t:128 * t + 128], ctx_sb[:, p, CSTART[c]:CSTART[c] + CHUNK[c]],
                             start=True, stop=True).then_inc(score_done, 1)

        def max_fill(pe, st, n):
            p, t, hp = st.par(2), n // 8, n % 8
            st.wait(pe, max_reduced, st.b(2) * 16 + n - 1)
            for w in range(2):
                h = 2 * hp + w
                last = nc.tensor.matmul(ring[:, 2 + n % 2, 256 * w:256 * w + 256],
                                        q_max[:, p, h * L + 128 * t:h * L + 128 * t + 128], k_max[:, p],
                                        start=True, stop=True)
            last.then_inc(max_done, 1)

        def exp_bank(st, n):
            if st.it is None and st.c > B:
                return (lg[:, 0], lg[:, 1], ring[:, 0], ring[:, 1])[n % 4]
            return lg[:, n % 2]

        def exp_fill(pe, st, n):
            p = st.par(3)
            c, j = n // 2, n % 2
            if st.it is None and st.c == B + 1 and 2 <= n < 4:
                pe.wait_ge(score_copied, 8 * B)
            elif st.it is None and st.c > B and (n >= 4 or st.c > B + 1):
                st.wait(pe, exp_done, st.b(3) * 16 + n - 3)
            else:
                st.wait(pe, exp_done, st.b(3) * 16 + n - 1)
            nc.tensor.matmul(exp_bank(st, n), k_exp[:, p, 128 * j:128 * j + 128], q_exp[:, p, 512 * c:512 * c + 512],
                             start=True, stop=True).then_inc(exp_mm, 1)

        def pv_round(pe, st, stage, r):
            if not st.on(stage):
                return
            p = st.par(stage)
            st.wait(pe, kv_kept, st.b(stage) * 2 + 2)
            st.wait(pe, exp_done, st.b(stage) * 16 + 8 * r + 8)
            st.wait(pe, pv_copied, st.b(stage) * 2 + r)
            for j in range(LT):
                for g in range(4):
                    c = 4 * r + g
                    last = nc.tensor.matmul(pv[32 * g:32 * g + 32], v_aug[:, p, j], probs[:, j, 512 * c:512 * c + 512],
                                            start=(j == 0), stop=(j == LT - 1))
            last.then_inc(pv_done, 1)

        def pe_scores(pe, st, stage, span):
            if st.on(stage):
                if span[0] == 0:
                    st.wait(pe, q_ready, st.b(stage) + 1)
                    st.wait(pe, ctx_loaded[st.par(stage)], st.half(stage) * 16 + 16)
                for i in range(*span):
                    score_fill(pe, st, stage, i)

        def pe_max(pe, st, span):
            if st.on(2):
                if span[0] == 0:
                    st.wait(pe, k_ready, st.b(2) + 1)
                    st.wait(pe, q_max_loaded[st.par(2)], st.half(2) * 48 + 48)
                for n in range(*span):
                    max_fill(pe, st, n)

        def pe_exp(pe, st, span):
            if st.on(3):
                if span[0] == 0:
                    st.wait(pe, shift_loaded, st.b(3) * 32 + 32)
                    st.wait(pe, q_exp_loaded[st.par(3)], st.half(3) * 16 + 16)
                    st.wait(pe, kv_kept, st.b(3) * 2 + 1)
                for n in range(*span):
                    exp_fill(pe, st, n)

        def misc_free(pe, st, use):
            readers = [(3, shift_ready, 2), (0, xn_t_ready, 1), (0, q_ready, 1), (4, x1_ready, LT), (1, mem_t_ready, 1),
                       (1, kv_copied, 2), (4, x2_t_ready, 2), (4, logit_ready, 1)]
            for step_, uses in ((st, range(use - 1, -1, -1)), (Step(st.it, st.c - 1), range(len(readers) - 1, -1, -1))):
                for n in uses:
                    stage, sm, per = readers[n]
                    if step_.on(stage):
                        st.wait(pe, sm, step_.b(stage) * per + (per + (sm is logit_ready)))
                        return

        def pe_shift(pe, st):
            if st.on(3):
                st.wait(pe, neg_ready, st.b(3) + 1)
                misc_free(pe, st, 0)
                for t in range(LT):
                    last = nc.tensor.transpose(misc[0:H, 128 * t:128 * t + 128], neg_max[:, t], ident[:, :])
                last.then_inc(shift_t_done, 1)

        def pe_xn(pe, st):
            if st.on(0):
                st.wait(pe, xn_ready, st.b(0) * LT + LT)
                misc_free(pe, st, 1)
                for t in range(LT):
                    last = nc.tensor.transpose(misc[:, 128 * t:128 * t + 128], xn[:, t], ident[:, :])
                last.then_inc(xn_t_done, 1)

        def pe_q(pe, st):
            if st.on(0):
                misc_free(pe, st, 2)
                nc.tensor.matmul(misc[:, 0:L], wq_sb[:, :], xn_t[:, :], start=True, stop=True).then_inc(q_done, 1)

        def pe_out(pe, st):
            if st.on(4):
                st.wait(pe, att_ready, st.b(4) + 1)
                misc_free(pe, st, 3)
                for t in range(LT):
                    last = nc.tensor.matmul(misc[:, 128 * t:128 * t + 128], att_t[:, 128 * t:128 * t + 128], wc_sb[:, :],
                                            start=True, stop=True)
                last.then_inc(out_done, 1)

        def pe_mem(pe, st):
            if st.on(1):
                misc_free(pe, st, 4)
                for t in range(LT):
                    st.wait(pe, mem_gathered[t], st.b(1) * 16 + 16)
                    last = nc.tensor.transpose(misc[:, 128 * t:128 * t + 128], mem[:, t], ident[:, :])
                last.then_inc(mem_t_done, 1)

        def pe_kv(pe, st):
            if st.on(1):
                misc_free(pe, st, 5)
                nc.tensor.matmul(misc[0:NSTACK, 0:L], wkr_sb[:, :], mem_t[:, :], start=True, stop=True)
                for j in range(LT):
                    last = nc.tensor.matmul(misc[:, L + DH * j:L + DH * j + DH], mem_t[:, 128 * j:128 * j + 128], wv_sb[:, :],
                                            start=True, stop=True)
                last.then_inc(kv_done, 1)

        def pe_x2(pe, st):
            if st.on(4):
                st.wait(pe, x2_ready, st.b(4) * LT + LT)
                misc_free(pe, st, 6)
                for t in range(LT):
                    last = nc.tensor.transpose(misc[:, 128 * t:128 * t + 128], x2[:, t], ident[:, :])
                last.then_inc(x2_t_done, 1)

        def pe_logits(pe, st):
            if st.on(4):
                misc_free(pe, st, 7)
                for t in range(LT):
                    last = nc.tensor.matmul(misc[:, E * t:E * t + E], x2_t[:, 128 * t:128 * t + 128], router_sb[:, :],
                                            start=True, stop=True)
                last.then_inc(logit_done, 1)

        def pe_step(pe, st):
            if st.it is None and st.c == B + 2:
                pe_shift(pe, st)
                pv_round(pe, st, 4, 1)
                pe_exp(pe, st, (0, 12))
                pv_round(pe, st, 3, 0)
                pe_exp(pe, st, (12, 16))
                pe_out(pe, st)
                pv_round(pe, Step(None, B + 3), 4, 1)
                pe_shared_chunk(pe, 0, 0)
                pe_shared_chunk(pe, 0, 1)
                pe_x2(pe, st)
                pe_shared_chunk(pe, 0, 2)
                pe_logits(pe, st)
                pe_shared_chunk(pe, 0, 3)
                return
            if st.it is None and st.c == B + 3:
                pe_out(pe, st)
                pe_shared_down(pe, 0, (0, 2))
                pe_x2(pe, st)
                pe_logits(pe, st)
                pe_shared_down(pe, 0, (2, 4))
                return
            if st.it is None and st.c == 1:
                pe.wait_ge(consts_loaded, CONST_LOADS * 16)
            pe_shift(pe, st)
            pe_scores(pe, st, 1, (4, 7))
            pv_round(pe, st, 4, 1)
            pe_max(pe, st, (0, 2))
            pe_exp(pe, st, (0, 2))
            pe_scores(pe, st, 1, (7, 8))
            pe_max(pe, st, (2, 3))
            pe_exp(pe, st, (2, 4))
            pe_xn(pe, st)
            pe_q(pe, st)
            pe_max(pe, st, (3, 4))
            pe_exp(pe, st, (4, 5))
            pe_scores(pe, st, 0, (0, 2))
            pe_exp(pe, st, (5, 6))
            pe_max(pe, st, (4, 5))
            pe_scores(pe, st, 0, (2, 3))
            pe_exp(pe, st, (6, 7))
            pe_max(pe, st, (5, 6))
            pe_exp(pe, st, (7, 8))
            pe_max(pe, st, (6, 7))
            pe_exp(pe, st, (8, 9))
            pe_max(pe, st, (7, 8))
            pv_round(pe, st, 3, 0)
            pe_max(pe, st, (8, 9))
            pe_out(pe, st)
            pe_exp(pe, st, (9, 10))
            pe_scores(pe, st, 0, (3, 4))
            pe_exp(pe, st, (10, 11))
            pe_max(pe, st, (9, 11))
            pe_mem(pe, st)
            pe_exp(pe, st, (11, 13))
            pe_max(pe, st, (11, 12))
            pe_kv(pe, st)
            pe_max(pe, st, (12, 13))
            pe_exp(pe, st, (13, 15))
            pe_max(pe, st, (13, 14))
            pe_x2(pe, st)
            pe_max(pe, st, (14, 15))
            pe_exp(pe, st, (15, 16))
            pe_max(pe, st, (15, 16))
            pe_logits(pe, st)

        def copy_scores(act, st, stage, span):
            if st.on(stage):
                for i in range(*span):
                    t, c = i // 4, i % 4
                    if c == 0:
                        st.wait(act, argmax_read, st.b(stage) * LT + t - 1)
                    st.wait(act, score_done, st.b(stage) * 8 + i + 1)
                    nc.scalar.copy(score_sb[:, t, CSTART[c]:CSTART[c] + CHUNK[c]], ring[:, i % 2, 0:CHUNK[c]]).then_inc(score_copied, 1)

        def exp_tile(act, st, n):
            c, j = n // 2, n % 2
            st.wait(act, exp_mm, st.b(3) * 16 + n + 1)
            if n % 8 == 0:
                st.wait(act, pv_done, st.b(3) * 2 + n // 8 - 1)
            nc.scalar.activation(probs[:, j, 512 * c:512 * c + 512], exp_bank(st, n), ACT.Exp,
                                 scale=DH ** -0.5).then_inc(exp_done, 1)

        def act_exp(act, st, span):
            if st.on(3):
                for n in range(*span):
                    exp_tile(act, st, n)

        def act_att(act, st, stage, r):
            if st.on(stage):
                st.wait(act, pv_done, st.b(stage) * 2 + r + 1)
                if r == 0:
                    st.wait(act, att_written, st.b(stage) * 64)
                nc.scalar.copy(att_raw[:, r], pv[:, :]).then_inc(pv_copied, 1)

        def act_xn(act, st):
            if st.on(0):
                st.wait(act, xn_t_done, st.b(0) + 1)
                st.wait(act, q_done, st.b(0))
                nc.scalar.copy(xn_t[:, :], misc[:, 0:L]).then_inc(xn_t_ready, 1)

        def act_q(act, st):
            if st.on(0):
                p = st.par(0)
                st.wait(act, q_done, st.b(0) + 1)
                st.wait(act, score_done, st.b(0) * 8 - 8)
                st.wait(act, q_split, st.b(0) * 4 - 4)
                nc.scalar.copy(q_t[:, p], misc[:, 0:L]).then_inc(q_ready, 1)

        def act_mem(act, st):
            if st.on(1):
                st.wait(act, mem_t_done, st.b(1) + 1)
                st.wait(act, kv_done, st.b(1))
                nc.scalar.copy(mem_t[:, :], misc[:, 0:L]).then_inc(mem_t_ready, 1)

        def act_kv(act, st):
            if st.on(1):
                st.wait(act, kv_done, st.b(1) + 1)
                st.wait(act, k_ready, st.b(1))
                nc.scalar.copy(keys[:, :], misc[0:NSTACK, 0:L]).then_inc(kv_copied, 1)
                st.wait(act, kv_kept, st.b(1) * 2 - 2)
                nc.scalar.copy(v_raw[:, st.par(1)], misc[:, L:L + LT * DH].rearrange("p (j v) -> p j v", v=DH)).then_inc(kv_copied, 1)

        def act_x2(act, st):
            if st.on(4):
                st.wait(act, x2_t_done, st.b(4) + 1)
                nc.scalar.copy(x2_t[:, :], misc[:, 0:L]).then_inc(x2_t_ready, 1)
                nc.scalar.copy(x2_all[:, bass.ds(st.value(st.b(4) * L), L)], misc[:, 0:L]).then_inc(x2_t_ready, 1)

        def load_ffn(act, turn):
            es = slice(turn * E // 4, (turn + 1) * E // 4)
            dst, src = ((tab[:, :], table), (sgate_sb[:, :], sgate_t.rearrange("d (c h) -> d c h", c=SHC)),
                        (sup_sb[:, :], sup_t.rearrange("d (c h) -> d c h", c=SHC)),
                        (sdown_sb[:, :], sdown_t.rearrange("(c h) d -> h c d", c=SHC)))[turn]
            act.dma_start(dst, src).then_inc(ffn_loaded, 16)
            act.dma_start(gu_sb[:, es], gate_up_t[:, es]).then_inc(ffn_loaded, 16)
            act.dma_start(down_sb[:, es], down_t[:, es]).then_inc(ffn_loaded, 16)

        def act_step(act, st):
            if st.it is None and st.c == B + 2:
                act_att(act, st, 4, 1)
                act_softmax(act, 0)
                act_exp(act, st, (0, 16))
                act_att(act, st, 3, 0)
                act_att(act, Step(None, B + 3), 4, 1)
                act_shared_chunk(act, 0, 0)
                act_shared_chunk(act, 0, 1)
                act_x2(act, st)
                act_shared_chunk(act, 0, 2)
                act_shared_chunk(act, 0, 3)
                return
            if st.it is None and st.c == B + 3:
                act_x2(act, st)
                return
            if st.it is None and st.c == 1:
                act.wait_ge(consts_loaded, CONST_LOADS * 16)
                nc.scalar.activation(tgx[:, :], gx[:, :], ACT.Tanh).then_inc(tanh_ready, 1)
                nc.scalar.activation(tgf[:, :], gf[:, :], ACT.Tanh).then_inc(tanh_ready, 1)
            if st.it is None and st.c < 4:
                load_ffn(act, st.c)
            act_att(act, st, 4, 1)
            act_exp(act, st, (0, 2))
            copy_scores(act, st, 1, (7, 8))
            act_xn(act, st)
            act_exp(act, st, (2, 4))
            act_q(act, st)
            copy_scores(act, st, 0, (0, 1))
            act_exp(act, st, (4, 9))
            copy_scores(act, st, 0, (1, 2))
            act_exp(act, st, (9, 11))
            act_att(act, st, 3, 0)
            act_mem(act, st)
            act_exp(act, st, (11, 13))
            act_kv(act, st)
            act_exp(act, st, (13, 14))
            act_x2(act, st)
            copy_scores(act, st, 0, (2, 3))
            act_exp(act, st, (14, 16))
            copy_scores(act, st, 0, (3, 7))

        def dve_argmax_value(dve, st, t):
            if st.on(1):
                st.wait(dve, score_copied, st.b(1) * 8 + 4 * t + 4)
                passed(dve, st)
                nc.vector.max(top8[:, t], score_sb[:, t]).then_inc(dve_argmax, 1)

        def dve_argmax_index(dve, st, t):
            if st.on(1):
                st.wait(dve, dve_argmax, st.b(1) * LT + t + 1)
                passed(dve, st)
                nc.vector.max_index(top_at[:, t], top8[:, t], score_sb[:, t]).then_inc(argmax_read, 1)
                st.wait(dve, argmax_read, st.b(1) * LT + t + 1)
                st.wait(dve, mem_gathered[t], st.b(1) * 16)
                passed(dve, st)
                nc.vector.tensor_tensor(row_at[:, t], top_at[:, t, 0:1], row_base[:, :], ALU.add).then_inc(row_ready, 1)
                if t == LT - 1:
                    st.wait(dve, row_ready, st.b(1) * LT + LT)
                    nc.vector.tensor_scalar(row_base[:, :], row_base[:, :], float(M), None, ALU.add).then_inc(row_base_set, 1)
                    st.wait(dve, row_base_set, st.b(1) + 2)

        def reduce_max(dve, st, span):
            if st.on(2):
                p = st.par(2)
                for n in range(*span):
                    t, hp = n // 8, n % 8
                    st.wait(dve, max_done, st.b(2) * 16 + n + 1)
                    nc.vector.tensor_reduce(row_max[:, p, t, 2 * hp:2 * hp + 2],
                                            ring[:, 2 + n % 2].rearrange("p (w m) -> p w m", w=2),
                                            AX.X, ALU.max).then_inc(max_reduced, 1)

        def dve_neg(dve, st):
            if st.on(3):
                st.wait(dve, max_reduced, st.b(3) * 16 + 16)
                st.wait(dve, shift_t_done, st.b(3))
                nc.vector.tensor_scalar(neg_max[:, :], row_max[:, st.par(3)], -1.0, None, ALU.mult).then_inc(neg_ready, 1)

        def dve_shift_parts(dve, st):
            if st.on(3):
                st.wait(dve, shift_t_done, st.b(3) + 1)
                st.wait(dve, shift_loaded, st.b(3) * 32)
                nc.vector.tensor_copy(shift_hi[:, :], misc[0:H, 0:L]).then_inc(shift_ready, 1)
                st.wait(dve, shift_ready, st.b(3) * 2 + 1)
                nc.vector.tensor_tensor(shift_lo[:, :], misc[0:H, 0:L], shift_hi[:, :], ALU.subtract).then_inc(shift_ready, 1)

        def layer_stats(dve, st, stage, xb, stats_, mean_var_, var_, link_sem, var_sem):
            ch = Chain(dve, st, link_sem, stage, 2 * LT)
            passed(dve, st)
            for t in range(LT):
                ch.link(nc.vector.bn_stats(stats_[:, t], xb[:, t]), wait=False)
            ch.wait()
            for t in range(LT):
                ch.link(nc.vector.bn_aggr(mean_var_[:, t], stats_[:, t]), wait=False)
            ch.wait()
            ch.end()
            nc.vector.tensor_scalar(var_[:, :], mean_var_[:, :, 1], EPS, None, ALU.add).then_inc(var_sem, 1)

        def batch_rows(st, stage):
            return x_in[:, bass.ds(st.value(st.b(stage) * LT), LT)]

        def dve_ln_x(dve, st):
            if st.on(0):
                layer_stats(dve, st, 0, batch_rows(st, 0), stats, mean_var, var_eps, dve_ln, var_ready)

        def dve_xn(dve, st):
            if st.on(0):
                xb = batch_rows(st, 0)
                st.wait(dve, rstd_ready, st.b(0) + 1)
                st.wait(dve, xn_t_done, st.b(0))
                for t in range(LT):
                    nc.vector.tensor_scalar(xn[:, t], xb[:, t], mean_var[:, t, 0:1], rstd[:, t:t + 1],
                                            ALU.subtract, ALU.mult).then_inc(xn_ready, 1)

        def dve_att(dve, st):
            if st.on(4):
                st.wait(dve, att_loaded, st.b(4) * 32 + 32)
                ch = Chain(dve, st, dve_out, 4, 1)
                ch.link(nc.vector.reciprocal(att_inv[:, :], att_den[:, :]))
                ch.end()
                nc.vector.tensor_tensor(att_t[:, :], att_num[:, :], att_inv[:, :], ALU.mult).then_inc(att_ready, 1)

        def dve_x1(dve, st):
            if st.on(4):
                xb = batch_rows(st, 4)
                st.wait(dve, out_done, st.b(4) + 1)
                for t in range(LT):
                    nc.vector.scalar_tensor_tensor(xb[:, t], misc[:, 128 * t:128 * t + 128], tgx[:, :], xb[:, t],
                                                   ALU.mult, ALU.add).then_inc(x1_ready, 1)
                st.wait(dve, x1_ready, st.b(4) * LT + LT)
                layer_stats(dve, st, 4, xb, stats2, mean_var2, var_eps2, dve_ln2, var2_ready)

        def dve_x2(dve, st):
            if st.on(4):
                xb = batch_rows(st, 4)
                st.wait(dve, rstd2_ready, st.b(4) + 1)
                st.wait(dve, x2_stored, st.b(4) * 16 + 1)
                for t in range(LT):
                    nc.vector.tensor_scalar(x2[:, t], xb[:, t], mean_var2[:, t, 0:1], rstd2[:, t:t + 1],
                                            ALU.subtract, ALU.mult).then_inc(x2_ready, 1)

        def dve_logits(dve, st):
            if st.on(4):
                st.wait(dve, logit_done, st.b(4) + 1)
                nc.vector.tensor_tensor(logits[:, bass.ds(st.value(st.b(4) * LT), LT)],
                                        misc[:, 0:LT * E].rearrange("p (t e) -> p t e", e=E),
                                        bias_sb[:, :].unsqueeze(1).broadcast_to([128, LT, E]), ALU.add).then_inc(logit_ready, 1)

        def dve_step(dve, st):
            if st.it is None and st.c == B + 2:
                dve_neg(dve, st)
                dve_shift_parts(dve, st)
                dve.wait_ge(ffn_loaded, FFN_LOADS * 16)
                nc.vector.tensor_copy(tri_bf[:, :], triangle)
                nc.vector.tensor_copy(token_f16[:, :], token_no)
                softmax_part(dve, 0, B - 2)
                dve_att(dve, st)
                dve_x1(dve, st)
                dve_x2(dve, st)
                dve_shared_chunk(dve, 0, 0)
                dve_shared_chunk(dve, 0, 1)
                dve_logits(dve, st)
                dve_shared_chunk(dve, 0, 2)
                dve_shared_chunk(dve, 0, 3)
                return
            if st.it is None and st.c == B + 3:
                dve_att(dve, st)
                dve_x1(dve, st)
                dve_x2(dve, st)
                dve_logits(dve, st)
                return
            if st.it is None and st.c == 1:
                dve.wait_ge(x_loaded, 16)
                dve.wait_ge(tanh_ready, 2)
            dve_neg(dve, st)
            dve_ln_x(dve, st)
            dve_shift_parts(dve, st)
            dve_argmax_value(dve, st, 0)
            dve_argmax_index(dve, st, 0)
            reduce_max(dve, st, (0, 1))
            dve_xn(dve, st)
            reduce_max(dve, st, (1, 3))
            dve_argmax_value(dve, st, 1)
            reduce_max(dve, st, (3, 4))
            dve_argmax_index(dve, st, 1)
            reduce_max(dve, st, (4, 6))
            dve_att(dve, st)
            reduce_max(dve, st, (6, 9))
            dve_x1(dve, st)
            reduce_max(dve, st, (9, 11))
            dve_x2(dve, st)
            reduce_max(dve, st, (11, 16))
            dve_logits(dve, st)

        def run(nc_engine, eng, step):
            for c in range(STAGES - 1):
                step(eng, Step(None, c))
            with eng.Fori(0, (B - STAGES + 1) // 2) as it:
                for u in range(2):
                    step(eng, Step(it, STAGES - 1 + u))
            for c in range(B, B + STAGES - 1):
                step(eng, Step(None, c))

        exp_wanted = sem("exp_wanted")
        routed = sem("routed")
        exp_ready, mask_ready, rank_done, onehots_ready, slot_done = (
            sem("exp_ready"), sem("mask_ready"), sem("rank_done"), sem("onehots_ready"), sem("slot_done"))
        slot_ready, items_ready, items_loaded, pos_ready = sem("slot_ready"), sem("items_ready"), sem("items_loaded"), sem("pos_ready")
        sh_done, sh_silu, sh_hid, sh_out, sh_copied = sem("sh_done"), sem("sh_silu"), sem("sh_hid"), sem("sh_out"), sem("sh_copied")
        rows_gathered = [sem(f"rows_gathered{i}") for i in range(4)]
        xs_done, xs_copied = sem("xs_done"), sem("xs_copied")
        weights_copied, gu_done, silu_done, hid_ready = sem("weights_copied"), sem("gu_done"), sem("silu_done"), sem("hid_ready")
        y_done, y_copied = sem("y_done"), sem("y_copied")
        y_stored = [sem("y_stored0"), sem("y_stored1")]
        back_gathered = [sem(f"back_gathered{i}") for i in range(4)]
        mixed, result_ready, out_stored = sem("mixed"), sem("result_ready"), [sem(f"out_stored{i}") for i in range(4)]
        sh_hid_pool = sem("sh_hid_pool")
        pad_zeroed, reps_loaded = sem("pad_zeroed"), sem("reps_loaded")
        xs_bank = [pv, misc]
        token_named, pos_named = sem("token_named"), sem("pos_named")

        def bc(ap, axis, shape):
            return ap.unsqueeze(axis).broadcast_to(shape)

        count_done = sem("count_done")

        routing = [0]

        def step(dve, ins):
            routing[0] += 1
            ins.then_inc(routed, 1)
            dve.wait_ge(routed, routing[0])

        def part_tiles(part):
            return slice(0, 2 * (B - 2)) if part == 0 else slice(2 * (B - 2), NT)

        def softmax_part(dve, part, batches):
            ts = part_tiles(part)
            n = ts.stop - ts.start
            top1, total, inv = (small[:, i, ts] for i in range(3))
            lg_ = logits[:, ts]
            dve.wait_ge(logit_ready, batches + 1)
            step(dve, nc.vector.tensor_reduce(top1, lg_, AX.X, ALU.max))
            nc.vector.tensor_tensor(lg_, lg_, bc(top1, 2, [128, n, E]), ALU.subtract).then_inc(exp_wanted, 1)
            dve.wait_ge(exp_ready, part + 1)
            step(dve, nc.vector.tensor_reduce(total, lg_, AX.X, ALU.add))
            step(dve, nc.vector.reciprocal(inv, total))
            step(dve, nc.vector.tensor_tensor(lg_, lg_, bc(inv, 2, [128, n, E]), ALU.mult))
            for t in range(ts.start, ts.stop):
                ins = nc.vector.max(top_p[:, t], logits[:, t])
            step(dve, ins)
            for t in range(ts.start, ts.stop):
                ins = nc.vector.max_index(top_e[:, t], top_p[:, t], logits[:, t])
            step(dve, ins)

        def act_softmax(act, part):
            act.wait_ge(exp_wanted, part + 1)
            nc.scalar.activation(logits[:, part_tiles(part)], logits[:, part_tiles(part)], ACT.Exp).then_inc(exp_ready, 1)

        def route(dve):
            four, inv4 = small[:, 3], small[:, 4]

            def link(ins):
                step(dve, ins)

            link(nc.vector.tensor_copy(top_f[:, :], top_e[:, :, 0:K].rearrange("p t k -> p k t")))
            dve.wait_ge(reps_loaded, 16)
            link(nc.vector.tensor_tensor(onehot.rearrange("p e k t -> p e (k t)"), expert_rep.rearrange("p e k t -> p e (k t)"),
                                         bc(top_f[:, :].rearrange("p k t -> p (k t)"), 1, [128, E, K * NT]), ALU.is_equal))
            link(nc.vector.tensor_tensor(half_mask, onehot[:, :, 0:2], onehot[:, :, 2:4], ALU.add))
            nc.vector.tensor_tensor(mask[:, :], half_mask[:, :, 0], half_mask[:, :, 1], ALU.add).then_inc(mask_ready, 1)
            link(nc.vector.tensor_reduce(four, top_p[:, :, 0:K], AX.X, ALU.add))
            link(nc.vector.tensor_scalar(four, four, 1e-12, None, ALU.max))
            link(nc.vector.reciprocal(inv4, four))
            link(nc.vector.tensor_tensor(weight[:, :], top_p[:, :, 0:K], bc(inv4, 2, [128, NT, K]), ALU.mult))
            dve.wait_ge(count_done, 1)
            cnt, tiles, tiles_to, cnt_to, tile_at, start, row_base_e, one = (counts[:, i] for i in range(8))
            link(nc.vector.tensor_copy(cnt, lg[:, 1, 0:E]))
            link(nc.vector.tensor_scalar(tiles_i[:, :], cnt, 127.0, None, ALU.add))
            link(nc.vector.tensor_scalar(tiles_i[:, :], tiles_i[:, :], 7, None, ALU.logical_shift_right))
            link(nc.vector.tensor_copy(tiles, tiles_i[:, :]))
            link(nc.vector.memset(one, 1.0))
            link(nc.vector.tensor_tensor_scan(tiles_to, one, tiles, 0.0, ALU.mult, ALU.add))
            link(nc.vector.tensor_tensor_scan(cnt_to, one, cnt, 0.0, ALU.mult, ALU.add))
            link(nc.vector.tensor_tensor(start, cnt_to, cnt, ALU.subtract))
            link(nc.vector.tensor_tensor(tile_at, tiles_to, tiles, ALU.subtract))

            def positions(base):
                link(nc.vector.tensor_tensor(ranks[:, :], lg[:, 0].rearrange("p (e t) -> p e t", t=NT), bc(base, 2, [128, E, NT]), ALU.add))
                link(nc.vector.tensor_tensor(sel, onehot, bc(ranks[:, :], 2, [128, E, K, NT]), ALU.mult))
                link(nc.vector.tensor_reduce(pos[:, :].rearrange("p k t -> p (k t)"), sel.rearrange("p e k t -> p (k t) e"), AX.X, ALU.add))

            dve.wait_ge(rank_done, 1)
            positions(start)
            link(nc.vector.tensor_copy(pos_i[:, 0], pos[:, :]))
            link(nc.vector.tensor_scalar(pos_i[:, 1], pos_i[:, 0], 7, None, ALU.logical_shift_right))
            link(nc.vector.tensor_copy(pos_g[:, :], pos_i[:, 1]))
            link(nc.vector.scalar_tensor_tensor(pos_r[:, :], pos_g[:, :], -128.0, pos[:, :], ALU.mult, ALU.add))
            for k in range(K):
                nc.vector.tensor_tensor(onehot_r[:, k], row_rep, bc(pos_r[:, k], 1, [128, 128, NT]), ALU.is_equal)
                link(nc.vector.tensor_tensor(onehot_g[:, k], row_rep[:, 0:NDENSE], bc(pos_g[:, k], 1, [128, NDENSE, NT]), ALU.is_equal))
                nc.vector.tensor_tensor(onehot_g[:, k], onehot_g[:, k], bc(token_f16[:, :], 1, [128, NDENSE, NT]),
                                        ALU.mult).then_inc(onehots_ready, 1)
            dve.wait_ge(slot_done, K)
            nc.vector.tensor_copy(slot_token[:, :], misc[:, 0:NDENSE]).then_inc(slot_ready, 1)
            ended, no_e, g, at_tile, at_start, off = (item[:, c:c + 1] for c in range(6))
            cmp, hot = counts[:, 8], counts[:, 9]
            link(nc.vector.tensor_scalar(cmp, tiles_to, part_no, None, ALU.is_le))
            link(nc.vector.tensor_reduce(ended, cmp, AX.X, ALU.add))
            link(nc.vector.tensor_scalar(no_e, ended, float(E - 1), None, ALU.min))
            link(nc.vector.tensor_scalar(hot, expert_no, no_e, None, ALU.is_equal))
            link(nc.vector.tensor_tensor(cmp, hot, tile_at, ALU.mult))
            link(nc.vector.tensor_reduce(at_tile, cmp, AX.X, ALU.add))
            link(nc.vector.tensor_tensor(cmp, hot, start, ALU.mult))
            link(nc.vector.tensor_reduce(at_start, cmp, AX.X, ALU.add))
            link(nc.vector.tensor_tensor(g, part_no, at_tile, ALU.subtract))
            link(nc.vector.scalar_tensor_tensor(off, g, 128.0, at_start, ALU.mult, ALU.add))
            link(nc.vector.tensor_scalar(off, off, float(NDENSE * 128), None, ALU.min))
            link(nc.vector.tensor_copy(item_i[:, 0:1], no_e))
            nc.vector.tensor_copy(item_i[:, 1:2], off).then_inc(items_ready, 1)
            link(nc.vector.tensor_scalar(row_base_e, tile_at, 128.0, None, ALU.mult))
            positions(row_base_e)
            nc.vector.tensor_copy(pos_i[:, 0], pos[:, :]).then_inc(pos_ready, 1)

        def pe_ranks(pe):
            pe.wait_ge(mask_ready, 1)
            below = lg[:, 0].rearrange("p (e t) -> p e t", t=NT)
            for t in range(NT):
                last = nc.tensor.matmul(lg[:, 1, 0:E], ones_bf[:, :], mask[:, :, t], start=(t == 0), stop=(t == NT - 1))
            last.then_inc(count_done, 1)
            nc.tensor.matmul(below, tri_bf[:, :], mask[:, :], start=True, stop=False)
            for s in range(1, NT):
                last = nc.tensor.matmul(below[:, :, s:NT], ones_bf[:, :], mask[:, :, 0:NT - s], start=False, stop=(s == NT - 1))
            last.then_inc(rank_done, 1)

        def pe_slots(pe, k):
            pe.wait_ge(onehots_ready, k + 1)
            for t in range(NT):
                last = nc.tensor.matmul(misc[:, 0:NDENSE], onehot_r[:, k, :, t], onehot_g[:, k, :, t],
                                        start=(k == 0 and t == 0), stop=(k == K - 1 and t == NT - 1))
            last.then_inc(slot_done, 1)

        def wait_hidden(eng, chunks):
            by_pool = sum(SHC * n + c < chunks for n, c in GPSIMD_CHUNKS)
            eng.wait_ge(sh_hid, chunks - by_pool)
            if by_pool:
                eng.wait_ge(sh_hid_pool, by_pool)

        def pe_shared_chunk(pe, n, c):
            b = 2 * (c % 2)
            if n == 0 and c < 2:
                pe.wait_ge(exp_done, 16 * B)
                pe.wait_ge(max_reduced, 16 * B)
                pe.wait_ge(score_copied, 8 * B)
                if c == 0:
                    pe.wait_ge(ffn_loaded, FFN_LOADS * 16)
            elif c < 2:
                pe.wait_ge(sh_copied, n)
            else:
                wait_hidden(pe, SHC * n + c - 1)
            xs = x2_all[:, n * 512:(n + 1) * 512]
            nc.tensor.matmul(ring[:, b], sgate_sb[:, c], xs, start=True, stop=True)
            nc.tensor.matmul(ring[:, b + 1], sup_sb[:, c], xs, start=True, stop=True).then_inc(sh_done, 1)

        def pe_shared_down(pe, n, span=(0, 4)):
            wait_hidden(pe, SHC * (n + 1))
            for t in range(*span):
                for c in range(SHC):
                    last = nc.tensor.matmul(ring[:, 0, 128 * t:128 * t + 128], hid_s[:, c, 128 * t:128 * t + 128], sdown_sb[:, c],
                                            start=(c == 0), stop=(c == SHC - 1))
            if span[1] == 4:
                last.then_inc(sh_out, 1)

        def act_shared_chunk(act, n, c):
            act.wait_ge(sh_done, SHC * n + c + 1)
            if SHC * n + c >= 2:
                wait_hidden(act, SHC * n + c - 1)
            b = 2 * (c % 2)
            if (n, c) in GPSIMD_CHUNKS:
                nc.scalar.copy(up_s[:, c % 2], ring[:, b + 1])
            nc.scalar.activation(silu_s[:, c % 2], ring[:, b], ACT.Silu).then_inc(sh_silu, 1)

        def act_shared_out(act, n):
            act.wait_ge(sh_out, n + 1)
            nc.scalar.copy(shared.rearrange("p t d -> p (t d)")[:, n * 512:(n + 1) * 512], ring[:, 0]).then_inc(sh_copied, 1)

        def act_shared_block(act, n):
            for c in range(SHC):
                act_shared_chunk(act, n, c)
            act_shared_out(act, n)

        def dve_shared_chunk(dve, n, c):
            dve.wait_ge(sh_silu, SHC * n + c + 1)
            if n:
                dve.wait_ge(sh_out, n)
            nc.vector.tensor_tensor(hid_s[:, c], silu_s[:, c % 2], ring[:, 2 * (c % 2) + 1], ALU.mult).then_inc(sh_hid, 1)

        def pool_shared_chunk(pool, n, c):
            pool.wait_ge(sh_silu, SHC * n + c + 1)
            pool.wait_ge(sh_out, n)
            nc.gpsimd.tensor_tensor(hid_s[:, c], silu_s[:, c % 2], up_s[:, c % 2], ALU.mult).then_inc(sh_hid_pool, 1)

        def pe_xs(pe, n, u, first):
            pe.wait_ge(rows_gathered[u], (n - u) * 16 + 64)
            if not first:
                pe.wait_ge(xs_copied, n - 1)
            for g in range(4):
                last = nc.tensor.transpose(xs_bank[u % 2][:, 128 * g:128 * g + 128], gathered[:, u, g], ident[:, :])
            last.then_inc(xs_done, 1)

        def act_xs(act, n, u, first):
            act.wait_ge(xs_done, n + 1)
            nc.scalar.copy(xs_t[:, bass.ds(n * 512, 512)], xs_bank[u % 2][:, :]).then_inc(xs_copied, 1)

        def pool_rows(pool, n, u, first):
            if not first:
                pool.wait_ge(xs_done, n - 3)
                pool.sem_inc(waits_passed, 1)
            if u % 2 == 0:
                if not first:
                    pool.wait_ge(rows_gathered[u + 1], (n - u) * 16)
                    pool.sem_inc(waits_passed, 1)
                nc.gpsimd.tensor_copy(token_now[:, u:u + 2], slot_token[:, bass.ds(n * 4, 8)].rearrange(
                    "p (a g) -> p a g", a=2)).then_inc(token_named, 2)
                pool.wait_ge(token_named, n + 2)
                if not first:
                    pool.sem_inc(waits_passed, 1)
            for g in range(4):
                nc.gpsimd.indirect_dma_start(
                    out=gathered[:, u, g], out_offset=None, in_=x2_scr,
                    in_offset=bass.IndirectOffsetOnAxis(ap=token_now[:, u, g:g + 1], axis=0)).then_inc(rows_gathered[u], 16)

        def item_values(engine, at, n, c, top):
            _, values = nc.values_load_multi_w_load_instructions(
                item_row[0:1, bass.ds(at + 128 * c, n)], engines=[engine], min_val=0, max_val=top,
                skip_runtime_bounds_check_because="VectorE has clamped them to the table's range")
            return values

        def pe_gate_up(pe, q, u, before, rows):
            pe.wait_ge(weights_copied, q + 1)
            if before >= 4:
                pe.wait_ge(hid_ready, q - 3)
            for w in range(2):
                xs = xs_t[:, bass.ds(rows[w], 128)]
                for c in range(2):
                    last = nc.tensor.matmul(ring[:, u, 256 * w + 128 * c:256 * w + 128 * c + 128], w_item[:, u, w, HID * c:HID * c + HID], xs,
                                            start=True, stop=True)
            last.then_inc(gu_done, 1)

        def pe_down(pe, q, u, before, experts):
            pe.wait_ge(hid_ready, q + 1)
            if before >= 2:
                pe.wait_ge(y_copied, q - 1)
            for w in range(2):
                last = nc.tensor.matmul(lg[:, u % 2, 128 * w:128 * w + 128], hid[:, u % 2, w],
                                        down_sb[:, bass.ds(experts[w], 1)].rearrange("p o n -> p (o n)"), start=True, stop=True)
            last.then_inc(y_done, 1)

        def dve_weights(dve, q, u, before, experts):
            if before >= 4:
                dve.wait_ge(gu_done, q - 3)
            for w in range(2):
                last = nc.vector.tensor_copy(w_item[:, u, w].unsqueeze(1), gu_sb[:, bass.ds(experts[w], 1)])
            last.then_inc(weights_copied, 1)

        def dve_hid(dve, q, u, before, _):
            dve.wait_ge(silu_done, q + 1)
            if before >= 2:
                dve.wait_ge(y_done, q - 1)
            nc.vector.tensor_tensor(hid[:, u % 2], silu_e[:, u % 2], ring[:, u].rearrange("p (w c n) -> p w c n", w=2, c=2)[:, :, 1],
                                    ALU.mult).then_inc(hid_ready, 1)

        def act_silu(act, q, u, before, _):
            act.wait_ge(gu_done, q + 1)
            if before >= 2:
                act.wait_ge(hid_ready, q - 1)
            nc.scalar.activation(silu_e[:, u % 2], ring[:, u].rearrange("p (w c n) -> p w c n", w=2, c=2)[:, :, 0],
                                 ACT.Silu).then_inc(silu_done, 1)

        def act_y(act, q, u, before, _):
            b = u % 2
            act.wait_ge(y_done, q + 1)
            if before >= 2:
                act.wait_ge(y_stored[b], q * 8 - 8 * b)
            nc.scalar.copy(y_sb[:, b].rearrange("p w n -> p (w n)"), lg[:, b, 0:256]).then_inc(y_copied, 1)

        def sp_y(sp, q, u, before, _):
            sp.wait_ge(y_copied, q + 1)
            if not isinstance(q, int):
                sp.sem_inc(waits_passed, 1)
            sp.dma_start(y_scr[bass.ds(q * 2, 2)].rearrange("w p d -> p w d"), y_sb[:, u % 2]).then_inc(y_stored[u % 2], 16)

        def run_items(eng, parts, engine=None, group=None, chase=False):
            back = max(lag for _, lag, _ in parts)

            def load(at, n, column):
                return item_values(engine, at, n, column, (E - 1, NDENSE * 128)[column]) if column is not None and n else []

            def turn(j, groups=0, buffer=0, wait=False):
                peeled = isinstance(j, int) and j == 0
                values = [load(j * 8 if peeled else j * 8 - 2 * lag, 8 - 2 * lag if peeled else 8, column) for _, lag, column in parts]
                for s in range(4):
                    if s % 2 == 0 and s // 2 < groups:
                        group(eng, j * 2 + (1 + s // 2), (buffer + s // 2) % 4, peeled and s == 0)
                    if wait:
                        eng.wait_ge(xs_copied, j * 2 + (s // 2 + 1))
                    for (f, lag, _), regs in zip(parts, values):
                        if not peeled or s >= lag:
                            at = 2 * (s - lag) if peeled else 2 * s
                            f(eng, j * 4 + (s - lag), (s - lag) % 4, s - lag if peeled else 4, regs[at:at + 2])

            if group:
                group(eng, 0, 0, True)
            turn(0, 2 if group else 0, 1, chase)
            first = 1
            if group:
                first = NDENSE // 8
                with eng.Fori(0, (first - 2) // 2) as it:
                    turn(it * 2 + 1, 2, 3, chase)
                    turn(it * 2 + 2, 2, 1, chase)
                turn(first - 1, 1, 3, chase)
            with eng.Fori(first, PAIRS // 4) as j:
                turn(j)
            values = [load(ITEMS - 2 * lag, 2 * lag, column) for _, lag, column in parts]
            for s in range(back):
                for (f, lag, _), regs in zip(parts, values):
                    if s < lag:
                        f(eng, PAIRS + s - lag, (s - lag) % 4, 4, regs[2 * s:2 * s + 2])

        def pool_back(pool, n, u, first):
            if not first:
                pool.wait_ge(mixed, n * 4 - 12)
                pool.sem_inc(waits_passed, 1)
            if u % 2 == 0:
                if not first:
                    pool.wait_ge(back_gathered[u + 1], (n - u) * 16)
                    pool.sem_inc(waits_passed, 1)
                nc.gpsimd.tensor_copy(pos_now[:, u:u + 2].rearrange("p a k -> p k a"), pos_i[:, 0, :, bass.ds(n, 2)]).then_inc(pos_named, 2)
                pool.wait_ge(pos_named, n + 2)
                if not first:
                    pool.sem_inc(waits_passed, 1)
            for k in range(K):
                nc.gpsimd.indirect_dma_start(
                    out=back[:, u, k], out_offset=None, in_=y_scr.rearrange("g p d -> (g p) d"),
                    in_offset=bass.IndirectOffsetOnAxis(ap=pos_now[:, u, k:k + 1], axis=0)).then_inc(back_gathered[u], 16)

        def dve_mix(dve, n, u, first):
            dve.wait_ge(back_gathered[u], (n - u) * 16 + 64)
            if not first:
                dve.wait_ge(out_stored[u], (n - u) * 4)
            for k in range(K):
                acc = shared[:, bass.ds(n, 1)] if k == 0 else mix[:, u].unsqueeze(1)
                nc.vector.scalar_tensor_tensor(mix[:, u].unsqueeze(1), back[:, u, k].unsqueeze(1),
                                               weight[:, bass.ds(n, 1), k:k + 1].rearrange("p a b -> p (a b)"),
                                               acc, ALU.mult, ALU.add).then_inc(mixed, 1)
                dve.wait_ge(mixed, n * 4 + (k + 1))
            nc.vector.scalar_tensor_tensor(result[:, u].unsqueeze(1), mix[:, u].unsqueeze(1), tgf[:, :],
                                           x_in[:, bass.ds(n, 1)], ALU.mult, ALU.add).then_inc(result_ready, 1)

        def sp_out(sp, n, u):
            sp.wait_ge(result_ready, n + 1)
            if not isinstance(n, int):
                sp.sem_inc(waits_passed, 1)
            sp.dma_start(out.rearrange("b (t p) d -> p (b t) d", p=128)[:, bass.ds(n, 1)].rearrange("p o d -> p (o d)"),
                         result[:, u]).then_inc(out_stored[u], 16)

        def quads(eng, f, first_arg=True):
            for u in range(4):
                f(eng, u, u, True) if first_arg else f(eng, u, u)
            with eng.Fori(1, NT // 4) as it:
                for u in range(4):
                    f(eng, it * 4 + u, u, False) if first_arg else f(eng, it * 4 + u, u)

        block = ctx.enter_context(nc.Block())

        @block.sync
        def _(sp):
            sp.dma_start(x_in[:, 0:LT], x[0].rearrange("(t p) d -> p t d", p=128)).then_inc(x_first, 16)
            sp.dma_start(wq_sb[:, :], wq_t).then_inc(wq_loaded, 16)
            run(nc.sync, sp, sp_step)
            sp.wait_ge(items_ready, 1)
            sp.dma_start(item_row[0:1, 0:128], item_i[:, 0:1]).then_inc(items_loaded, 16)
            sp.dma_start(item_row[0:1, 128:256], item_i[:, 1:2]).then_inc(items_loaded, 16)
            run_items(sp, [(sp_y, 0, None)])
            quads(sp, sp_out, False)
            for b in range(2):
                sp.wait_ge(y_stored[b], 16 * PAIRS // 2)
            sp.wait_ge(x2_stored, 16 * B + 1)
            for u in range(4):
                sp.wait_ge(out_stored[u], 16 * NT // 4)

        @block.gpsimd
        def _(pool):
            nc.gpsimd.memset(ident[:, :], 0.0).then_inc(ident_ready, 1)
            pool.wait_ge(ident_ready, 1)
            nc.gpsimd.affine_select(out=ident[:, :], in_=ident[:, :], compare_op=ALU.not_equal, fill=1.0, base=0,
                                    pattern=[[-1, 128]], channel_multiplier=1).then_inc(ident_ready, 1)
            nc.gpsimd.memset(expo[:, :], -0.5).then_inc(presets, 1)
            nc.gpsimd.memset(k_exp[:, :], 1.0).then_inc(presets, 1)
            nc.gpsimd.memset(v_aug[:, :], 0.0).then_inc(presets, 1)
            pool.wait_ge(presets, 3)
            nc.gpsimd.memset(v_aug[:, :, :, DH:16], 1.0).then_inc(presets, 1)
            nc.gpsimd.memset(xs_t[:, NDENSE * 128:NDENSE * 128 + 128], 0.0).then_inc(pad_zeroed, 1)
            pool.wait_ge(presets, 4)
            run(nc.gpsimd, pool, pool_step)
            for n, c in GPSIMD_CHUNKS:
                pool_shared_chunk(pool, n, c)
            pool.wait_ge(x2_stored, 16 * B + 1)
            pool.wait_ge(slot_ready, 1)
            quads(pool, pool_rows)
            pool.wait_ge(pos_ready, 1)
            for b in range(2):
                pool.wait_ge(y_stored[b], 16 * PAIRS // 2)
            quads(pool, pool_back)

        @block.scalar
        def _(act):
            for dst, src in ((wkr_sb, wk_rep), (wv_sb, wv_t), (wc_sb, wc_t), (kmask_sb, kmask), (router_sb, router_t)):
                act.dma_start(dst[:, :], src).then_inc(consts_loaded, 16)
            for dst, src in ((gx, g_xattn), (gf, g_ffn), (bias_sb, router_bias)):
                act.dma_start(dst[:, :], src.rearrange("(o a) -> o a", o=1).broadcast_to([128, dst.shape[1]])).then_inc(consts_loaded, 16)
            act.dma_start(x_in[:, LT:B * LT], x[1:B].rearrange("b (t p) d -> p (b t) d", p=128)).then_inc(x_loaded, 16)
            run(nc.scalar, act, act_step)
            act_softmax(act, 1)
            act_shared_out(act, 0)
            act_shared_block(act, 1)
            run_items(act, [(act_silu, 0, None), (act_y, 2, None)], group=act_xs)
            act_shared_block(act, 2)
            act_shared_block(act, 3)

        @block.tensor
        def _(pe):
            pe.wait_ge(ident_ready, 2)
            pe.wait_ge(presets, 4)
            pe.wait_ge(wq_loaded, 16)
            run(nc.tensor, pe, pe_step)
            pe_ranks(pe)
            pe_shared_chunk(pe, 1, 0)
            pe_shared_chunk(pe, 1, 1)
            pe_shared_chunk(pe, 1, 2)
            pe_shared_chunk(pe, 1, 3)
            for k in range(K):
                pe_slots(pe, k)
            pe_shared_down(pe, 1)
            pe.wait_ge(sh_copied, 2)
            pe.wait_ge(pad_zeroed, 1)
            pe.wait_ge(items_loaded, 32)
            run_items(pe, [(pe_gate_up, 0, 1), (pe_down, 2, 0)], mybir.EngineType.PE, group=pe_xs, chase=True)
            pe.wait_ge(hid_ready, PAIRS)
            for n in (2, 3):
                for c in range(SHC):
                    pe_shared_chunk(pe, n, c)
                pe_shared_down(pe, n)

        @block.vector
        def _(dve):
            nc.vector.memset(row_base[:, :], 0).then_inc(row_base_set, 1)
            nc.vector.memset(x2[:, :], 0.0).then_inc(x2_stored, 1)
            nc.vector.memset(mean_var2[:, :], 0.0).then_inc(logit_ready, 1)
            nc.vector.memset(ones_bf[:, :], 1.0)
            dve.wait_ge(row_base_set, 1)
            dve.wait_ge(x_first, 16)
            run(nc.vector, dve, dve_step)
            softmax_part(dve, 1, B)
            route(dve)
            dve.wait_ge(items_loaded, 32)
            run_items(dve, [(dve_weights, 0, 0), (dve_hid, 2, None)], mybir.EngineType.DVE)
            for c in range(SHC):
                dve_shared_chunk(dve, 2, c)
            dve.wait_ge(sh_copied, 3)
            dve_mix(dve, 0, 0, True)
            dve_shared_chunk(dve, 3, 0)
            dve_shared_chunk(dve, 3, 1)
            dve_mix(dve, 1, 1, True)
            dve_shared_chunk(dve, 3, 2)
            dve_shared_chunk(dve, 3, 3)
            dve_mix(dve, 2, 2, True)
            dve_mix(dve, 3, 3, True)
            dve.wait_ge(sh_copied, 4)
            with dve.Fori(1, NT // 4) as it:
                for u in range(4):
                    dve_mix(dve, it * 4 + u, u, False)


def kernel(**inp):
    import numpy as np
    import concourse.bacc as bacc
    from concourse.bass_utils import run_bass_kernel_spmd

    f = {k: np.ascontiguousarray(v) for k, v in inp.items()}
    ctx_in = f["ctx_1024"]
    wkv = f["L0_xattn_Wkv"]
    order = [8 * (8 * r + 2 * j + w) + dd for j in range(4) for dd in range(DH) for r in range(2) for w in range(2)]
    mask = np.zeros((NSTACK, 2), np.float32)
    mask[24:, 0] = -1.0
    mask[40:, 1] = -1.0
    part = np.arange(128, dtype=np.float32)[:, None]

    def row(n, scale=1):
        return np.tile(np.arange(n, dtype=np.float32) * scale, (128, 1))

    table = np.concatenate([row(E), row(NT, 128) + part, part,
                            np.triu(np.ones((128, 128), np.float32), 1)], 1)
    repeats = np.concatenate([np.repeat(np.arange(n), m) for n, m in ((E, K * NT), (128, NT))]).astype(np.float16)
    repeats = np.tile(repeats, (128, 1))
    gate, up, down = (f["L0_ffn_" + n] for n in ("gate_w", "up_w", "down_w"))
    arrays = {
        "x": f["x"], "ctx_rows": ctx_in.reshape(B * M, D), "ctx_t": ctx_in.transpose(0, 2, 1), "wq_t": f["L0_xattn_Wq"].T,
        "wk_rep": np.tile(wkv[0:DH].T, (1, 6)), "wv_t": wkv[DH:].T, "wc_t": f["L0_xattn_Wc"].T[order],
        "kmask": mask, "g_xattn": f["g_xattn"], "g_ffn": f["g_ffn"], "table": table,
        "repeats": repeats, "router_t": f["L0_ffn_router_w"].T, "router_bias": f["L0_ffn_router_bias"],
        "gate_up_t": np.concatenate([gate, up], 1).transpose(2, 0, 1), "down_t": down.transpose(2, 0, 1),
        "sgate_t": f["L0_ffn_sgate_w"].T, "sup_t": f["L0_ffn_sup_w"].T, "sdown_t": f["L0_ffn_sdown_w"].T,
    }
    arrays = {k: np.ascontiguousarray(v) for k, v in arrays.items()}
    nc = bacc.Bacc("TRN2", target_bir_lowering=False, num_devices=1)
    args = [nc.dram_tensor("in_" + k, v.shape, mybir.dt.from_np(v.dtype), kind="ExternalInput").ap() for k, v in arrays.items()]
    out = nc.dram_tensor("out", (B, L, D), F32, kind="ExternalOutput").ap()
    build(nc, *args, out)
    r = run_bass_kernel_spmd(nc, [{"in_" + k: v for k, v in arrays.items()}], core_ids=[0])
    return r.results[0]["out"]
```
